# Optimizing a Trainium2 kernel written in Bass

```python
import numpy as np
import jax
import jax.numpy as jnp

def _softmax(x, axis=-1):
    return jax.nn.softmax(x, axis=axis)

def _gelu(x):
    return jax.nn.gelu(x, approximate=True)

def _silu(x):
    return jax.nn.silu(x)

def _sigmoid(x):
    return jax.nn.sigmoid(x)

def _layernorm(x, axis=-1, eps=1e-05):
    m = jnp.mean(x, axis=axis, keepdims=True)
    v = jnp.var(x, axis=axis, keepdims=True)
    return (x - m) / jnp.sqrt(v + eps)

def _scatter_add(tgt, idx, src, axis=0):
    return tgt.at[idx].add(src)

def _segment_sum(src, seg, n):
    return jax.ops.segment_sum(src, seg, n)
kernel_name = 'mk_gps_d2_gnn_r16_a80ff8'

def setup_inputs(seed: int=0):
    np.random.seed(seed)
    _w = jnp.asarray

    def _rec_inputs():
        import jax
        import jax.numpy as jnp
        _gk = jax.random.key(seed)
        x = -0.0002117 + 1 * jax.random.normal(jax.random.fold_in(_gk, 1), (6250, 256), jnp.float32)
        src = jax.random.randint(jax.random.fold_in(_gk, 2), (100000,), 0, 6250, jnp.int32)
        dst = jax.random.randint(jax.random.fold_in(_gk, 3), (100000,), 0, 6250, jnp.int32)
        _o = jnp.argsort(dst, stable=True)
        src = src[_o]
        dst = dst[_o]
        edge_weight = jax.random.uniform(jax.random.fold_in(_gk, 14), (100000,), jnp.float32, 0.0, 1)
        return (x, src, dst, edge_weight)
    x, src, dst, edge_weight = _rec_inputs()

    def _L0_gnn_setup():
        import jax, jax.numpy as jnp
        import numpy as np
        BN_EPS = 1e-05

        def _batchnorm(h, gamma, beta):
            mean = jnp.mean(h, axis=0, keepdims=True)
            var = jnp.var(h, axis=0, keepdims=True)
            return (h - mean) * jax.lax.rsqrt(var + BN_EPS) * gamma + beta
        key = jax.random.key(seed)
        ks = jax.random.split(key, 10)
        N, E, D = (6250, 200000, 256)
        x = jax.random.normal(ks[0], (N, D), dtype=jnp.float32)
        edge_src = jax.random.randint(ks[1], (E,), 0, N, dtype=jnp.int32)
        edge_dst = jax.random.randint(ks[2], (E,), 0, N, dtype=jnp.int32)
        edge_vals = jnp.ones((E,), dtype=jnp.float32)
        n_norm = jax.random.uniform(ks[3], (N, 1), dtype=jnp.float32)
        s = 1.0 / np.sqrt(D)
        w1 = jax.random.uniform(ks[4], (D, D), jnp.float32, -s, s)
        gamma1 = jnp.ones((D,), jnp.float32)
        beta1 = jnp.zeros((D,), jnp.float32)
        w2 = jax.random.uniform(ks[5], (D, D), jnp.float32, -s, s)
        eps_weight = jnp.zeros((1,), jnp.float32)
        gamma_h = jnp.ones((D,), jnp.float32)
        beta_h = jnp.zeros((D,), jnp.float32)
        return {'x': x, 'edge_src': edge_src, 'edge_dst': edge_dst, 'edge_vals': edge_vals, 'n_norm': n_norm, 'w1': w1, 'gamma1': gamma1, 'beta1': beta1, 'w2': w2, 'eps_weight': eps_weight, 'gamma_h': gamma_h, 'beta_h': beta_h}
    _L0_gnn_all = _L0_gnn_setup()
    _L0_gnn_in = {k: v for k, v in _L0_gnn_all.items() if k in ('w1', 'gamma1', 'beta1', 'w2', 'eps_weight', 'gamma_h', 'beta_h')}
    del _L0_gnn_all

    def _L0_mix_setup():
        import jax, jax.numpy as jnp
        import numpy as np
        D_MODEL = 256
        NUM_HEADS = 8
        DEPTH = D_MODEL // NUM_HEADS
        B, L = (32, 256)

        def _feature_map(x):
            return jax.nn.elu(x) + 1.0
        key = jax.random.key(seed)
        ks = jax.random.split(key, 9)
        sc = 1.0 / np.sqrt(D_MODEL)
        return {'x': jax.random.normal(ks[0], (B, L, D_MODEL), dtype=jnp.float32), 'wq': jax.random.normal(ks[1], (D_MODEL, D_MODEL), dtype=jnp.float32) * sc, 'bq': jnp.zeros((D_MODEL,), dtype=jnp.float32), 'wk': jax.random.normal(ks[2], (D_MODEL, D_MODEL), dtype=jnp.float32) * sc, 'bk': jnp.zeros((D_MODEL,), dtype=jnp.float32), 'wv': jax.random.normal(ks[3], (D_MODEL, D_MODEL), dtype=jnp.float32) * sc, 'bv': jnp.zeros((D_MODEL,), dtype=jnp.float32), 'wo': jax.random.normal(ks[4], (D_MODEL, D_MODEL), dtype=jnp.float32) * sc, 'bo': jnp.zeros((D_MODEL,), dtype=jnp.float32)}
    _L0_mix_all = _L0_mix_setup()
    _L0_mix_in = {k: v for k, v in _L0_mix_all.items() if k in ('wq', 'bq', 'wk', 'bk', 'wv', 'bv', 'wo', 'bo')}
    del _L0_mix_all

    def _L0_ffn_setup():
        import jax, jax.numpy as jnp
        import numpy as np
        B, K, D = (512, 16, 256)
        E = 32
        H = int(D * 0.25)
        key = jax.random.key(seed)
        ks = jax.random.split(key, 7)
        d_rs = D ** (-0.5)
        h_rs = H ** (-0.5)
        x = jax.random.normal(ks[0], (B, K, D), dtype=jnp.float32)
        router_w = jax.random.uniform(ks[1], (E, D), jnp.float32, -d_rs, d_rs)
        router_b = jax.random.uniform(ks[2], (E,), jnp.float32, -d_rs, d_rs)
        W1 = jax.random.uniform(ks[3], (E, D, H), jnp.float32, -h_rs, h_rs)
        b1 = jax.random.uniform(ks[4], (E, H), jnp.float32, -h_rs, h_rs)
        W2 = jax.random.uniform(ks[5], (E, H, D), jnp.float32, -d_rs, d_rs)
        b2 = jax.random.uniform(ks[6], (E, D), jnp.float32, -d_rs, d_rs)
        return {'x': x, 'router_w': router_w, 'router_b': router_b, 'W1': W1, 'b1': b1, 'W2': W2, 'b2': b2}
    _L0_ffn_all = _L0_ffn_setup()
    _L0_ffn_in = {k: v for k, v in _L0_ffn_all.items() if k in ('router_w', 'router_b', 'W1', 'b1', 'W2', 'b2')}
    del _L0_ffn_all

    def _L1_gnn_setup():
        import jax, jax.numpy as jnp
        import numpy as np
        N_NODES = 3125
        N_EDGES = 100000
        F_IN = 256
        F_OUT = 256

        def _gcn_conv(x, src, dst, ew, W, b, n_nodes):
            xW = x @ W
            deg = jax.ops.segment_sum(ew, dst, num_segments=n_nodes) + 1.0
            dinv = jnp.where(deg > 0, jax.lax.rsqrt(deg), 0.0)
            norm = dinv[src] * ew * dinv[dst]
            agg = jax.ops.segment_sum(norm[:, None] * xW[src], dst, num_segments=n_nodes)
            agg = agg + (dinv * dinv)[:, None] * xW
            return agg + b
        key = jax.random.key(seed)
        ks = jax.random.split(key, 7)
        x = jax.random.normal(ks[0], (N_NODES, F_IN), dtype=jnp.float32)
        edge_index = jax.random.randint(ks[1], (2, N_EDGES), 0, N_NODES, dtype=jnp.int64)
        edge_weight = jax.random.uniform(ks[2], (N_EDGES,), dtype=jnp.float32)
        W1 = jax.random.normal(ks[3], (F_IN, F_OUT), dtype=jnp.float32) * (1.0 / np.sqrt(F_IN))
        b1 = jnp.zeros((F_OUT,), dtype=jnp.float32)
        W2 = jax.random.normal(ks[4], (F_OUT, F_OUT), dtype=jnp.float32) * (1.0 / np.sqrt(F_OUT))
        b2 = jnp.zeros((F_OUT,), dtype=jnp.float32)
        return {'x': x, 'edge_index': edge_index, 'edge_weight': edge_weight, 'W1': W1, 'b1': b1, 'W2': W2, 'b2': b2}
    _L1_gnn_all = _L1_gnn_setup()
    _L1_gnn_in = {k: v for k, v in _L1_gnn_all.items() if k in ('W1', 'b1', 'W2', 'b2')}
    del _L1_gnn_all

    def _L1_mix_setup():
        import jax, jax.numpy as jnp
        import numpy as np
        BN_EPS = 1e-05
        key = jax.random.key(seed)
        ks = jax.random.split(key, 4)
        B, N, D = (8, 512, 256)
        outD = 256
        s = 1.0 / np.sqrt(D)
        return {'feature': jax.random.normal(ks[0], (B, N, D), dtype=jnp.float32), 'W_qk': jax.random.normal(ks[1], (2, D, D), dtype=jnp.float32) * s, 'b_qk': jnp.zeros((2, D), dtype=jnp.float32), 'W_v': jax.random.normal(ks[2], (D, outD), dtype=jnp.float32) * s, 'b_v': jnp.zeros((outD,), dtype=jnp.float32), 'gamma': jnp.ones((D,), dtype=jnp.float32), 'beta': jnp.zeros((D,), dtype=jnp.float32)}
    _L1_mix_all = _L1_mix_setup()
    _L1_mix_in = {k: v for k, v in _L1_mix_all.items() if k in ('W_qk', 'b_qk', 'W_v', 'b_v', 'gamma', 'beta')}
    del _L1_mix_all

    def _L1_ffn_setup():
        import jax, jax.numpy as jnp
        import numpy as np
        DIM = 256
        H = 8
        D = 64
        G = 64
        INNER = H * D
        SCALE = D ** (-0.5)
        key = jax.random.key(seed)
        ks = jax.random.split(key, 12)
        B, N = (4, 1024)
        x = jax.random.normal(ks[0], (B, N, DIM), dtype=jnp.float32)
        s = lambda fan_in: 1.0 / np.sqrt(fan_in)
        W_fx = jax.random.normal(ks[1], (DIM, INNER), dtype=jnp.float32) * s(DIM)
        b_fx = jnp.zeros((INNER,), dtype=jnp.float32)
        W_x = jax.random.normal(ks[2], (DIM, INNER), dtype=jnp.float32) * s(DIM)
        b_x = jnp.zeros((INNER,), dtype=jnp.float32)
        A = jax.random.normal(ks[3], (G, D), dtype=jnp.float32)
        Q, _ = jnp.linalg.qr(A.T)
        W_slice = Q[:, :G].astype(jnp.float32)
        b_slice = jnp.zeros((G,), dtype=jnp.float32)
        W_q = jax.random.normal(ks[4], (D, D), dtype=jnp.float32) * s(D)
        W_k = jax.random.normal(ks[5], (D, D), dtype=jnp.float32) * s(D)
        W_v = jax.random.normal(ks[6], (D, D), dtype=jnp.float32) * s(D)
        W_out = jax.random.normal(ks[7], (INNER, DIM), dtype=jnp.float32) * s(INNER)
        b_out = jnp.zeros((DIM,), dtype=jnp.float32)
        temperature = jnp.ones((1, H, 1, 1), dtype=jnp.float32) * 0.5
        return {'x': x, 'W_fx': W_fx, 'b_fx': b_fx, 'W_x': W_x, 'b_x': b_x, 'W_slice': W_slice, 'b_slice': b_slice, 'W_q': W_q, 'W_k': W_k, 'W_v': W_v, 'W_out': W_out, 'b_out': b_out, 'temperature': temperature}
    _L1_ffn_all = _L1_ffn_setup()
    _L1_ffn_in = {k: v for k, v in _L1_ffn_all.items() if k in ('W_fx', 'b_fx', 'W_x', 'b_x', 'W_slice', 'b_slice', 'W_q', 'W_k', 'W_v', 'W_out', 'b_out', 'temperature')}
    del _L1_ffn_all
    return {'x': x, 'src': src, 'dst': dst, 'edge_weight': edge_weight, 'L0_gnn_w1': _L0_gnn_in['w1'], 'L0_gnn_gamma1': _L0_gnn_in['gamma1'], 'L0_gnn_beta1': _L0_gnn_in['beta1'], 'L0_gnn_w2': _L0_gnn_in['w2'], 'L0_gnn_eps_weight': _L0_gnn_in['eps_weight'], 'L0_gnn_gamma_h': _L0_gnn_in['gamma_h'], 'L0_gnn_beta_h': _L0_gnn_in['beta_h'], 'L0_mix_wq': _L0_mix_in['wq'], 'L0_mix_bq': _L0_mix_in['bq'], 'L0_mix_wk': _L0_mix_in['wk'], 'L0_mix_bk': _L0_mix_in['bk'], 'L0_mix_wv': _L0_mix_in['wv'], 'L0_mix_bv': _L0_mix_in['bv'], 'L0_mix_wo': _L0_mix_in['wo'], 'L0_mix_bo': _L0_mix_in['bo'], 'L0_ffn_router_w': _L0_ffn_in['router_w'], 'L0_ffn_router_b': _L0_ffn_in['router_b'], 'L0_ffn_W1': _L0_ffn_in['W1'], 'L0_ffn_b1': _L0_ffn_in['b1'], 'L0_ffn_W2': _L0_ffn_in['W2'], 'L0_ffn_b2': _L0_ffn_in['b2'], 'L1_gnn_W1': _L1_gnn_in['W1'], 'L1_gnn_b1': _L1_gnn_in['b1'], 'L1_gnn_W2': _L1_gnn_in['W2'], 'L1_gnn_b2': _L1_gnn_in['b2'], 'L1_mix_W_qk': _L1_mix_in['W_qk'], 'L1_mix_b_qk': _L1_mix_in['b_qk'], 'L1_mix_W_v': _L1_mix_in['W_v'], 'L1_mix_b_v': _L1_mix_in['b_v'], 'L1_mix_gamma': _L1_mix_in['gamma'], 'L1_mix_beta': _L1_mix_in['beta'], 'L1_ffn_W_fx': _L1_ffn_in['W_fx'], 'L1_ffn_b_fx': _L1_ffn_in['b_fx'], 'L1_ffn_W_x': _L1_ffn_in['W_x'], 'L1_ffn_b_x': _L1_ffn_in['b_x'], 'L1_ffn_W_slice': _L1_ffn_in['W_slice'], 'L1_ffn_b_slice': _L1_ffn_in['b_slice'], 'L1_ffn_W_q': _L1_ffn_in['W_q'], 'L1_ffn_W_k': _L1_ffn_in['W_k'], 'L1_ffn_W_v': _L1_ffn_in['W_v'], 'L1_ffn_W_out': _L1_ffn_in['W_out'], 'L1_ffn_b_out': _L1_ffn_in['b_out'], 'L1_ffn_temperature': _L1_ffn_in['temperature']}

def reference(x, src, dst, edge_weight, L0_gnn_w1, L0_gnn_gamma1, L0_gnn_beta1, L0_gnn_w2, L0_gnn_eps_weight, L0_gnn_gamma_h, L0_gnn_beta_h, L0_mix_wq, L0_mix_bq, L0_mix_wk, L0_mix_bk, L0_mix_wv, L0_mix_bv, L0_mix_wo, L0_mix_bo, L0_ffn_router_w, L0_ffn_router_b, L0_ffn_W1, L0_ffn_b1, L0_ffn_W2, L0_ffn_b2, L1_gnn_W1, L1_gnn_b1, L1_gnn_W2, L1_gnn_b2, L1_mix_W_qk, L1_mix_b_qk, L1_mix_W_v, L1_mix_b_v, L1_mix_gamma, L1_mix_beta, L1_ffn_W_fx, L1_ffn_b_fx, L1_ffn_W_x, L1_ffn_b_x, L1_ffn_W_slice, L1_ffn_b_slice, L1_ffn_W_q, L1_ffn_W_k, L1_ffn_W_v, L1_ffn_W_out, L1_ffn_b_out, L1_ffn_temperature):
    import jax
    import jax.numpy as jnp

    def _L0_gnn_ref(x, edge_src, edge_dst, edge_vals, n_norm, w1, gamma1, beta1, w2, eps_weight, gamma_h, beta_h):
        import jax, jax.numpy as jnp
        import numpy as np
        BN_EPS = 1e-05

        def _batchnorm(h, gamma, beta):
            mean = jnp.mean(h, axis=0, keepdims=True)
            var = jnp.var(h, axis=0, keepdims=True)
            return (h - mean) * jax.lax.rsqrt(var + BN_EPS) * gamma + beta
        N = x.shape[0]
        msgs = edge_vals[:, None] * x[edge_src]
        agg = jax.ops.segment_sum(msgs, edge_dst, num_segments=N)
        y = agg + eps_weight * x
        h = jax.nn.relu(_batchnorm(y @ w1.T, gamma1, beta1))
        y = h @ w2.T
        y = y * n_norm
        y = _batchnorm(y, gamma_h, beta_h)
        y = jax.nn.relu(y)
        y = y + x
        return y

    def _L0_mix_ref(x, wq, bq, wk, bk, wv, bv, wo, bo):
        import jax, jax.numpy as jnp
        import numpy as np
        D_MODEL = 256
        NUM_HEADS = 8
        DEPTH = D_MODEL // NUM_HEADS
        B, L = (32, 256)

        def _feature_map(x):
            return jax.nn.elu(x) + 1.0
        b, l, _ = x.shape
        q = (x @ wq + bq).reshape(b, l, NUM_HEADS, DEPTH)
        k = (x @ wk + bk).reshape(b, l, NUM_HEADS, DEPTH)
        v = (x @ wv + bv).reshape(b, l, NUM_HEADS, DEPTH)
        q = _feature_map(q)
        k = _feature_map(k)
        kv = jnp.einsum('blhd,blhe->bhde', k, v)
        k_sum = jnp.sum(k, axis=1)
        qkv = jnp.einsum('blhd,bhde->blhe', q, kv)
        normalizer = jnp.einsum('blhd,bhd->blh', q, k_sum) + 1e-06
        out = qkv / normalizer[..., None]
        out = out.reshape(b, l, D_MODEL)
        return out @ wo + bo

    def _L0_ffn_ref(x, router_w, router_b, W1, b1, W2, b2):
        import jax, jax.numpy as jnp
        import numpy as np
        B, K, D = (512, 16, 256)
        E = 32
        H = int(D * 0.25)
        xf = x.reshape(-1, D)
        logits = xf @ router_w.T + router_b
        idx = jnp.argmax(logits, axis=-1)
        w1t = jnp.take(W1, idx, axis=0)
        h = jnp.einsum('nd,ndh->nh', xf, w1t) + jnp.take(b1, idx, axis=0)
        h = jax.nn.relu(h)
        w2t = jnp.take(W2, idx, axis=0)
        out = jnp.einsum('nh,nhd->nd', h, w2t) + jnp.take(b2, idx, axis=0)
        out = jax.nn.relu(out)
        return out.reshape(x.shape)

    def _L1_gnn_ref(x, edge_index, edge_weight, W1, b1, W2, b2):
        import jax, jax.numpy as jnp
        import numpy as np
        N_NODES = 3125
        N_EDGES = 100000
        F_IN = 256
        F_OUT = 256

        def _gcn_conv(x, src, dst, ew, W, b, n_nodes):
            xW = x @ W
            deg = jax.ops.segment_sum(ew, dst, num_segments=n_nodes) + 1.0
            dinv = jnp.where(deg > 0, jax.lax.rsqrt(deg), 0.0)
            norm = dinv[src] * ew * dinv[dst]
            agg = jax.ops.segment_sum(norm[:, None] * xW[src], dst, num_segments=n_nodes)
            agg = agg + (dinv * dinv)[:, None] * xW
            return agg + b
        src = edge_index[0]
        dst = edge_index[1]
        n = x.shape[0]
        h1 = jax.nn.relu(_gcn_conv(x, src, dst, edge_weight, W1, b1, n))
        h2 = jax.nn.relu(_gcn_conv(h1, src, dst, edge_weight, W2, b2, n))
        return h2

    def _L1_mix_ref(feature, W_qk, b_qk, W_v, b_v, gamma, beta):
        import jax, jax.numpy as jnp
        import numpy as np
        BN_EPS = 1e-05
        QK = jnp.einsum('bnd,kde->bkne', feature, W_qk) + b_qk[None, :, None, :]
        value = jnp.einsum('bnd,de->bne', feature, W_v) + b_v
        query = QK[:, 0]
        key = QK[:, 1]
        sm = jax.nn.softmax(key, axis=1)
        lam = jnp.einsum('bnd,bne->bde', sm, value)
        mean = jnp.mean(lam, axis=(0, 2), keepdims=True)
        var = jnp.var(lam, axis=(0, 2), keepdims=True)
        bn = (lam - mean) * jax.lax.rsqrt(var + BN_EPS)
        bn = bn * gamma[None, :, None] + beta[None, :, None]
        return jnp.einsum('bnd,bde->bne', query, bn)

    def _L1_ffn_ref(x, W_fx, b_fx, W_x, b_x, W_slice, b_slice, W_q, W_k, W_v, W_out, b_out, temperature):
        import jax, jax.numpy as jnp
        import numpy as np
        DIM = 256
        H = 8
        D = 64
        G = 64
        INNER = H * D
        SCALE = D ** (-0.5)
        B, N, _ = x.shape
        fx_mid = (x @ W_fx + b_fx).reshape(B, N, H, D).transpose(0, 2, 1, 3)
        x_mid = (x @ W_x + b_x).reshape(B, N, H, D).transpose(0, 2, 1, 3)
        temp = jnp.clip(temperature, 0.1, 5.0)
        slice_weights = jax.nn.softmax((x_mid @ W_slice + b_slice) / temp, axis=-1)
        slice_norm = slice_weights.sum(axis=2)
        slice_token = jnp.einsum('bhnc,bhng->bhgc', fx_mid, slice_weights)
        slice_token = slice_token / (slice_norm[..., None] + 1e-05)
        q = slice_token @ W_q
        k = slice_token @ W_k
        v = slice_token @ W_v
        attn = jax.nn.softmax(jnp.einsum('bhgc,bhkc->bhgk', q, k) * SCALE, axis=-1)
        out_slice = jnp.einsum('bhgk,bhkc->bhgc', attn, v)
        out_x = jnp.einsum('bhgc,bhng->bhnc', out_slice, slice_weights)
        out_x = out_x.transpose(0, 2, 1, 3).reshape(B, N, INNER)
        return out_x @ W_out + b_out
    edge_index = jnp.stack([src, dst])
    deg = jnp.maximum(jax.ops.segment_sum(jnp.ones(dst.shape, jnp.float32), dst, num_segments=6250), 1.0)
    deg_isqrt = deg ** (-0.5)
    xn = _layernorm(x, axis=-1)
    x = x + _L0_gnn_ref(xn, src, dst, edge_weight, deg_isqrt[:, None], L0_gnn_w1, L0_gnn_gamma1, L0_gnn_beta1, L0_gnn_w2, L0_gnn_eps_weight, L0_gnn_gamma_h, L0_gnn_beta_h) + _L0_mix_ref(xn[None], L0_mix_wq, L0_mix_bq, L0_mix_wk, L0_mix_bk, L0_mix_wv, L0_mix_bv, L0_mix_wo, L0_mix_bo)[0]
    x = x + _L0_ffn_ref(_layernorm(x, axis=-1)[None], L0_ffn_router_w, L0_ffn_router_b, L0_ffn_W1, L0_ffn_b1, L0_ffn_W2, L0_ffn_b2)[0]
    xn = _layernorm(x, axis=-1)
    x = x + _L1_gnn_ref(xn, edge_index, edge_weight, L1_gnn_W1, L1_gnn_b1, L1_gnn_W2, L1_gnn_b2) + _L1_mix_ref(xn[None], L1_mix_W_qk, L1_mix_b_qk, L1_mix_W_v, L1_mix_b_v, L1_mix_gamma, L1_mix_beta)[0]
    x = x + _L1_ffn_ref(_layernorm(x, axis=-1)[None], L1_ffn_W_fx, L1_ffn_b_fx, L1_ffn_W_x, L1_ffn_b_x, L1_ffn_W_slice, L1_ffn_b_slice, L1_ffn_W_q, L1_ffn_W_k, L1_ffn_W_v, L1_ffn_W_out, L1_ffn_b_out, L1_ffn_temperature)[0]
    return x

_drawn_inputs = setup_inputs


def setup_inputs(seed=0):
    import zlib

    import numpy as np

    out = dict(_drawn_inputs(seed))
    spreads = {'L0_gnn_gamma1': (1.0, 0.2),
     'L0_gnn_beta1': (0.0, 0.1),
     'L0_gnn_gamma_h': (1.0, 0.2),
     'L0_gnn_beta_h': (0.0, 0.1),
     'L0_mix_bq': (0.0, 0.8),
     'L0_mix_bk': (0.0, 0.8),
     'L0_mix_bv': (0.0, 0.1),
     'L0_mix_bo': (0.0, 0.1),
     'L1_gnn_b1': (0.0, 0.8),
     'L1_gnn_b2': (0.0, 0.8),
     'L1_mix_b_qk': (0.0, 0.1),
     'L1_mix_b_v': (0.0, 0.1),
     'L1_mix_gamma': (1.0, 0.2),
     'L1_mix_beta': (0.0, 0.8),
     'L1_ffn_b_fx': (0.0, 0.8),
     'L1_ffn_b_x': (0.0, 0.8),
     'L1_ffn_b_slice': (0.0, 0.8),
     'L1_ffn_b_out': (0.0, 2.0),
     'L1_ffn_temperature': (0.5, 0.6)}
    factors = {'L0_mix_wq': 8.0,
     'L0_ffn_b1': 8.0,
     'L0_ffn_b2': 3.453,
     'L1_gnn_W1': 8.0,
     'L1_gnn_W2': 8.0,
     'L1_ffn_W_fx': 7.349,
     'L1_ffn_W_x': 8.0,
     'L1_ffn_W_slice': 8.0,
     'L1_ffn_W_q': 8.0,
     'L1_ffn_W_k': 7.11,
     'L1_ffn_W_v': 5.276,
     'L1_ffn_W_out': 5.528}
    for name, (base, spread) in spreads.items():
        noise = np.random.default_rng([zlib.crc32(name.encode()), seed]).standard_normal(out[name].shape)
        drawn = base * np.exp(spread * noise) if base else spread * noise
        out[name] = jnp.asarray(drawn.astype(out[name].dtype))
    for name, factor in factors.items():
        out[name] = (out[name] * factor).astype(out[name].dtype)
    return out
```

```python
from contextlib import ExitStack

import concourse.bass as bass
from concourse import mybir

F32 = mybir.dt.float32
I32 = mybir.dt.int32
ALU = mybir.AluOpType
ACT = mybir.ActivationFunctionType
AX = mybir.AxisListType

N, E, D = 6250, 100000, 256
P = 128
C = D // P
BODY = 2 * P
FULL = N // BODY
LAST = N - FULL * BODY
NTILE = 2 * FULL + 1
GT = 8
GE = GT * P
NG = -(-E // GE)
NET = NG * GT
AW = D + 3
FAR = 65536.0
HEADS, EXPERTS, HID = 8, 32, 64
SLICES, SDIM = 64, 64
LN_EPS = 1e-5
POOL_DMA = ("stored", "scattered")


def wait(eng, sem, value, gate=None):
    if isinstance(value, int):
        if value > 0:
            eng.wait_ge(sem, value)
        return
    eng.wait_ge(sem, value)
    if gate is not None:
        eng.sem_inc(gate, 1)


def bodies(eng, body):
    body(0, (P, P))
    with eng.Fori(1, FULL) as i:
        body(i, (P, P))
    body(FULL, (LAST,))


def rows(ap, i, tiles, width=None):
    if len(tiles) == 2:
        return ap[bass.ds(i * BODY, BODY), :].rearrange("(j p) d -> p j d", p=P)
    return ap[FULL * BODY:N, :].rearrange("(j p) d -> p j d", j=1)


def bcast_rows(ap, n):
    return bass.AP(tensor=ap.tensor, offset=ap.offset, ap=[[0, P], [1, n]])


class Kit:
    pass


class Stage:

    def __init__(self, nc, kit):
        self.nc, self.kit, self.ctx, self.sems = nc, kit, ExitStack(), []
        kit.stages += 1
        self.tag = f"_{kit.stages}"

    def __enter__(self):
        return self

    def __exit__(self, *exc):
        if exc[0] is None and self.sems:
            with self.nc.Block() as block:
                @block.gpsimd
                def _(pool):
                    for s in self.sems:
                        pool.sem_clear(s)
        self.ctx.close()

    def sem(self, name):
        if name in POOL_DMA:
            return self.pool_dma(name)
        s = self.ctx.enter_context(self.nc.semaphore(name + self.tag))
        self.sems.append(s)
        return s

    def pool_dma(self, name):
        return self.kit.ctx.enter_context(self.nc.semaphore(name + self.tag))

    def sb(self, name, shape, dt=F32):
        return self.ctx.enter_context(self.nc.sbuf_tensor(name + self.tag, shape, dt))


class Norm:

    def __init__(self, st, tag, src, src_ready, src_step=1):
        self.src, self.src_ready, self.src_step = src, src_ready, src_step
        self.stat = st.sb(f"stat{tag}", [P, 2, 6])
        self.mv = st.sb(f"mv{tag}", [P, 2, 2])
        self.sd = st.sb(f"sd{tag}", [P, 2])
        self.rs = st.sb(f"rs{tag}", [P, 2])
        self.xn = st.sb(f"xn{tag}", [P, 2, D])
        self.stats_done = st.sem(f"stats_done{tag}")
        self.moments_done = st.sem(f"moments_done{tag}")
        self.sd_done = st.sem(f"sd_done{tag}")
        self.rs_done = st.sem(f"rs_done{tag}")
        self.xn_done = st.sem(f"xn_done{tag}")
        self.gate = st.sem(f"gate{tag}")
        self.kit = st.kit

    def dve_moments(self, eng, i, tiles):
        wait(eng, self.src_ready, (i + 1) * self.src_step)
        for j, w in enumerate(tiles):
            ins = eng.bn_stats(self.stat[0:w, j, :], self.src[0:w, j, :])
        ins.then_inc(self.stats_done, 1)
        wait(eng, self.stats_done, i + 1)
        wait(eng, self.sd_done, i)
        wait(eng, self.xn_done, i, self.gate)
        for j, w in enumerate(tiles):
            ins = eng.bn_aggr(self.mv[0:w, j, :], self.stat[0:w, j, :])
        ins.then_inc(self.moments_done, 1)

    def act_sd(self, eng, i, tiles):
        w, n = tiles[0], len(tiles)
        wait(eng, self.moments_done, i + 1)
        wait(eng, self.rs_done, i)
        eng.activation(self.sd[0:w, 0:n], self.mv[0:w, 0:n, 1], ACT.Sqrt,
                       bias=self.kit.eps[0:w, :]).then_inc(self.sd_done, 1)

    def dve_normalise(self, eng, i, tiles, used=()):
        w, n = tiles[0], len(tiles)
        wait(eng, self.sd_done, i + 1)
        wait(eng, self.xn_done, i)
        eng.reciprocal(self.rs[0:w, 0:n], self.sd[0:w, 0:n]).then_inc(self.rs_done, 1)
        wait(eng, self.rs_done, i + 1)
        for sem, step in used:
            wait(eng, sem, i * step)
        for j, w in enumerate(tiles):
            ins = eng.tensor_scalar(self.xn[0:w, j, :], self.src[0:w, j, :], self.mv[0:w, j, 0:1],
                                    self.rs[0:w, j:j + 1], ALU.subtract, ALU.mult)
        ins.then_inc(self.xn_done, 1)


def pe_turn(kit, eng, bank, src, tiles, done):
    for j, w in enumerate(tiles):
        for c in range(C):
            ins = eng.transpose(bank[:, c * BODY + j * P:c * BODY + j * P + w],
                                src[0:w, j, c * P:(c + 1) * P], kit.ident[0:w, 0:w])
    ins.then_inc(done, 1)


def halves(ap):
    return ap.rearrange("p (c n) -> p c n", c=C)


def project(eng, out, wT, x, w, m=None, n=D):
    for c in range(C):
        ins = eng.matmul(out, x(c), w(c), start=(c == 0), stop=(c == C - 1))
    return ins


def stage_setup(nc, kit, a, d):
    k = kit
    with Stage(nc, kit) as st:
        raw = {n: st.sb("raw_" + n, [P, C, D]) for n in ("L0_gnn_w1", "L0_gnn_w2", "L1_q")}
        wx = st.sb("wx", [P, C, 2 * D])
        bxb = st.sb("bxb", [SDIM, HEADS, P])
        wxT = st.sb("wxT", [SDIM, HEADS, D])
        bxc = st.sb("bxc", [SDIM, HEADS])
        src_f = st.sb("src_f", [P, NET])
        rraw = st.sb("rraw", [EXPERTS, D])
        epad_i = st.sb("epad_i", [P, 2, GE], I32)
        esrc = st.sb("esrc", [P, GE])
        edst = st.sb("edst", [P, GE])
        eew = st.sb("eew", [P, GE])
        chg = st.sb("chg", [P, GE])
        zed = st.sb("zed", [P, GE])
        rank = st.sb("rank", [P, GE])
        fd = st.sb("fd", [P, GE])
        tmp = st.sb("tmp", [P, GE])
        okc = st.sb("okc", [P, 4])
        mset, cst, idn = st.sem("mset"), st.sem("cst"), st.sem("idn")
        wld, eld = st.sem("wld"), st.sem("eld")
        step = st.sem("step")
        tdone, cdone = st.sem("tdone"), st.sem("cdone")
        nload = [0]

        with nc.Block() as block:
            @block.sync
            def _(sp):
                def load(dst, src):
                    sp.dma_start(dst, src, allow_slow_non_contiguous=True).then_inc(wld, 16)
                    nload[0] += 1
                full, rest = E // GE, E % GE
                sp.wait_ge(mset, 1)
                for n, name in enumerate(("src", "dst")):
                    sp.dma_start(epad_i[0:full, n, :], a[name][0:full * GE].rearrange("(g e) -> g e", e=GE)).then_inc(eld, 16)
                    sp.dma_start(epad_i[full:full + 1, n, 0:rest], a[name][full * GE:E].rearrange("(g e) -> g e", g=1)).then_inc(eld, 16)
                sp.dma_start(eew[0:full, :], a["edge_weight"][0:full * GE].rearrange("(g e) -> g e", e=GE)).then_inc(eld, 16)
                sp.dma_start(eew[full:full + 1, 0:rest], a["edge_weight"][full * GE:E].rearrange("(g e) -> g e", g=1)).then_inc(eld, 16)
                sp.wait_ge(eld, 96)
                sq = lambda ap: ap.rearrange("(c p) n -> p c n", p=P)
                load(raw["L0_gnn_w1"][:], sq(a["L0_gnn_w1"]))
                load(raw["L0_gnn_w2"][:], sq(a["L0_gnn_w2"]))
                load(raw["L1_q"][:], sq(a["L1_mix_W_qk"][0]))
                load(rraw[:], a["L0_ffn_router_w"])
                load(k.wq0[:], sq(a["L0_mix_wq"]))
                load(k.wkv0[:, :, 0:D], sq(a["L0_mix_wk"]))
                load(k.wkv0[:, :, D:2 * D], sq(a["L0_mix_wv"]))
                load(k.wo0[:], sq(a["L0_mix_wo"]))
                load(k.rb[:], bcast_rows(a["L0_ffn_router_b"], EXPERTS))
                load(k.wg1[:], sq(a["L1_gnn_W1"]))
                load(k.wg2[:], sq(a["L1_gnn_W2"]))
                load(k.wkv1[:, :, 0:D], sq(a["L1_mix_W_qk"][1]))
                load(k.wkv1[:, :, D:2 * D], sq(a["L1_mix_W_v"]))
                load(k.wfx[:], sq(a["L1_ffn_W_fx"]))
                load(wx[:], sq(a["L1_ffn_W_x"]))
                load(k.wout[:], a["L1_ffn_W_out"].rearrange("(h c) n -> c h n", c=SDIM))
                for dst, name in ((k.wslice, "L1_ffn_W_slice"), (k.wsq, "L1_ffn_W_q"), (k.wsk, "L1_ffn_W_k"), (k.wsv, "L1_ffn_W_v")):
                    load(dst[:], a[name])
                load(k.bkv0[:, 0:D], bcast_rows(a["L0_mix_bk"], D))
                load(k.bkv0[:, D:2 * D], bcast_rows(a["L0_mix_bv"], D))
                load(k.bk1row[:], bcast_rows(a["L1_mix_b_qk"][1], D))
                load(k.bkv1[:, D:2 * D], bcast_rows(a["L1_mix_b_v"], D))
                load(k.bg1[:], bcast_rows(a["L1_gnn_b1"], D))
                load(k.bg2[:], bcast_rows(a["L1_gnn_b2"], D))
                load(k.bout[:], bcast_rows(a["L1_ffn_b_out"], D))
                load(k.bfx[:], a["L1_ffn_b_fx"].rearrange("(a n) -> a n", a=1))
                load(k.bslice_row[:], bcast_rows(a["L1_ffn_b_slice"], SLICES))
                load(k.temp[:], bcast_rows(a["L1_ffn_temperature"].rearrange("a h b c -> (a h b c)"), HEADS))
                load(k.epsw[:], bcast_rows(a["L0_gnn_eps_weight"], 1))
                cols = ((k.g1c, "L0_gnn_gamma1"), (k.be1c, "L0_gnn_beta1"), (k.ghc, "L0_gnn_gamma_h"), (k.behc, "L0_gnn_beta_h"),
                        (k.bqc, "L0_mix_bq"), (k.boc, "L0_mix_bo"), (k.gmc, "L1_mix_gamma"), (k.bemc, "L1_mix_beta"))
                for dst, name in cols:
                    load(dst[:], a[name].rearrange("(c p) -> p c", p=P))
                load(k.bq1c[:], a["L1_mix_b_qk"][0].rearrange("(c p) -> p c", p=P))
                load(k.bk1c[:], a["L1_mix_b_qk"][1].rearrange("(c p) -> p c", p=P))
                load(bxc[:], a["L1_ffn_b_x"].rearrange("(h c) -> c h", c=SDIM))
                sp.dma_start(d.dst.rearrange("(g e) -> g e", e=GE), epad_i[0:NG, 1, :]).then_inc(eld, 16)
                sp.wait_ge(eld, 112)
                sp.wait_ge(wld, 16 * nload[0])

            @block.gpsimd
            def _(pool):
                pool.memset(epad_i[:, 0, :], 0).then_inc(cst, 1)
                pool.memset(epad_i[:, 1, :], N).then_inc(cst, 1)
                pool.memset(eew[:], 0.0).then_inc(cst, 1)
                pool.wait_ge(cst, 3)
                pool.sem_inc(mset, 1)
                pool.memset(k.ident[:], 0.0).then_inc(idn, 1)
                pool.wait_ge(idn, 1)
                pool.memset(k.tri[:], 1.0).then_inc(idn, 1)
                pool.wait_ge(idn, 2)
                pool.memset(k.hmask[:], 0.0).then_inc(idn, 1)
                pool.wait_ge(idn, 3)
                pool.memset(k.far[:], 0.0).then_inc(idn, 1)
                pool.wait_ge(idn, 4)
                pool.affine_select(out=k.ident[:], in_=k.ident[:], compare_op=ALU.not_equal, fill=1.0, base=0,
                                   pattern=[[-1, P]], channel_multiplier=1).then_inc(idn, 1)
                pool.wait_ge(idn, 5)
                pool.affine_select(out=k.tri[:], in_=k.tri[:], compare_op=ALU.is_gt, fill=0.0, base=0,
                                   pattern=[[-1, P]], channel_multiplier=1).then_inc(idn, 1)
                pool.wait_ge(idn, 6)
                for h in range(4):
                    pool.memset(k.hmask[32 * h:32 * h + 32, 32 * h:32 * h + 32], 1.0).then_inc(idn, 1)
                    pool.wait_ge(idn, 7 + h)
                pool.affine_select(out=k.far[:].rearrange("p (e h) -> p e h", h=HID), in_=k.far[:].rearrange("p (e h) -> p e h", h=HID),
                                   compare_op=ALU.not_equal, fill=-1e30, base=0,
                                   pattern=[[-1, EXPERTS], [0, HID]], channel_multiplier=1).then_inc(idn, 1)
                pool.wait_ge(idn, 11)
                pool.iota(k.iota_i[:], [[1, P]], base=0, channel_multiplier=0).then_inc(idn, 1)
                pool.wait_ge(idn, 12)
                pool.memset(k.ones[:], 1.0).then_inc(idn, 1)
                pool.wait_ge(idn, 13)
                pool.memset(k.zeros[:], 0.0).then_inc(idn, 1)
                pool.wait_ge(idn, 14)
                pool.memset(k.eps[:], LN_EPS).then_inc(idn, 1)
                pool.wait_ge(idn, 15)
                pool.memset(zed[:], 0.0).then_inc(idn, 1)
                pool.wait_ge(idn, 16)

            @block.vector
            def _(dve):
                n = [0]

                def then(ins):
                    n[0] += 1
                    ins.then_inc(step, 1)
                    dve.wait_ge(step, n[0])
                dve.wait_ge(idn, 16)
                then(dve.tensor_copy(k.iota[:], k.iota_i[:]))
                dve.wait_ge(eld, 96)
                then(dve.tensor_copy(esrc[0:NG, :], epad_i[0:NG, 0, :]))
                then(dve.tensor_copy(edst[0:NG, :], epad_i[0:NG, 1, :]))
                then(dve.memset(chg[:], 0.0))
                then(dve.tensor_tensor(chg[0:NG, 1:GE], edst[0:NG, 1:GE], edst[0:NG, 0:GE - 1], ALU.not_equal))
                then(dve.tensor_tensor_scan(rank[0:NG, :], chg[0:NG, :], zed[0:NG, :], 0.0, ALU.add, ALU.add))
                then(dve.memset(tmp[:], 0.0))
                then(dve.tensor_tensor(tmp[0:NG, 1:GE], edst[0:NG, 1:GE], edst[0:NG, 0:GE - 1], ALU.subtract))
                then(dve.tensor_reduce(okc[0:NG, 0:1], tmp[0:NG, :], AX.X, ALU.min))
                then(dve.tensor_scalar(okc[0:NG, 1:2], okc[0:NG, 0:1], 0.0, None, ALU.is_ge))
                then(dve.tensor_scalar(okc[0:NG, 2:3], rank[0:NG, GE - 1:GE], float(P - 1), None, ALU.is_le))
                then(dve.tensor_tensor(okc[0:NG, 3:4], okc[0:NG, 1:2], okc[0:NG, 2:3], ALU.mult))
                then(dve.memset(chg[:, 0:1], 1.0))
                then(dve.scalar_tensor_tensor(out=fd[0:NG, :], in0=edst[0:NG, :], scalar=-FAR, in1=chg[0:NG, :], op0=ALU.add, op1=ALU.mult))
                then(dve.memset(k.ext[:], 1.0))
                dst = ((src_f, esrc), (k.dst_f, edst), (k.rank_f, rank), (k.ew_f, eew), (k.fd_f, fd))
                kk = 0
                for out, _ in dst:
                    for u in range(GT):
                        dve.wait_ge(tdone, kk + 1)
                        dve.tensor_copy(out[:].rearrange("p (g u) -> p g u", u=GT)[:, :, u], k.bank[kk % 2][:, 0:NG]).then_inc(cdone, 1)
                        kk += 1
                dve.wait_ge(cdone, kk)
                then(dve.tensor_copy(k.src_i[:], src_f[:]))
                then(dve.tensor_copy(k.dst_i[:], k.dst_f[:]))
                then(dve.tensor_copy(k.ext[:, :, 0], k.ew_f[:]))
                then(dve.tensor_copy(k.ext[:, :, 2], k.fd_f[:]))
                dve.wait_ge(tdone, kk + 1)
                dve.tensor_scalar(k.flag[0:1, :], k.bank[kk % 2][0:1, 0:1], float(NG), None, ALU.is_equal).then_inc(cdone, 1)
                kk += 1
                for out in (k.w1T, k.w2T, k.wq1T):
                    for c in range(C):
                        dve.wait_ge(tdone, kk + 1)
                        dve.tensor_copy(out[:, c, :], k.bank[kk % 2][:, 0:D]).then_inc(cdone, 1)
                        kk += 1
                for c in range(C):
                    dve.wait_ge(tdone, kk + 1)
                    dve.tensor_copy(k.rT[:, c, :], k.bank[kk % 2][:, 0:EXPERTS]).then_inc(cdone, 1)
                    kk += 1
                dve.wait_ge(wld, 16 * nload[0])
                then(dve.memset(k.wdeg[:], 1.0))
                then(dve.tensor_scalar(k.temp[:], k.temp[:], 0.1, 5.0, ALU.max, ALU.min))
                then(dve.reciprocal(k.rtemp[:], k.temp[:]))
                for h in range(HEADS):
                    dve.wait_ge(tdone, kk + 1)
                    dve.tensor_copy(wxT[:, h, :], k.bank[kk % 2][0:SDIM, 0:D]).then_inc(cdone, 1)
                    kk += 1
                    for c in range(C):
                        dve.wait_ge(tdone, kk + 1)
                        dve.tensor_scalar(k.wxs[:, c, h * SLICES:(h + 1) * SLICES], k.bank[kk % 2][:, 0:SLICES],
                                          k.rtemp[:, h:h + 1], None, ALU.mult).then_inc(cdone, 1)
                        kk += 1
                    dve.wait_ge(tdone, kk + 1)
                    then(dve.tensor_tensor(k.bxs[:, h * SLICES:(h + 1) * SLICES], k.bank[kk % 2][:, 0:SLICES], k.bslice_row[:], ALU.add))
                    dve.tensor_scalar(k.bxs[:, h * SLICES:(h + 1) * SLICES], k.bxs[:, h * SLICES:(h + 1) * SLICES],
                                      k.rtemp[:, h:h + 1], None, ALU.mult).then_inc(cdone, 1)
                    kk += 1

            @block.scalar
            def _(act):
                act.wait_ge(wld, 16 * nload[0])
                act.wait_ge(idn, 16)
                for h in range(HEADS):
                    act.activation(bxb[:, h, :], k.ones[0:SDIM, :], ACT.Copy, scale=bxc[:, h:h + 1]).then_inc(cst, 1)

            @block.tensor
            def _(pe):
                pe.wait_ge(idn, 16)
                kk = 0

                def go():
                    nonlocal kk
                    if kk >= 2:
                        pe.wait_ge(cdone, kk - 1)
                    kk += 1
                    return k.bank[(kk - 1) % 2]
                pe.wait_ge(step, 14)
                for x in (esrc, edst, rank, eew, fd):
                    for u in range(GT):
                        b = go()
                        pe.transpose(b[:, 0:NG], x[0:NG, u * P:(u + 1) * P], k.ident[0:NG, 0:NG]).then_inc(tdone, 1)
                b = go()
                pe.matmul(b[0:1, 0:1], okc[0:NG, 3:4], k.ones[0:NG, 0:1], start=True, stop=True).then_inc(tdone, 1)
                pe.wait_ge(wld, 16 * nload[0])
                for x in (raw["L0_gnn_w1"], raw["L0_gnn_w2"], raw["L1_q"]):
                    for c in range(C):
                        b = go()
                        for o in range(C):
                            ins = pe.transpose(b[:, o * P:(o + 1) * P], x[:, o, c * P:(c + 1) * P], k.ident[:])
                        ins.then_inc(tdone, 1)
                for c in range(C):
                    b = go()
                    pe.transpose(b[:, 0:EXPERTS], rraw[:, c * P:(c + 1) * P], k.ident[0:EXPERTS, 0:EXPERTS]).then_inc(tdone, 1)
                for h in range(HEADS):
                    b = go()
                    for c in range(C):
                        ins = pe.transpose(b[0:SDIM, c * P:(c + 1) * P], wx[:, c, h * SDIM:(h + 1) * SDIM], k.ident[:])
                    ins.then_inc(tdone, 1)
                    for c in range(C):
                        b = go()
                        if c == 0:
                            pe.wait_ge(cdone, kk - 1)
                        pe.matmul(b[:, 0:SLICES], wxT[:, h, c * P:(c + 1) * P], k.wslice[:], start=True, stop=True).then_inc(tdone, 1)
                    b = go()
                    if h == 0:
                        pe.wait_ge(cst, 3 + HEADS)
                    pe.matmul(b[:, 0:SLICES], bxb[:, h, :], k.wslice[:], start=True, stop=True).then_inc(tdone, 1)


def stage_front(nc, kit, a, d):
    k = kit
    with Stage(nc, kit) as st:
        xt = st.sb("xt", [P, 2, D])
        xnT = st.sb("xnT", [P, C, BODY])
        z = st.sb("z", [P, 2, D])
        mn = st.sb("mn", [P, 2, D])
        kf = st.sb("kf", [P, 2, D])
        v = st.sb("v", [P, 2, D])
        loaded, stored = st.sem("loaded"), st.sem("stored")
        nm = Norm(st, "a", xt, loaded, 16)
        turned, xnT_done = st.sem("turned"), st.sem("xnT_done")
        kv_done, z_done, mn_done, e_done, kf_done, sum_done = (st.sem(s) for s in ("kv_done", "z_done", "mn_done", "e_done", "kf_done", "sum_done"))
        gsp, gpool = st.sem("gsp"), st.sem("gpool")
        with nc.Block() as block:
            @block.sync
            def _(sp):
                def body(i, tiles):
                    wait(sp, nm.xn_done, i, gsp)
                    sp.dma_start(xt[0:tiles[0], 0:len(tiles), :], rows(a["x"], i, tiles)).then_inc(loaded, 16)
                bodies(sp, body)

            @block.gpsimd
            def _(pool):
                def body(i, tiles):
                    wait(pool, nm.xn_done, i + 1, gpool)
                    pool.dma_start(rows(d.xn, i, tiles), nm.xn[0:tiles[0], 0:len(tiles), :]).then_inc(stored, 16)
                bodies(pool, body)
                pool.wait_ge(stored, 16 * (FULL + 1))

            @block.vector
            def _(dve):
                def body(i, tiles):
                    nm.dve_moments(dve, i, tiles)
                    nm.dve_normalise(dve, i, tiles, [(stored, 16), (turned, 1)])
                    wait(dve, kv_done, i + 1)
                    wait(dve, sum_done, i)
                    for j, w in enumerate(tiles):
                        dve.tensor_tensor(v[0:w, j, :], k.bank[1 + j][0:w, D:2 * D], k.bkv0[0:w, D:2 * D], ALU.add)
                        ins = dve.tensor_tensor(z[0:w, j, :], k.bank[1 + j][0:w, 0:D], k.bkv0[0:w, 0:D], ALU.add)
                    ins.then_inc(z_done, 1)
                    wait(dve, z_done, i + 1)
                    w, n = tiles[0], len(tiles)
                    dve.tensor_scalar(mn[0:w, 0:n, :], z[0:w, 0:n, :], 0.0, None, ALU.min).then_inc(mn_done, 1)
                    wait(dve, e_done, i + 1)
                    dve.scalar_tensor_tensor(out=kf[0:w, 0:n, :], in0=z[0:w, 0:n, :], scalar=0.0, in1=mn[0:w, 0:n, :],
                                             op0=ALU.max, op1=ALU.add).then_inc(kf_done, 1)
                bodies(dve, body)

            @block.scalar
            def _(act):
                def body(i, tiles):
                    w, n = tiles[0], len(tiles)
                    nm.act_sd(act, i, tiles)
                    wait(act, turned, i + 1)
                    wait(act, kv_done, i)
                    for c in range(C):
                        ins = act.activation(xnT[:, c, 0:sum(tiles)], k.bank[0][:, c * BODY:c * BODY + sum(tiles)], ACT.Copy)
                    ins.then_inc(xnT_done, 1)
                    wait(act, mn_done, i + 1)
                    act.activation(mn[0:w, 0:n, :], mn[0:w, 0:n, :], ACT.Exp).then_inc(e_done, 1)
                bodies(act, body)

            @block.tensor
            def _(pe):
                def body(i, tiles):
                    wait(pe, nm.xn_done, i + 1)
                    wait(pe, xnT_done, i)
                    pe_turn(k, pe, k.bank[0], nm.xn, tiles, turned)
                    wait(pe, xnT_done, i + 1)
                    wait(pe, z_done, i)
                    for j, w in enumerate(tiles):
                        for c in range(C):
                            ins = pe.matmul(k.bank[1 + j][0:w, :], xnT[:, c, j * P:j * P + w], k.wkv0[:, c, :], start=(c == 0), stop=(c == C - 1))
                    ins.then_inc(kv_done, 1)
                    wait(pe, kf_done, i + 1)
                    first, last = isinstance(i, int) and i == 0, isinstance(i, int) and i == FULL
                    for j, w in enumerate(tiles):
                        for c in range(C):
                            f = slice(c * P, (c + 1) * P)
                            pe.matmul(k.bank[3 + c][:, 0:P], v[0:w, j, f], kf[0:w, j, f], start=first and j == 0, stop=last)
                            ins = pe.matmul(k.bank[5 + c][:, 0:1], kf[0:w, j, f], k.ones[0:w, 0:1], start=first and j == 0, stop=last)
                    ins.then_inc(sum_done, 1)
                bodies(pe, body)
        kvm = st.sb("kvm", [P, C, P])
        s1, s2, s3 = st.sem("masked"), st.sem("m0_done"), st.sem("m0_out")
        with nc.Block() as block:
            @block.vector
            def _(dve):
                for c in range(C):
                    dve.tensor_tensor(kvm[:, c, :], k.bank[3 + c][:, 0:P], k.hmask[:], ALU.mult)
                    dve.tensor_scalar(k.ks[:, c, :], k.hmask[:], k.bank[5 + c][:, 0:1], None, ALU.mult).then_inc(s1, 1)
                for c in range(C):
                    dve.wait_ge(s2, c + 1)
                    dve.tensor_copy(k.m0[:, c, :], k.bank[c][:, 0:D]).then_inc(s3, 1)

            @block.tensor
            def _(pe):
                pe.wait_ge(s1, C)
                for c in range(C):
                    pe.matmul(k.bank[c][:, 0:D], kvm[:, c, :], k.wo0[:, c, :], start=True, stop=True).then_inc(s2, 1)


def stage_clear(nc, kit, d):
    with Stage(nc, kit) as st:
        done = st.sem("cleared")
        with nc.Block() as block:
            @block.sync
            def _(sp):
                for n in range(7):
                    r = NTILE * P // 7
                    sp.dma_start(d.acc[n * r:(n + 1) * r, :].rearrange("(p t) w -> p (t w)", p=P), kit.zeros[:]).then_inc(done, 16)
                sp.wait_ge(done, 7 * 16)


def stage_aggregate(nc, kit, a, d, table):
    k = kit
    stage_clear(nc, kit, d)
    with Stage(nc, kit) as st:
        fast = st.ctx.enter_context(ExitStack())

        def sb(name, shape, dt=F32):
            return fast.enter_context(nc.sbuf_tensor(name + st.tag, shape, dt))
        gidx = [sb(f"gidx{h}", [P, GT], I32) for h in range(2)]
        sidx = [sb(f"sidx{h}", [P, 1], I32) for h in range(2)]
        g = [sb(f"g{u}", [P, D]) for u in range(2 * GT)]
        gw = [sb(f"gw{h}", [P, GT, AW]) for h in range(2)]
        m = [sb(f"m{u}", [P, P]) for u in range(2 * GT)]
        r = [sb(f"r{h}", [P, AW]) for h in range(2)]
        gathered = [st.pool_dma(f"gathered{u}") for u in range(2 * GT)]
        idx_done, ext_done, m_done, weighted, multiplied, row_done, scattered = (
            st.sem(s) for s in ("idx_done", "ext_done", "m_done", "weighted", "multiplied", "row_done", "scattered"))
        gpool, gact = st.sem("gpool"), st.sem("gact")
        NB = NG // 2
        drow = sb("drow", [P, P], I32)
        dup = sb("dup", [P, P])
        ndup = sb("ndup", [P, 1])
        row_loaded, dup_done = st.sem("row_loaded"), st.sem("dup_done")
        gsp = st.sem("gsp")

        def loop(eng, body):
            body(0)
            with eng.Fori(1, NB) as i:
                body(i)

        def fast_pool(pool):
            def scatter(i, h):
                grp = 2 * i + h
                wait(pool, row_done, grp + 1, gpool)
                wait(pool, scattered, 16 * grp, gpool)
                pool.indirect_dma_start(d.acc, bass.IndirectOffsetOnAxis(ap=sidx[h][:], axis=0), r[h][:], None,
                                        bounds_check=N - 1, oob_is_err=False, compute_op=ALU.add).then_inc(scattered, 16)

            def body(i):
                for h in range(2):
                    wait(pool, idx_done, 2 * i + h + 1, gpool)
                    for u in range(GT):
                        s = h * GT + u
                        wait(pool, weighted, 16 * i + s - 15, gpool)
                        pool.indirect_dma_start(g[s][:], None, table, bass.IndirectOffsetOnAxis(ap=gidx[h][:, u:u + 1], axis=0)).then_inc(gathered[s], 16)
                    if h == 1:
                        scatter(i, 0)
                    elif not (isinstance(i, int) and i == 0):
                        scatter(i - 1, 1)
            loop(pool, body)
            scatter(NB - 1, 1)
            pool.wait_ge(scattered, 16 * NG)

        def fast_act(act):
            def body(i):
                for s in range(2 * GT):
                    wait(act, multiplied, 16 * i + s - 15, gact)
                    wait(act, gathered[s], 16 * (i + 1), gact)
                    act.activation(gw[s // GT][:, s % GT, 0:D], g[s][:], ACT.Copy, scale=k.ew_f[:, bass.ds(i * 16 + s, 1)]).then_inc(weighted, 1)
            loop(act, body)

        def fast_dve(dve):
            def prepare(i, h):
                wait(dve, weighted, 16 * i + 8 * h - 8)
                dve.tensor_copy(gidx[h][:], k.src_i[:, bass.ds(i * 16 + h * 8, 8)]).then_inc(idx_done, 1)
                wait(dve, multiplied, 16 * i + 8 * h - 8)
                dve.tensor_copy(gw[h][:, :, D:AW], k.ext[:, bass.ds(i * 16 + h * 8, 8), :]).then_inc(ext_done, 1)
                for u in range(GT):
                    dve.tensor_scalar(m[h * GT + u][:], k.iota[:], k.rank_f[:, bass.ds(i * 16 + h * 8 + u, 1)], None, ALU.is_equal).then_inc(m_done, 1)

            def finish(i, h):
                wait(dve, multiplied, 16 * i + 8 * h + 8)
                wait(dve, scattered, 16 * (2 * i + h - 1))
                dve.tensor_scalar(sidx[h][:], k.bank[h][:, AW - 1:AW], FAR, None, ALU.add)
                dve.tensor_copy(r[h][:], k.bank[h][:, 0:AW]).then_inc(row_done, 1)

            def body(i):
                prepare(i, 0)
                if not (isinstance(i, int) and i == 0):
                    finish(i - 1, 1)
                prepare(i, 1)
                finish(i, 0)
            loop(dve, body)
            finish(NB - 1, 1)

        def fast_pe(pe):
            def body(i):
                for s in range(2 * GT):
                    h, u = s // GT, s % GT
                    if u == 0:
                        wait(pe, ext_done, 2 * i + h + 1)
                        wait(pe, row_done, 2 * i + h - 1)
                    wait(pe, m_done, 16 * i + s + 1)
                    wait(pe, weighted, 16 * i + s + 1)
                    pe.matmul(k.bank[h][:, 0:AW], m[s][:], gw[h][:, u, :], start=(u == 0), stop=(u == GT - 1)).then_inc(multiplied, 1)
            loop(pe, body)

        def tiles_of_edges(eng, body):
            body(0)
            with eng.Fori(1, NET) as t:
                body(t)

        def general_sp(sp):
            def body(t):
                wait(sp, m_done, t, gsp)
                wait(sp, dup_done, 2 * t, gsp)
                sp.dma_start(drow[:], bass.AP(tensor=d.dst.tensor, offset=t * P, ap=[[0, P], [1, P]])).then_inc(row_loaded, 16)
            tiles_of_edges(sp, body)

        def general_pool(pool):
            def body(t):
                wait(pool, idx_done, t + 1, gpool)
                wait(pool, weighted, t, gpool)
                pool.indirect_dma_start(g[0][:], None, table, bass.IndirectOffsetOnAxis(ap=gidx[0][:, 0:1], axis=0)).then_inc(gathered[0], 16)
                wait(pool, row_done, t + 1, gpool)
                wait(pool, scattered, 16 * t, gpool)
                pool.indirect_dma_start(d.acc, bass.IndirectOffsetOnAxis(ap=sidx[0][:], axis=0), r[0][:], None,
                                        bounds_check=N - 1, oob_is_err=False, compute_op=ALU.add).then_inc(scattered, 16)
            tiles_of_edges(pool, body)
            pool.wait_ge(scattered, 16 * NET)

        def general_act(act):
            def body(t):
                wait(act, multiplied, t, gact)
                wait(act, gathered[0], 16 * (t + 1), gact)
                act.activation(gw[0][:, 0, 0:D], g[0][:], ACT.Copy, scale=k.ew_f[:, bass.ds(t, 1)]).then_inc(weighted, 1)
            tiles_of_edges(act, body)

        def general_dve(dve):
            def body(t):
                wait(dve, weighted, t)
                dve.tensor_copy(gidx[0][:, 0:1], k.src_i[:, bass.ds(t, 1)]).then_inc(idx_done, 1)
                wait(dve, multiplied, t)
                dve.tensor_copy(gw[0][:, 0:1, D:AW], k.ext[:, bass.ds(t, 1), :]).then_inc(ext_done, 1)
                wait(dve, row_loaded, 16 * (t + 1))
                dve.tensor_scalar(m[0][:], drow[:], k.dst_f[:, bass.ds(t, 1)], None, ALU.is_equal).then_inc(m_done, 1)
                wait(dve, dup_done, 2 * t)
                wait(dve, m_done, t + 1)
                dve.tensor_tensor(dup[:], m[0][:], k.tri[:], ALU.mult).then_inc(dup_done, 1)
                wait(dve, dup_done, 2 * t + 1)
                wait(dve, row_done, t)
                dve.tensor_reduce(ndup[:], dup[:], AX.X, ALU.add).then_inc(dup_done, 1)
                wait(dve, dup_done, 2 * t + 2)
                wait(dve, scattered, 16 * t)
                dve.scalar_tensor_tensor(out=sidx[0][:], in0=ndup[:], scalar=FAR, in1=k.dst_f[:, bass.ds(t, 1)], op0=ALU.mult, op1=ALU.add)
                wait(dve, multiplied, t + 1)
                dve.tensor_copy(r[0][:], k.bank[0][:, 0:AW]).then_inc(row_done, 1)
            tiles_of_edges(dve, body)

        def general_pe(pe):
            def body(t):
                wait(pe, ext_done, t + 1)
                wait(pe, row_done, t)
                wait(pe, m_done, t + 1)
                wait(pe, weighted, t + 1)
                pe.matmul(k.bank[0][:, 0:AW], m[0][:], gw[0][:, 0, :], start=True, stop=True).then_inc(multiplied, 1)
            tiles_of_edges(pe, body)

        def either(eng, fast_path, general_path):
            grouped = eng.value_load(k.flag[0:1, 0:1])
            with eng.If(grouped == 1):
                fast_path(eng)
            with eng.Else():
                general_path(eng)

        with nc.Block() as block:
            @block.sync
            def _(sp):
                either(sp, lambda eng: eng.nop(), general_sp)

            @block.gpsimd
            def _(pool):
                either(pool, fast_pool, general_pool)

            @block.scalar
            def _(act):
                either(act, fast_act, general_act)

            @block.vector
            def _(dve):
                either(dve, fast_dve, general_dve)

            @block.tensor
            def _(pe):
                either(pe, fast_pe, general_pe)


def coefficients(nc, st, kit, stats, gamma, beta, scale, shift, tag):
    mv = st.sb("bmv" + tag, [P, C, 2])
    sd = st.sb("bsd" + tag, [P, C])
    s1, s2, s3 = st.sem("bm" + tag), st.sem("bs" + tag), st.sem("bc" + tag)
    with nc.Block() as block:
        @block.vector
        def _(dve):
            for c in range(C):
                ins = dve.bn_aggr(mv[:, c, :], stats[:, c, :, :].rearrange("p i s -> p (i s)"))
            ins.then_inc(s1, 1)
            dve.wait_ge(s2, 1)
            dve.reciprocal(sd[:], sd[:]).then_inc(s3, 1)
            dve.wait_ge(s3, 1)
            dve.tensor_tensor(scale[:], sd[:], gamma[:], ALU.mult).then_inc(s3, 1)
            dve.wait_ge(s3, 2)
            dve.tensor_tensor(sd[:], mv[:, :, 0], scale[:], ALU.mult).then_inc(s3, 1)
            dve.wait_ge(s3, 3)
            dve.tensor_tensor(shift[:], beta[:], sd[:], ALU.subtract).then_inc(s3, 1)

        @block.scalar
        def _(act):
            act.wait_ge(s1, 1)
            act.activation(sd[:], mv[:, :, 1], ACT.Sqrt, bias=kit.eps[:]).then_inc(s2, 1)


def stage_gnn_first(nc, kit, a, d):
    k = kit
    with Stage(nc, kit) as st:
        at = st.sb("at", [P, 2, AW])
        xn = st.sb("xnb", [P, 2, D])
        y = st.sb("y", [P, 2, D])
        yT = st.sb("yT", [P, C, BODY])
        cnt = st.sb("cnt", [P, 2])
        nnb = st.sb("nnb", [P, 2, P])
        stats = st.sb("stats", [P, C, FULL + 1, 6])
        loaded, y_done, cnt_done, root_done, rn_done, nnb_done, turned, yT_done, z_done, kept, nbc_done, nkept, stat_done, wd_done = (
            st.sem(s) for s in ("loaded", "y_done", "cnt_done", "root_done", "rn_done", "nnb_done", "turned", "yT_done", "z_done", "kept", "nbc_done", "nkept", "stat_done", "wd_done"))
        gsp, gact, gdve = st.sem("gsp"), st.sem("gact"), st.sem("gdve")
        with nc.Block() as block:
            @block.sync
            def _(sp):
                def body(i, tiles):
                    w, n = tiles[0], len(tiles)
                    wait(sp, y_done, i, gsp)
                    wait(sp, wd_done, i, gsp)
                    sp.dma_start(at[0:w, 0:n, :], rows(d.acc, i, tiles)).then_inc(loaded, 16)
                    sp.dma_start(xn[0:w, 0:n, :], rows(d.xn, i, tiles)).then_inc(loaded, 16)
                bodies(sp, body)

            @block.vector
            def _(dve):
                def body(i, tiles):
                    w, n, wt = tiles[0], len(tiles), sum(tiles)
                    wait(dve, loaded, 32 * (i + 1))
                    wait(dve, nnb_done, i)
                    dve.tensor_scalar(cnt[0:w, 0:n], at[0:w, 0:n, D + 1], 1.0, None, ALU.max).then_inc(cnt_done, 1)
                    dve.tensor_copy(k.wdeg[0:w, bass.ds(i * 2, n)], at[0:w, 0:n, D]).then_inc(wd_done, 1)
                    wait(dve, turned, i)
                    dve.scalar_tensor_tensor(out=y[0:w, 0:n, :], in0=xn[0:w, 0:n, :], scalar=k.epsw[0:w, :], in1=at[0:w, 0:n, 0:D],
                                             op0=ALU.mult, op1=ALU.add).then_inc(y_done, 1)
                    wait(dve, root_done, i + 1)
                    dve.reciprocal(cnt[0:w, 0:n], cnt[0:w, 0:n]).then_inc(rn_done, 1)
                    wait(dve, rn_done, i + 1)
                    wait(dve, nbc_done, i)
                    for j in range(n):
                        ins = dve.tensor_scalar(nnb[0:w, j, :], k.ones[0:w, :], cnt[0:w, j:j + 1], None, ALU.mult)
                    ins.then_inc(nnb_done, 1)
                    wait(dve, kept, i + 1, gdve)
                    for c in range(C):
                        ins = dve.bn_stats(stats[:, c, i, :] if isinstance(i, int) else stats[:, c, bass.ds(i, 1), :].rearrange("p a s -> p (a s)"),
                                           k.bank[1 + c][:, 0:wt])
                    ins.then_inc(stat_done, 1)
                bodies(dve, body)

            @block.scalar
            def _(act):
                def body(i, tiles):
                    w, n, wt = tiles[0], len(tiles), sum(tiles)
                    wait(act, cnt_done, i + 1)
                    act.activation(cnt[0:w, 0:n], cnt[0:w, 0:n], ACT.Sqrt).then_inc(root_done, 1)
                    wait(act, turned, i + 1)
                    wait(act, z_done, i)
                    act.activation(yT[:, :, 0:wt], halves(k.bank[0][:])[:, :, 0:wt], ACT.Copy).then_inc(yT_done, 1)
                    wait(act, z_done, i + 1, gact)
                    for c in range(C):
                        ins = act.activation(k.zT[:, c, bass.ds(i * BODY, wt)], k.bank[1 + c][:, 0:wt], ACT.Copy)
                    ins.then_inc(kept, 1)
                    wait(act, nbc_done, i + 1, gact)
                    act.activation(k.nbc[:, bass.ds(i * BODY, wt)], k.bank[3][:, 0:wt], ACT.Copy).then_inc(nkept, 1)
                bodies(act, body)

            @block.tensor
            def _(pe):
                def body(i, tiles):
                    wt = sum(tiles)
                    wait(pe, y_done, i + 1)
                    wait(pe, yT_done, i)
                    pe_turn(k, pe, k.bank[0], y, tiles, turned)
                    wait(pe, yT_done, i + 1)
                    wait(pe, kept, i)
                    wait(pe, stat_done, i)
                    for o in range(C):
                        for c in range(C):
                            ins = pe.matmul(k.bank[1 + o][:, 0:wt], k.w1T[:, c, o * P:(o + 1) * P], yT[:, c, 0:wt], start=(c == 0), stop=(c == C - 1))
                    ins.then_inc(z_done, 1)
                    wait(pe, nnb_done, i + 1)
                    wait(pe, nkept, i)
                    for j, w in enumerate(tiles):
                        ins = pe.matmul(k.bank[3][:, j * P:j * P + w], nnb[0:w, j, :], k.ident[0:w, 0:w], start=True, stop=True)
                    ins.then_inc(nbc_done, 1)
                bodies(pe, body)
        coefficients(nc, st, kit, stats, k.g1c, k.be1c, k.s1, k.t1, "1")
        c1, c2 = st.sem("dg"), st.sem("dgs")
        pos = st.sb("pos", [P, NTILE + 1])
        with nc.Block() as block:
            @block.vector
            def _(dve):
                dve.tensor_scalar(k.wdeg[:], k.wdeg[:], 1.0, None, ALU.add).then_inc(c1, 1)
                dve.wait_ge(c1, 1)
                dve.tensor_scalar(pos[:], k.wdeg[:], 0.0, None, ALU.is_gt).then_inc(c1, 1)
                dve.wait_ge(c1, 2)
                dve.tensor_scalar(k.wdeg[:], k.wdeg[:], 1e-30, None, ALU.max).then_inc(c1, 1)
                dve.wait_ge(c2, 1)
                dve.reciprocal(k.wdeg[:], k.wdeg[:]).then_inc(c1, 1)
                dve.wait_ge(c1, 4)
                dve.tensor_tensor(k.wdeg[:], k.wdeg[:], pos[:], ALU.mult).then_inc(c1, 1)

            @block.scalar
            def _(act):
                act.wait_ge(c1, 3)
                act.activation(k.wdeg[:], k.wdeg[:], ACT.Sqrt).then_inc(c2, 1)


def stage_gnn_second(nc, kit, a, d):
    k = kit
    with Stage(nc, kit) as st:
        hT = st.sb("hT", [P, C, BODY])
        stats = st.sb("stats", [P, C, FULL + 1, 6])
        h_done, u_done, kept, stat_done = (st.sem(s) for s in ("h_done", "u_done", "kept", "stat_done"))
        gact, gdve = st.sem("gact"), st.sem("gdve")
        with nc.Block() as block:
            @block.scalar
            def _(act):
                def body(i, tiles):
                    wt = sum(tiles)
                    wait(act, u_done, i, gact)
                    for c in range(C):
                        ins = act.activation(hT[:, c, 0:wt], k.zT[:, c, bass.ds(i * BODY, wt)], ACT.Relu, bias=k.t1[:, c:c + 1], scale=k.s1[:, c:c + 1])
                    ins.then_inc(h_done, 1)
                bodies(act, body)

            @block.vector
            def _(dve):
                def body(i, tiles):
                    wt = sum(tiles)
                    wait(dve, u_done, i + 1, gdve)
                    for c in range(C):
                        ins = dve.tensor_tensor(k.zT[:, c, bass.ds(i * BODY, wt)], k.bank[c][:, 0:wt], k.nbc[:, bass.ds(i * BODY, wt)], ALU.mult)
                    ins.then_inc(kept, 1)
                    wait(dve, kept, i + 1, gdve)
                    for c in range(C):
                        ins = dve.bn_stats(stats[:, c, i, :] if isinstance(i, int) else stats[:, c, bass.ds(i, 1), :].rearrange("p a s -> p (a s)"),
                                           k.zT[:, c, bass.ds(i * BODY, wt)])
                    ins.then_inc(stat_done, 1)
                bodies(dve, body)

            @block.tensor
            def _(pe):
                def body(i, tiles):
                    wt = sum(tiles)
                    wait(pe, h_done, i + 1)
                    wait(pe, kept, i)
                    for o in range(C):
                        for c in range(C):
                            ins = pe.matmul(k.bank[o][:, 0:wt], k.w2T[:, c, o * P:(o + 1) * P], hT[:, c, 0:wt], start=(c == 0), stop=(c == C - 1))
                    ins.then_inc(u_done, 1)
                bodies(pe, body)
        coefficients(nc, st, kit, stats, k.ghc, k.behc, k.s2, k.t2, "2")


def stage_gnn_mix(nc, kit, a, d):
    k = kit
    with Stage(nc, kit) as st:
        xt = st.sb("xt", [P, 2, D])
        xn = st.sb("xnc", [P, 2, D])
        xnT = st.sb("xnT", [P, C, BODY])
        rT = st.sb("reluT", [P, C, BODY])
        qm = st.sb("qm", [P, C, BODY])
        qp = st.sb("qp", [P, C, BODY])
        nr = st.sb("nr", [P, C, BODY])
        s = st.sb("s", [P, C, BODY])
        x1 = st.sb("x1", [P, 2, D])
        (loaded, turned, xnT_done, q_done, qm_done, qe_done, q_read, qf_done, nrm_done, nr_done, rec_done, qn_done, r_done, mix_done, s_done, back_done, x1a_done, x1_done, stored) = (
            st.sem(n) for n in ("loaded turned xnT_done q_done qm_done qe_done q_read qf_done nrm_done nr_done rec_done qn_done r_done mix_done s_done back_done x1a_done x1_done stored").split())
        gsp, gact, gpool = st.sem("gsp"), st.sem("gact"), st.sem("gpool")
        with nc.Block() as block:
            @block.sync
            def _(sp):
                def body(i, tiles):
                    w, n = tiles[0], len(tiles)
                    wait(sp, x1_done, i, gsp)
                    wait(sp, turned, i, gsp)
                    sp.dma_start(xn[0:w, 0:n, :], rows(d.xn, i, tiles)).then_inc(loaded, 16)
                    sp.dma_start(xt[0:w, 0:n, :], rows(a["x"], i, tiles)).then_inc(loaded, 16)
                bodies(sp, body)

            @block.gpsimd
            def _(pool):
                def body(i, tiles):
                    w, n = tiles[0], len(tiles)
                    wait(pool, x1_done, i + 1, gpool)
                    pool.dma_start(rows(d.x1, i, tiles), x1[0:w, 0:n, :]).then_inc(stored, 16)
                bodies(pool, body)
                pool.wait_ge(stored, 16 * (FULL + 1))

            @block.scalar
            def _(act):
                def body(i, tiles):
                    wt = sum(tiles)
                    wait(act, turned, i + 1)
                    wait(act, q_done, i)
                    act.activation(xnT[:, :, 0:wt], halves(k.bank[0][:])[:, :, 0:wt], ACT.Copy).then_inc(xnT_done, 1)
                    wait(act, s_done, i, gact)
                    for c in range(C):
                        ins = act.activation(rT[:, c, 0:wt], k.zT[:, c, bass.ds(i * BODY, wt)], ACT.Relu, bias=k.t2[:, c:c + 1], scale=k.s2[:, c:c + 1])
                    ins.then_inc(r_done, 1)
                    wait(act, qm_done, i + 1)
                    act.activation(qm[:, :, 0:wt], qm[:, :, 0:wt], ACT.Exp).then_inc(qe_done, 1)
                bodies(act, body)

            @block.vector
            def _(dve):
                def body(i, tiles):
                    w, n, wt = tiles[0], len(tiles), sum(tiles)
                    wait(dve, q_done, i + 1)
                    wait(dve, mix_done, i)
                    for c in range(C):
                        dve.tensor_scalar(qm[:, c, 0:wt], k.bank[1 + c][:, 0:wt], k.bqc[:, c:c + 1], 0.0, ALU.add, ALU.min)
                    ins = dve.tensor_scalar(qp[:, 0, 0:wt], k.bank[1][:, 0:wt], k.bqc[:, 0:1], 0.0, ALU.add, ALU.max)
                    ins.then_inc(qm_done, 1)
                    ins = dve.tensor_scalar(qp[:, 1, 0:wt], k.bank[2][:, 0:wt], k.bqc[:, 1:2], 0.0, ALU.add, ALU.max)
                    ins.then_inc(q_read, 1)
                    wait(dve, q_read, i + 1)
                    wait(dve, qe_done, i + 1)
                    dve.tensor_tensor(qp[:, :, 0:wt], qp[:, :, 0:wt], qm[:, :, 0:wt], ALU.add).then_inc(qf_done, 1)
                    wait(dve, nrm_done, i + 1)
                    dve.tensor_scalar(nr[:, :, 0:wt], halves(k.bank[3][:])[:, :, 0:wt], 1e-6, None, ALU.add).then_inc(nr_done, 1)
                    wait(dve, nr_done, i + 1)
                    dve.reciprocal(nr[:, :, 0:wt], nr[:, :, 0:wt]).then_inc(rec_done, 1)
                    wait(dve, rec_done, i + 1)
                    dve.tensor_tensor(qp[:, :, 0:wt], qp[:, :, 0:wt], nr[:, :, 0:wt], ALU.mult).then_inc(qn_done, 1)
                    wait(dve, mix_done, i + 1)
                    wait(dve, r_done, i + 1)
                    wait(dve, back_done, i)
                    for c in range(C):
                        ins = dve.scalar_tensor_tensor(out=s[:, c, 0:wt], in0=k.bank[4 + c][:, 0:wt], scalar=k.boc[:, c:c + 1], in1=rT[:, c, 0:wt], op0=ALU.add, op1=ALU.add)
                    ins.then_inc(s_done, 1)
                    wait(dve, loaded, 32 * (i + 1))
                    wait(dve, back_done, i + 1)
                    wait(dve, stored, 16 * i)
                    dve.tensor_tensor(x1[0:w, 0:n, :], k.bank[6][0:w, 0:n * D].rearrange("p (j d) -> p j d", d=D), xt[0:w, 0:n, :], ALU.add).then_inc(x1a_done, 1)
                    wait(dve, x1a_done, i + 1)
                    dve.tensor_tensor(x1[0:w, 0:n, :], x1[0:w, 0:n, :], xn[0:w, 0:n, :], ALU.add).then_inc(x1_done, 1)
                bodies(dve, body)

            @block.tensor
            def _(pe):
                def body(i, tiles):
                    wt = sum(tiles)
                    wait(pe, loaded, 32 * (i + 1))
                    wait(pe, xnT_done, i)
                    pe_turn(k, pe, k.bank[0], xn, tiles, turned)
                    wait(pe, xnT_done, i + 1)
                    wait(pe, q_read, i)
                    for o in range(C):
                        for c in range(C):
                            ins = pe.matmul(k.bank[1 + o][:, 0:wt], k.wq0[:, c, o * P:(o + 1) * P], xnT[:, c, 0:wt], start=(c == 0), stop=(c == C - 1))
                    ins.then_inc(q_done, 1)
                    wait(pe, qf_done, i + 1)
                    wait(pe, nr_done, i)
                    for c in range(C):
                        ins = pe.matmul(k.bank[3][:, c * BODY:c * BODY + wt], k.ks[:, c, :], qp[:, c, 0:wt], start=True, stop=True)
                    ins.then_inc(nrm_done, 1)
                    wait(pe, qn_done, i + 1)
                    wait(pe, s_done, i)
                    for o in range(C):
                        for c in range(C):
                            ins = pe.matmul(k.bank[4 + o][:, 0:wt], k.m0[:, c, o * P:(o + 1) * P], qp[:, c, 0:wt], start=(c == 0), stop=(c == C - 1))
                    ins.then_inc(mix_done, 1)
                    wait(pe, s_done, i + 1)
                    wait(pe, x1a_done, i)
                    for j, w in enumerate(tiles):
                        for c in range(C):
                            ins = pe.transpose(k.bank[6][0:w, j * D + c * P:j * D + (c + 1) * P], s[:, c, j * P:j * P + w], k.ident[:])
                    ins.then_inc(back_done, 1)
                bodies(pe, body)


def stage_experts(nc, kit, a, d):
    k = kit
    NBLK = EXPERTS * HID // P
    with Stage(nc, kit) as st:
        xt = st.sb("xt", [P, 2, D])
        x2 = st.sb("x2", [P, 2, D])
        xnT = st.sb("xnT", [P, C, BODY])
        wm1 = st.sb("wm1", [P, C, EXPERTS * HID])
        wm2 = st.sb("wm2", [P, NBLK, D])
        b1m = st.sb("b1m", [P, NBLK])
        b2m = st.sb("b2m", [EXPERTS, D])
        lg = st.sb("lg", [P, 2, EXPERTS])
        top = st.sb("top", [P, 2, 8])
        topi = st.sb("topi", [P, 2, 8], mybir.dt.uint32)
        topf = st.sb("topf", [P, 2, 1])
        one = st.sb("one", [P, 2, EXPERTS])
        oneT = st.sb("oneT", [EXPERTS, BODY])
        offT = st.sb("offT", [EXPERTS, BODY])
        hT = [st.sb(f"hT{b}", [P, BODY]) for b in range(4)]
        loaded = st.sem("loaded")
        nm = Norm(st, "d", xt, loaded, 16)
        (turned, xnT_done, lg_psum, lg_done, top_done, topi_done, topf_done, one_done, one_turned, oneT_done, hid_done, h_done, fed, relu_done, x2_done, stored) = (
            st.sem(n) for n in "turned xnT_done lg_psum lg_done top_done topi_done topf_done one_done one_turned oneT_done hid_done h_done fed relu_done x2_done stored".split())
        gsp, gpool, gdve, wloaded = st.sem("gsp"), st.sem("gpool"), st.sem("gdve"), st.sem("wloaded")
        with nc.Block() as block:
            @block.sync
            def _(sp):
                for c in range(C):
                    sp.dma_start(wm1[:, c, :].rearrange("p (e h) -> p e h", e=EXPERTS),
                                 a["L0_ffn_W1"][:, c * P:(c + 1) * P, :].rearrange("e d h -> d e h")).then_inc(wloaded, 16)
                sp.dma_start(wm2[:], a["L0_ffn_W2"].rearrange("(b two) h d -> (two h) b d", two=2)).then_inc(wloaded, 16)
                sp.dma_start(b1m[:], a["L0_ffn_b1"].rearrange("(b two) h -> (two h) b", two=2), allow_slow_non_contiguous=True).then_inc(wloaded, 16)
                sp.dma_start(b2m[:], a["L0_ffn_b2"]).then_inc(wloaded, 16)

                def body(i, tiles):
                    wait(sp, x2_done, i, gsp)
                    sp.dma_start(xt[0:tiles[0], 0:len(tiles), :], rows(d.x1, i, tiles)).then_inc(loaded, 16)
                bodies(sp, body)

            @block.gpsimd
            def _(pool):
                def body(i, tiles):
                    w, n = tiles[0], len(tiles)
                    wait(pool, x2_done, i + 1, gpool)
                    pool.dma_start(rows(d.x2, i, tiles), x2[0:w, 0:n, :]).then_inc(stored, 16)
                bodies(pool, body)
                pool.wait_ge(stored, 16 * (FULL + 1))

            @block.scalar
            def _(act):
                act.wait_ge(wloaded, 16 * 5)

                def body(i, tiles):
                    w, n, wt = tiles[0], len(tiles), sum(tiles)
                    nm.act_sd(act, i, tiles)
                    wait(act, turned, i + 1)
                    wait(act, hid_done, NBLK * i)
                    act.activation(xnT[:, :, 0:wt], halves(k.bank[0][:])[:, :, 0:wt], ACT.Copy).then_inc(xnT_done, 1)
                    for b in range(NBLK):
                        wait(act, hid_done, NBLK * i + b + 1)
                        wait(act, fed, NBLK * i + b - 3)
                        act.activation(hT[b % 4][:, 0:wt], k.bank[2 + b % 4][:, 0:wt], ACT.Relu, bias=b1m[:, b:b + 1]).then_inc(h_done, 1)
                    wait(act, fed, NBLK * (i + 1))
                    wait(act, stored, 16 * i)
                    for j, wj in enumerate(tiles):
                        ins = act.activation(x2[0:wj, j, :], k.bank[6 + j][0:wj, 0:D], ACT.Relu)
                    ins.then_inc(relu_done, 1)
                bodies(act, body)

            @block.vector
            def _(dve):
                def body(i, tiles):
                    w, n, wt = tiles[0], len(tiles), sum(tiles)
                    nm.dve_moments(dve, i, tiles)
                    nm.dve_normalise(dve, i, tiles, [(turned, 1)])
                    wait(dve, lg_psum, i + 1)
                    wait(dve, topi_done, i)
                    for j in range(n):
                        ins = dve.tensor_tensor(lg[0:w, j, :], k.bank[1][0:w, j * EXPERTS:(j + 1) * EXPERTS], k.rb[0:w, :], ALU.add)
                    ins.then_inc(lg_done, 1)
                    wait(dve, lg_done, i + 1, gdve)
                    for j in range(n):
                        ins = dve.max(top[0:w, j, :], lg[0:w, j, :])
                    ins.then_inc(top_done, 1)
                    wait(dve, top_done, i + 1, gdve)
                    for j in range(n):
                        ins = dve.max_index(topi[0:w, j, :], top[0:w, j, :], lg[0:w, j, :])
                    ins.then_inc(topi_done, 1)
                    wait(dve, topi_done, i + 1)
                    dve.tensor_copy(topf[0:w, 0:n, :], topi[0:w, 0:n, 0:1]).then_inc(topf_done, 1)
                    wait(dve, topf_done, i + 1)
                    wait(dve, one_turned, i)
                    for j in range(n):
                        ins = dve.tensor_scalar(one[0:w, j, :], k.iota[0:w, 0:EXPERTS], topf[0:w, j, :], None, ALU.is_equal)
                    ins.then_inc(one_done, 1)
                    wait(dve, one_turned, i + 1)
                    wait(dve, fed, NBLK * i)
                    dve.tensor_copy(oneT[:, 0:wt], k.bank[1][0:EXPERTS, BODY:BODY + wt])
                    dve.tensor_scalar(offT[:, 0:wt], k.bank[1][0:EXPERTS, BODY:BODY + wt], -1.0, 1.0, ALU.mult, ALU.add).then_inc(oneT_done, 1)
                    wait(dve, relu_done, i + 1)
                    dve.tensor_tensor(x2[0:w, 0:n, :], x2[0:w, 0:n, :], xt[0:w, 0:n, :], ALU.add).then_inc(x2_done, 1)
                bodies(dve, body)

            @block.tensor
            def _(pe):
                pe.wait_ge(wloaded, 16 * 5)

                def body(i, tiles):
                    wt = sum(tiles)
                    wait(pe, nm.xn_done, i + 1)
                    wait(pe, xnT_done, i)
                    pe_turn(k, pe, k.bank[0], nm.xn, tiles, turned)
                    wait(pe, xnT_done, i + 1)
                    wait(pe, lg_done, i)
                    wait(pe, oneT_done, i)
                    for j, w in enumerate(tiles):
                        for c in range(C):
                            ins = pe.matmul(k.bank[1][0:w, j * EXPERTS:(j + 1) * EXPERTS], xnT[:, c, j * P:j * P + w], k.rT[:, c, :], start=(c == 0), stop=(c == C - 1))
                    ins.then_inc(lg_psum, 1)
                    wait(pe, one_done, i + 1)
                    wait(pe, oneT_done, i)
                    for j, w in enumerate(tiles):
                        ins = pe.transpose(k.bank[1][0:EXPERTS, BODY + j * P:BODY + j * P + w], one[0:w, j, :], k.ident[0:w, 0:w])
                    ins.then_inc(one_turned, 1)
                    wait(pe, oneT_done, i + 1)

                    def hidden(b):
                        wait(pe, h_done, NBLK * i + b - 3)
                        for c in range(C):
                            pe.matmul(k.bank[2 + b % 4][:, 0:wt], wm1[:, c, b * P:(b + 1) * P], xnT[:, c, 0:wt], start=(c == 0), stop=False)
                        pe.matmul(k.bank[2 + b % 4][:, 0:wt], k.far[:, b * P:(b + 1) * P], offT[:, 0:wt], start=False, stop=True).then_inc(hid_done, 1)

                    def feed(b):
                        wait(pe, h_done, NBLK * i + b + 1)
                        for j, w in enumerate(tiles):
                            ins = pe.matmul(k.bank[6 + j][0:w, 0:D], hT[b % 4][:, j * P:j * P + w], wm2[:, b, :], start=False, stop=(b == NBLK - 1))
                        ins.then_inc(fed, 1)
                    wait(pe, relu_done, i)
                    for j, w in enumerate(tiles):
                        pe.matmul(k.bank[6 + j][0:w, 0:D], oneT[:, j * P:j * P + w], b2m[:], start=True, stop=False)
                    for b in range(NBLK):
                        hidden(b)
                        if b >= 2:
                            feed(b - 2)
                    feed(NBLK - 2)
                    feed(NBLK - 1)
                bodies(pe, body)


def stage_second_front(nc, kit, a, d):
    k = kit
    with Stage(nc, kit) as st:
        xt = st.sb("xt", [P, 2, D])
        xnT = st.sb("xnT", [P, C, BODY])
        t = st.sb("t", [P, 2, D])
        kmax = st.sb("kmax", [P, C, FULL + 1])
        loaded = st.sem("loaded")
        nm = Norm(st, "e", xt, loaded, 16)
        turned, xnT_done, t_psum, t_done, stored, key_psum, max_done = (st.sem(n) for n in "turned xnT_done t_psum t_done stored key_psum max_done".split())
        gsp, gpool, gact, gdve = (st.sem(n) for n in "gsp gpool gact gdve".split())
        with nc.Block() as block:
            @block.sync
            def _(sp):
                def body(i, tiles):
                    wait(sp, nm.xn_done, i, gsp)
                    sp.dma_start(xt[0:tiles[0], 0:len(tiles), :], rows(d.x2, i, tiles)).then_inc(loaded, 16)
                bodies(sp, body)

            @block.gpsimd
            def _(pool):
                def body(i, tiles):
                    wait(pool, t_done, i + 1, gpool)
                    pool.dma_start(rows(d.t1, i, tiles), t[0:tiles[0], 0:len(tiles), :]).then_inc(stored, 16)
                bodies(pool, body)
                pool.wait_ge(stored, 16 * (FULL + 1))

            @block.scalar
            def _(act):
                def body(i, tiles):
                    wt = sum(tiles)
                    nm.act_sd(act, i, tiles)
                    wait(act, turned, i + 1)
                    wait(act, key_psum, i)
                    act.activation(xnT[:, :, 0:wt], halves(k.bank[0][:])[:, :, 0:wt], ACT.Copy).then_inc(xnT_done, 1)
                    wait(act, t_psum, i + 1)
                    wait(act, stored, 16 * i, gact)
                    for j, w in enumerate(tiles):
                        ins = act.activation(t[0:w, j, :], k.bank[1 + j][0:w, 0:D], ACT.Copy, scale=k.wdeg[0:w, bass.ds(i * 2 + j, 1)])
                    ins.then_inc(t_done, 1)
                bodies(act, body)

            @block.vector
            def _(dve):
                def body(i, tiles):
                    wt = sum(tiles)
                    nm.dve_moments(dve, i, tiles)
                    nm.dve_normalise(dve, i, tiles, [(turned, 1)])
                    wait(dve, key_psum, i + 1, gdve)
                    for c in range(C):
                        ins = dve.tensor_reduce(kmax[:, c, bass.ds(i, 1)], k.bank[3 + c][:, 0:wt], AX.X, ALU.max)
                    ins.then_inc(max_done, 1)
                bodies(dve, body)

            @block.tensor
            def _(pe):
                def body(i, tiles):
                    wt = sum(tiles)
                    wait(pe, nm.xn_done, i + 1)
                    wait(pe, xnT_done, i)
                    pe_turn(k, pe, k.bank[0], nm.xn, tiles, turned)
                    wait(pe, xnT_done, i + 1)
                    wait(pe, t_done, i)
                    for j, w in enumerate(tiles):
                        for c in range(C):
                            ins = pe.matmul(k.bank[1 + j][0:w, 0:D], xnT[:, c, j * P:j * P + w], k.wg1[:, c, :], start=(c == 0), stop=(c == C - 1))
                    ins.then_inc(t_psum, 1)
                    wait(pe, max_done, i)
                    for o in range(C):
                        for c in range(C):
                            ins = pe.matmul(k.bank[3 + o][:, 0:wt], k.wkv1[:, c, o * P:(o + 1) * P], xnT[:, c, 0:wt], start=(c == 0), stop=(c == C - 1))
                    ins.then_inc(key_psum, 1)
                bodies(pe, body)
        mx = st.sb("mx", [P, C])
        mb = st.sb("mb", [P, C, P])
        s1, s2 = st.sem("s1"), st.sem("s2")
        with nc.Block() as block:
            @block.vector
            def _(dve):
                dve.tensor_reduce(mx[:], kmax[:], AX.X, ALU.max).then_inc(s1, 1)
                dve.wait_ge(s1, 1)
                dve.tensor_tensor(mx[:], mx[:], k.bk1c[:], ALU.add).then_inc(s1, 1)
                dve.wait_ge(s1, 2)
                for c in range(C):
                    ins = dve.tensor_scalar(mb[:, c, :], k.ones[:], mx[:, c:c + 1], None, ALU.mult)
                ins.then_inc(s1, 1)
                dve.wait_ge(s2, 1)
                dve.tensor_tensor(k.bkv1[:, 0:D], k.bk1row[:], k.bank[0][:, 0:D], ALU.subtract).then_inc(s1, 1)

            @block.tensor
            def _(pe):
                pe.wait_ge(s1, 3)
                for c in range(C):
                    ins = pe.matmul(k.bank[0][:, c * P:(c + 1) * P], mb[:, c, :], k.ident[:], start=True, stop=True)
                ins.then_inc(s2, 1)


def stage_lambda(nc, kit, a, d):
    k = kit
    with Stage(nc, kit) as st:
        xt = st.sb("xt", [P, 2, D])
        xnT = st.sb("xnT", [P, C, BODY])
        z = st.sb("z", [P, 2, D])
        v = st.sb("v", [P, 2, D + 1])
        loaded = st.sem("loaded")
        nm = Norm(st, "f", xt, loaded, 16)
        turned, xnT_done, kv_done, z_done, e_done, sum_done, one = (st.sem(n) for n in "turned xnT_done kv_done z_done e_done sum_done one".split())
        gsp = st.sem("gsp")
        with nc.Block() as block:
            @block.sync
            def _(sp):
                def body(i, tiles):
                    wait(sp, nm.xn_done, i, gsp)
                    sp.dma_start(xt[0:tiles[0], 0:len(tiles), :], rows(d.x2, i, tiles)).then_inc(loaded, 16)
                bodies(sp, body)

            @block.vector
            def _(dve):
                dve.memset(v[:, :, D:D + 1], 1.0).then_inc(one, 1)

                def body(i, tiles):
                    nm.dve_moments(dve, i, tiles)
                    nm.dve_normalise(dve, i, tiles, [(turned, 1)])
                    wait(dve, kv_done, i + 1)
                    wait(dve, sum_done, i)
                    for j, w in enumerate(tiles):
                        dve.tensor_tensor(z[0:w, j, :], k.bank[1 + j][0:w, 0:D], k.bkv1[0:w, 0:D], ALU.add)
                        ins = dve.tensor_tensor(v[0:w, j, 0:D], k.bank[1 + j][0:w, D:2 * D], k.bkv1[0:w, D:2 * D], ALU.add)
                    ins.then_inc(z_done, 1)
                bodies(dve, body)

            @block.scalar
            def _(act):
                def body(i, tiles):
                    w, n, wt = tiles[0], len(tiles), sum(tiles)
                    nm.act_sd(act, i, tiles)
                    wait(act, turned, i + 1)
                    wait(act, kv_done, i)
                    act.activation(xnT[:, :, 0:wt], halves(k.bank[0][:])[:, :, 0:wt], ACT.Copy).then_inc(xnT_done, 1)
                    wait(act, z_done, i + 1)
                    act.activation(z[0:w, 0:n, :], z[0:w, 0:n, :], ACT.Exp).then_inc(e_done, 1)
                bodies(act, body)

            @block.tensor
            def _(pe):
                pe.wait_ge(one, 1)

                def body(i, tiles):
                    wait(pe, nm.xn_done, i + 1)
                    wait(pe, xnT_done, i)
                    pe_turn(k, pe, k.bank[0], nm.xn, tiles, turned)
                    wait(pe, xnT_done, i + 1)
                    wait(pe, z_done, i)
                    for j, w in enumerate(tiles):
                        for c in range(C):
                            ins = pe.matmul(k.bank[1 + j][0:w, :], xnT[:, c, j * P:j * P + w], k.wkv1[:, c, :], start=(c == 0), stop=(c == C - 1))
                    ins.then_inc(kv_done, 1)
                    wait(pe, e_done, i + 1)
                    first, last = isinstance(i, int) and i == 0, isinstance(i, int) and i == FULL
                    for j, w in enumerate(tiles):
                        for c in range(C):
                            ins = pe.matmul(k.bank[3 + c][:, 0:D + 1], z[0:w, j, c * P:(c + 1) * P], v[0:w, j, :], start=first and j == 0, stop=last)
                    ins.then_inc(sum_done, 1)
                bodies(pe, body)
        lam = st.sb("lam", [P, C, D])
        rs = st.sb("rsum", [P, C])
        stl = st.sb("stl", [P, C, 6])
        mv = st.sb("mvl", [P, C, 2])
        sd = st.sb("sdl", [P, C])
        sc = st.sb("scl", [P, C])
        sh = st.sb("shl", [P, C])
        qb = st.sb("qb", [P, C, P])
        s1, s2, s3 = st.sem("s1"), st.sem("s2"), st.sem("s3")
        with nc.Block() as block:
            @block.vector
            def _(dve):
                n = [0]

                def then(ins):
                    n[0] += 1
                    ins.then_inc(s1, 1)
                    dve.wait_ge(s1, n[0])
                for c in range(C):
                    then(dve.reciprocal(rs[:, c:c + 1], k.bank[3 + c][:, D:D + 1]))
                    then(dve.tensor_scalar(lam[:, c, :], k.bank[3 + c][:, 0:D], rs[:, c:c + 1], None, ALU.mult))
                    then(dve.bn_stats(stl[:, c, :], lam[:, c, :]))
                    then(dve.bn_aggr(mv[:, c, :], stl[:, c, :]))
                dve.wait_ge(s2, 1)
                then(dve.reciprocal(sd[:], sd[:]))
                then(dve.tensor_tensor(sc[:], sd[:], k.gmc[:], ALU.mult))
                then(dve.tensor_tensor(sd[:], mv[:, :, 0], sc[:], ALU.mult))
                then(dve.tensor_tensor(sh[:], k.bemc[:], sd[:], ALU.subtract))
                for c in range(C):
                    then(dve.tensor_scalar(lam[:, c, :], lam[:, c, :], sc[:, c:c + 1], sh[:, c:c + 1], ALU.mult, ALU.add))
                    then(dve.tensor_scalar(qb[:, c, :], k.ones[:], k.bq1c[:, c:c + 1], None, ALU.mult))
                dve.wait_ge(s3, 1)
                for c in range(C):
                    dve.tensor_copy(k.mq[:, c, :], k.bank[c][:, 0:D])
                then(dve.tensor_copy(k.bmq[:], k.bank[2][:, 0:D]))

            @block.scalar
            def _(act):
                act.wait_ge(s1, 8)
                act.activation(sd[:], mv[:, :, 1], ACT.Sqrt, bias=k.eps[:]).then_inc(s2, 1)

            @block.tensor
            def _(pe):
                pe.wait_ge(s1, 16)
                for o in range(C):
                    for c in range(C):
                        pe.matmul(k.bank[o][:, 0:D], k.wq1T[:, c, o * P:(o + 1) * P], lam[:, c, :], start=(c == 0), stop=(c == C - 1))
                for c in range(C):
                    ins = pe.matmul(k.bank[2][:, 0:D], qb[:, c, :], lam[:, c, :], start=(c == 0), stop=(c == C - 1))
                ins.then_inc(s3, 1)


class Convolved:

    def __init__(self, st, d, table, bias):
        self.table, self.bias, self.d, self.kit = table, bias, d, st.kit
        self.at = st.sb("cat", [P, 2, D])
        self.tt = st.sb("ctt", [P, 2, D])
        self.h = st.sb("ch", [P, 2, D])
        self.loaded, self.added, self.scaled, self.h_done = (st.sem(n) for n in ("c_loaded", "c_added", "c_scaled", "c_h_done"))

    def sp_load(self, sp, i, tiles, gate):
        w, n = tiles[0], len(tiles)
        wait(sp, self.added, i, gate)
        sp.dma_start(self.at[0:w, 0:n, :], rows(self.d.acc[:, 0:D], i, tiles)).then_inc(self.loaded, 16)
        sp.dma_start(self.tt[0:w, 0:n, :], rows(self.table, i, tiles)).then_inc(self.loaded, 16)

    def dve(self, dve, i, tiles, used):
        w, n = tiles[0], len(tiles)
        wait(dve, self.loaded, 32 * (i + 1))
        for sem, step in used:
            wait(dve, sem, i * step)
        dve.tensor_tensor(self.h[0:w, 0:n, :], self.at[0:w, 0:n, :], self.tt[0:w, 0:n, :], ALU.add).then_inc(self.added, 1)
        wait(dve, self.added, i + 1)
        for j, wj in enumerate(tiles):
            ins = dve.scalar_tensor_tensor(out=self.h[0:wj, j, :], in0=self.h[0:wj, j, :], scalar=self.kit.wdeg[0:wj, bass.ds(i * 2 + j, 1)],
                                           in1=self.bias[0:wj, :], op0=ALU.mult, op1=ALU.add)
        ins.then_inc(self.scaled, 1)

    def act(self, act, i, tiles):
        w, n = tiles[0], len(tiles)
        wait(act, self.scaled, i + 1)
        act.activation(self.h[0:w, 0:n, :], self.h[0:w, 0:n, :], ACT.Relu).then_inc(self.h_done, 1)


def stage_conv_between(nc, kit, a, d):
    k = kit
    with Stage(nc, kit) as st:
        cv = Convolved(st, d, d.t1, k.bg1)
        hT = st.sb("hT", [P, C, BODY])
        t = st.sb("t", [P, 2, D])
        turned, hT_done, t_psum, t_done, stored, gsp, gpool, gact = (st.sem(n) for n in "turned hT_done t_psum t_done stored gsp gpool gact".split())
        with nc.Block() as block:
            @block.sync
            def _(sp):
                bodies(sp, lambda i, tiles: cv.sp_load(sp, i, tiles, gsp))

            @block.gpsimd
            def _(pool):
                def body(i, tiles):
                    wait(pool, t_done, i + 1, gpool)
                    pool.dma_start(rows(d.t2, i, tiles), t[0:tiles[0], 0:len(tiles), :]).then_inc(stored, 16)
                bodies(pool, body)
                pool.wait_ge(stored, 16 * (FULL + 1))

            @block.vector
            def _(dve):
                bodies(dve, lambda i, tiles: cv.dve(dve, i, tiles, [(turned, 1)]))

            @block.scalar
            def _(act):
                def body(i, tiles):
                    cv.act(act, i, tiles)
                    wt = sum(tiles)
                    wait(act, turned, i + 1)
                    wait(act, t_psum, i)
                    act.activation(hT[:, :, 0:wt], halves(k.bank[0][:])[:, :, 0:wt], ACT.Copy).then_inc(hT_done, 1)
                    wait(act, t_psum, i + 1)
                    wait(act, stored, 16 * i, gact)
                    for j, w in enumerate(tiles):
                        ins = act.activation(t[0:w, j, :], k.bank[1 + j][0:w, 0:D], ACT.Copy, scale=k.wdeg[0:w, bass.ds(i * 2 + j, 1)])
                    ins.then_inc(t_done, 1)
                bodies(act, body)

            @block.tensor
            def _(pe):
                def body(i, tiles):
                    wait(pe, cv.h_done, i + 1)
                    wait(pe, hT_done, i)
                    pe_turn(k, pe, k.bank[0], cv.h, tiles, turned)
                    wait(pe, hT_done, i + 1)
                    wait(pe, t_done, i)
                    for j, w in enumerate(tiles):
                        for c in range(C):
                            ins = pe.matmul(k.bank[1 + j][0:w, 0:D], hT[:, c, j * P:j * P + w], k.wg2[:, c, :], start=(c == 0), stop=(c == C - 1))
                    ins.then_inc(t_psum, 1)
                bodies(pe, body)


def stage_layer_end(nc, kit, a, d):
    k = kit
    with Stage(nc, kit) as st:
        cv = Convolved(st, d, d.t2, k.bg2)
        xt = st.sb("xt", [P, 2, D])
        xnT = st.sb("xnT", [P, C, BODY])
        x3 = st.sb("x3", [P, 2, D])
        loaded = st.sem("loaded")
        nm = Norm(st, "h", xt, loaded, 16)
        turned, xnT_done, q_psum, a_done, b_done, x3_done, stored, gsp, gpool = (st.sem(n) for n in "turned xnT_done q_psum a_done b_done x3_done stored gsp gpool".split())
        with nc.Block() as block:
            @block.sync
            def _(sp):
                def body(i, tiles):
                    cv.sp_load(sp, i, tiles, gsp)
                    wait(sp, x3_done, i, gsp)
                    sp.dma_start(xt[0:tiles[0], 0:len(tiles), :], rows(d.x2, i, tiles)).then_inc(loaded, 16)
                bodies(sp, body)

            @block.gpsimd
            def _(pool):
                def body(i, tiles):
                    wait(pool, x3_done, i + 1, gpool)
                    pool.dma_start(rows(d.x3, i, tiles), x3[0:tiles[0], 0:len(tiles), :]).then_inc(stored, 16)
                bodies(pool, body)
                pool.wait_ge(stored, 16 * (FULL + 1))

            @block.vector
            def _(dve):
                def body(i, tiles):
                    w, n = tiles[0], len(tiles)
                    cv.dve(dve, i, tiles, [(x3_done, 1)])
                    nm.dve_moments(dve, i, tiles)
                    nm.dve_normalise(dve, i, tiles, [(turned, 1)])
                    wait(dve, q_psum, i + 1)
                    wait(dve, stored, 16 * i)
                    for j, wj in enumerate(tiles):
                        ins = dve.tensor_tensor(x3[0:wj, j, :], k.bank[1 + j][0:wj, 0:D], k.bmq[0:wj, :], ALU.add)
                    ins.then_inc(a_done, 1)
                    wait(dve, a_done, i + 1)
                    wait(dve, cv.h_done, i + 1)
                    dve.tensor_tensor(x3[0:w, 0:n, :], x3[0:w, 0:n, :], cv.h[0:w, 0:n, :], ALU.add).then_inc(b_done, 1)
                    wait(dve, b_done, i + 1)
                    dve.tensor_tensor(x3[0:w, 0:n, :], x3[0:w, 0:n, :], xt[0:w, 0:n, :], ALU.add).then_inc(x3_done, 1)
                bodies(dve, body)

            @block.scalar
            def _(act):
                def body(i, tiles):
                    wt = sum(tiles)
                    cv.act(act, i, tiles)
                    nm.act_sd(act, i, tiles)
                    wait(act, turned, i + 1)
                    wait(act, q_psum, i)
                    act.activation(xnT[:, :, 0:wt], halves(k.bank[0][:])[:, :, 0:wt], ACT.Copy).then_inc(xnT_done, 1)
                bodies(act, body)

            @block.tensor
            def _(pe):
                def body(i, tiles):
                    wait(pe, nm.xn_done, i + 1)
                    wait(pe, xnT_done, i)
                    pe_turn(k, pe, k.bank[0], nm.xn, tiles, turned)
                    wait(pe, xnT_done, i + 1)
                    wait(pe, a_done, i)
                    for j, w in enumerate(tiles):
                        for c in range(C):
                            ins = pe.matmul(k.bank[1 + j][0:w, 0:D], xnT[:, c, j * P:j * P + w], k.mq[:, c, :], start=(c == 0), stop=(c == C - 1))
                    ins.then_inc(q_psum, 1)
                bodies(pe, body)


def stage_slices(nc, kit, a, d):
    k = kit
    HS = HEADS * SLICES
    with Stage(nc, kit) as st:
        xt = st.sb("xt", [P, 2, D])
        xnT = st.sb("xnT", [P, C, BODY])
        lg = st.sb("lg", [P, 2, HS])
        mx = st.sb("mxs", [P, 2, HEADS])
        loaded = st.sem("loaded")
        nm = Norm(st, "s", xt, loaded, 16)
        (turned, xnT_done, lg_psum, lg_done, mx_done, sub_done, e_done, sum_done, rec_done, sw_done, acc_done, stored) = (
            st.sem(n) for n in "turned xnT_done lg_psum lg_done mx_done sub_done e_done sum_done rec_done sw_done acc_done stored".split())
        gsp, gpool = st.sem("gsp"), st.sem("gpool")

        def heads(t, j, w):
            return t[0:w, j, :].rearrange("p (h g) -> p h g", g=SLICES)

        def over(t, j, w):
            return t[0:w, j, :].rearrange("p (h a) -> p h a", a=1).to_broadcast([w, HEADS, SLICES])
        with nc.Block() as block:
            @block.sync
            def _(sp):
                def body(i, tiles):
                    wait(sp, nm.xn_done, i, gsp)
                    sp.dma_start(xt[0:tiles[0], 0:len(tiles), :], rows(d.x3, i, tiles)).then_inc(loaded, 16)
                bodies(sp, body)

            @block.gpsimd
            def _(pool):
                def body(i, tiles):
                    wait(pool, sw_done, i + 1, gpool)
                    pool.dma_start(rows(d.sw, i, tiles), lg[0:tiles[0], 0:len(tiles), :]).then_inc(stored, 16)
                bodies(pool, body)
                pool.wait_ge(stored, 16 * (FULL + 1))

            @block.vector
            def _(dve):
                def body(i, tiles):
                    nm.dve_moments(dve, i, tiles)
                    nm.dve_normalise(dve, i, tiles, [(acc_done, 1)])
                    wait(dve, lg_psum, i + 1)
                    wait(dve, stored, 16 * i)
                    for j, w in enumerate(tiles):
                        ins = dve.tensor_tensor(lg[0:w, j, :], k.bank[1 + j][0:w, :], k.bxs[0:w, :], ALU.add)
                    ins.then_inc(lg_done, 1)
                    wait(dve, lg_done, i + 1)
                    for j, w in enumerate(tiles):
                        ins = dve.tensor_reduce(mx[0:w, j, :], heads(lg, j, w), AX.X, ALU.max)
                    ins.then_inc(mx_done, 1)
                    wait(dve, mx_done, i + 1)
                    for j, w in enumerate(tiles):
                        ins = dve.tensor_tensor(heads(lg, j, w), heads(lg, j, w), over(mx, j, w), ALU.subtract)
                    ins.then_inc(sub_done, 1)
                    wait(dve, e_done, i + 1)
                    for j, w in enumerate(tiles):
                        ins = dve.tensor_reduce(mx[0:w, j, :], heads(lg, j, w), AX.X, ALU.add)
                    ins.then_inc(sum_done, 1)
                    wait(dve, sum_done, i + 1)
                    w, n = tiles[0], len(tiles)
                    dve.reciprocal(mx[0:w, 0:n, :], mx[0:w, 0:n, :]).then_inc(rec_done, 1)
                    wait(dve, rec_done, i + 1)
                    for j, w in enumerate(tiles):
                        ins = dve.tensor_tensor(heads(lg, j, w), heads(lg, j, w), over(mx, j, w), ALU.mult)
                    ins.then_inc(sw_done, 1)
                bodies(dve, body)

            @block.scalar
            def _(act):
                def body(i, tiles):
                    w, n, wt = tiles[0], len(tiles), sum(tiles)
                    nm.act_sd(act, i, tiles)
                    wait(act, turned, i + 1)
                    wait(act, lg_psum, i)
                    act.activation(xnT[:, :, 0:wt], halves(k.bank[0][:])[:, :, 0:wt], ACT.Copy).then_inc(xnT_done, 1)
                    wait(act, sub_done, i + 1)
                    act.activation(lg[0:w, 0:n, :], lg[0:w, 0:n, :], ACT.Exp).then_inc(e_done, 1)
                bodies(act, body)

            @block.tensor
            def _(pe):
                def body(i, tiles):
                    wait(pe, nm.xn_done, i + 1)
                    wait(pe, xnT_done, i)
                    pe_turn(k, pe, k.bank[0], nm.xn, tiles, turned)
                    wait(pe, xnT_done, i + 1)
                    wait(pe, lg_done, i)
                    for j, w in enumerate(tiles):
                        for c in range(C):
                            ins = pe.matmul(k.bank[1 + j][0:w, :], xnT[:, c, j * P:j * P + w], k.wxs[:, c, :], start=(c == 0), stop=(c == C - 1))
                    ins.then_inc(lg_psum, 1)
                    wait(pe, sw_done, i + 1)
                    first, last = isinstance(i, int) and i == 0, isinstance(i, int) and i == FULL
                    for j, w in enumerate(tiles):
                        for c in range(C):
                            pe.matmul(k.bank[3 + c][:, :], nm.xn[0:w, j, c * P:(c + 1) * P], lg[0:w, j, :], start=first and j == 0, stop=last)
                        ins = pe.matmul(k.bank[5][0:1, :], k.ones[0:w, 0:1], lg[0:w, j, :], start=first and j == 0, stop=last)
                    ins.then_inc(acc_done, 1)
                bodies(pe, body)
        T = st.sb("T", [P, C, HS])
        norm = st.sb("norm", [1, HS])
        rn = st.sb("rn", [SLICES, 1])
        tok, tokT, qT, kT, vv, at, atT, oT = (st.sb(n, [SLICES, SDIM]) for n in "tok tokT qT kT vv at atT oT".split())
        mo = st.sb("mo", [SLICES, D])
        sm = st.sb("sm", [SLICES, 4])
        vs, ps, as_, ds = st.sem("vs"), st.sem("ps"), st.sem("as_"), st.sem("ds")
        b = k.bank
        with nc.Block() as block:
            @block.vector
            def _(dve):
                n, p = [0], [0]

                def then(ins):
                    n[0] += 1
                    ins.then_inc(vs, 1)
                    dve.wait_ge(vs, n[0])

                def psum():
                    p[0] += 1
                    dve.wait_ge(ps, p[0])
                for c in range(C):
                    then(dve.tensor_copy(T[:, c, :], b[3 + c][:, :]))
                then(dve.tensor_copy(norm[:], b[5][0:1, :]))
                for h in range(HEADS):
                    psum()
                    then(dve.tensor_scalar(rn[:], b[1][0:SLICES, 0:1], 1e-5, None, ALU.add))
                    then(dve.reciprocal(rn[:], rn[:]))
                    then(dve.tensor_scalar(tok[:], b[0][0:SLICES, 0:SDIM], rn[:], None, ALU.mult))
                    psum()
                    then(dve.tensor_copy(tokT[:], b[0][0:SDIM, 0:SLICES]))
                    psum()
                    dve.tensor_copy(qT[:], b[0][0:SDIM, 0:SLICES])
                    dve.tensor_copy(kT[:], b[1][0:SDIM, 0:SLICES])
                    then(dve.tensor_copy(vv[:], b[2][0:SLICES, 0:SDIM]))
                    psum()
                    then(dve.tensor_reduce(sm[:, 0:1], b[0][0:SLICES, 0:SLICES], AX.X, ALU.max))
                    then(dve.tensor_scalar(sm[:, 1:2], sm[:, 0:1], -SDIM ** -0.5, None, ALU.mult))
                    dve.wait_ge(as_, h + 1)
                    then(dve.reciprocal(sm[:, 3:4], sm[:, 2:3]))
                    then(dve.tensor_scalar(at[:], at[:], sm[:, 3:4], None, ALU.mult))
                    psum()
                    then(dve.tensor_copy(atT[:], b[1][0:SLICES, 0:SLICES]))
                    psum()
                    then(dve.tensor_copy(oT[:], b[2][0:SDIM, 0:SLICES]))
                    psum()
                    if h:
                        dve.wait_ge(ds, 16 * h)
                    then(dve.tensor_copy(mo[:], b[0][0:SLICES, 0:D]))

            @block.scalar
            def _(act):
                for h in range(HEADS):
                    act.wait_ge(vs, 3 + 12 * h + 7)
                    act.activation(at[:], b[0][0:SLICES, 0:SLICES], ACT.Exp, bias=sm[:, 1:2], scale=SDIM ** -0.5,
                                   accum_out=sm[:, 2:3]).then_inc(as_, 1)

            @block.sync
            def _(sp):
                for h in range(HEADS):
                    sp.wait_ge(vs, 3 + 12 * (h + 1))
                    sp.dma_start(k.mout[(h % 2) * SLICES:(h % 2 + 1) * SLICES, h // 2, :], mo[:]).then_inc(ds, 16)
                sp.wait_ge(ds, 16 * HEADS)

            @block.tensor
            def _(pe):
                for h in range(HEADS):
                    hs = slice(h * SLICES, (h + 1) * SLICES)
                    o = 3 + 12 * h
                    pe.wait_ge(vs, o)
                    for c in range(C):
                        pe.matmul(b[0][0:SLICES, 0:SDIM], T[:, c, hs], k.wfx[:, c, hs], start=(c == 0), stop=False)
                    pe.matmul(b[0][0:SLICES, 0:SDIM], norm[:, hs], k.bfx[:, hs], start=False, stop=True)
                    pe.matmul(b[1][0:SLICES, 0:1], norm[:, hs], k.ones[0:1, 0:1], start=True, stop=True).then_inc(ps, 1)
                    pe.wait_ge(vs, o + 3)
                    pe.transpose(b[0][0:SDIM, 0:SLICES], tok[:], k.ident[0:SLICES, 0:SLICES]).then_inc(ps, 1)
                    pe.wait_ge(vs, o + 4)
                    pe.matmul(b[0][0:SDIM, 0:SLICES], k.wsq[:], tokT[:], start=True, stop=True)
                    pe.matmul(b[1][0:SDIM, 0:SLICES], k.wsk[:], tokT[:], start=True, stop=True)
                    pe.matmul(b[2][0:SLICES, 0:SDIM], tokT[:], k.wsv[:], start=True, stop=True).then_inc(ps, 1)
                    pe.wait_ge(vs, o + 5)
                    pe.matmul(b[0][0:SLICES, 0:SLICES], qT[:], kT[:], start=True, stop=True).then_inc(ps, 1)
                    pe.wait_ge(vs, o + 9)
                    pe.transpose(b[1][0:SLICES, 0:SLICES], at[:], k.ident[0:SLICES, 0:SLICES]).then_inc(ps, 1)
                    pe.wait_ge(vs, o + 10)
                    pe.matmul(b[2][0:SDIM, 0:SLICES], vv[:], atT[:], start=True, stop=True).then_inc(ps, 1)
                    pe.wait_ge(vs, o + 11)
                    pe.matmul(b[0][0:SLICES, 0:D], oT[:], k.wout[:, h, :], start=True, stop=True).then_inc(ps, 1)


def stage_out(nc, kit, a, d, out):
    k = kit
    HS = HEADS * SLICES
    NC4 = HS // P
    with Stage(nc, kit) as st:
        sw = st.sb("sw", [P, 2, HS])
        xt = st.sb("xt", [P, 2, D])
        swT = st.sb("swT", [P, 2, NC4, P])
        y = st.sb("y", [P, 2, D])
        loaded, turned, swT_done, y_psum, a_done, y_done, stored, gsp, gpool = (st.sem(n) for n in "loaded turned swT_done y_psum a_done y_done stored gsp gpool".split())
        with nc.Block() as block:
            @block.sync
            def _(sp):
                def body(i, tiles):
                    w, n = tiles[0], len(tiles)
                    wait(sp, y_done, i, gsp)
                    sp.dma_start(sw[0:w, 0:n, :], rows(d.sw, i, tiles)).then_inc(loaded, 16)
                    sp.dma_start(xt[0:w, 0:n, :], rows(d.x3, i, tiles)).then_inc(loaded, 16)
                bodies(sp, body)

            @block.gpsimd
            def _(pool):
                def body(i, tiles):
                    wait(pool, y_done, i + 1, gpool)
                    pool.dma_start(rows(out, i, tiles), y[0:tiles[0], 0:len(tiles), :]).then_inc(stored, 16)
                bodies(pool, body)
                pool.wait_ge(stored, 16 * (FULL + 1))

            @block.scalar
            def _(act):
                def body(i, tiles):
                    wait(act, turned, i + 1)
                    wait(act, y_psum, i)
                    for j, w in enumerate(tiles):
                        ins = act.activation(swT[:, j, :, 0:w], k.bank[j][:].rearrange("p (c n) -> p c n", c=NC4)[:, :, 0:w], ACT.Copy)
                    ins.then_inc(swT_done, 1)
                bodies(act, body)

            @block.vector
            def _(dve):
                def body(i, tiles):
                    w, n = tiles[0], len(tiles)
                    wait(dve, y_psum, i + 1)
                    wait(dve, stored, 16 * i)
                    for j, wj in enumerate(tiles):
                        ins = dve.tensor_tensor(y[0:wj, j, :], k.bank[2 + j][0:wj, 0:D], k.bout[0:wj, :], ALU.add)
                    ins.then_inc(a_done, 1)
                    wait(dve, a_done, i + 1)
                    dve.tensor_tensor(y[0:w, 0:n, :], y[0:w, 0:n, :], xt[0:w, 0:n, :], ALU.add).then_inc(y_done, 1)
                bodies(dve, body)

            @block.tensor
            def _(pe):
                def body(i, tiles):
                    wait(pe, loaded, 32 * (i + 1))
                    wait(pe, swT_done, i)
                    for j, w in enumerate(tiles):
                        for c in range(NC4):
                            ins = pe.transpose(k.bank[j][:, c * P:c * P + w], sw[0:w, j, c * P:(c + 1) * P], k.ident[0:w, 0:w])
                    ins.then_inc(turned, 1)
                    wait(pe, swT_done, i + 1)
                    wait(pe, a_done, i)
                    for j, w in enumerate(tiles):
                        for c in range(NC4):
                            ins = pe.matmul(k.bank[2 + j][0:w, 0:D], swT[:, j, c, 0:w], k.mout[:, c, :], start=(c == 0), stop=(c == NC4 - 1))
                    ins.then_inc(y_psum, 1)
                bodies(pe, body)


def build(nc, a, out):
    HS = HEADS * SLICES
    with ExitStack() as ctx:
        k, d = Kit(), Kit()
        k.ctx, k.stages = ctx, 0

        def sb(name, shape, dt=F32):
            return ctx.enter_context(nc.sbuf_tensor(name, shape, dt))

        def dram(name, shape, dt=F32):
            return nc.dram_tensor("d_" + name, shape, dt).ap()
        k.bank = [ctx.enter_context(nc.psum_tensor(f"bank{b}", [P, 512], F32)) for b in range(8)]
        d.xn = dram("xn", [N, D])
        d.x1 = dram("x1", [N, D])
        d.t1 = dram("t1", [N, D])
        d.t2 = dram("t2", [N, D])
        d.x2 = dram("x2", [N, D])
        d.x3 = dram("x3", [N, D])
        d.dst = dram("dst", [NG * GE], I32)
        d.sw = dram("sw", [N, HS], F32)
        d.acc = dram("acc", [NTILE * P, AW], F32)
        k.ident = sb("ident", [P, P])
        k.tri = sb("tri", [P, P])
        k.hmask = sb("hmask", [P, P])
        k.ones = sb("ones", [P, P])
        k.far = sb("far", [EXPERTS, EXPERTS * HID])
        k.iota_i = sb("iota_i", [P, P], I32)
        k.iota = sb("iota", [P, P])
        k.eps = sb("eps", [P, 1])
        k.zeros = sb("zeros", [P, 7 * AW])
        k.wq0 = sb("wq0", [P, C, D])
        k.wo0 = sb("wo0", [P, C, D])
        k.wg1 = sb("wg1", [P, C, D])
        k.wg2 = sb("wg2", [P, C, D])
        k.w1T = sb("w1T", [P, C, D])
        k.w2T = sb("w2T", [P, C, D])
        k.wq1T = sb("wq1T", [P, C, D])
        k.m0 = sb("m0", [P, C, D])
        k.mq = sb("mq", [P, C, D])
        k.wkv0 = sb("wkv0", [P, C, 2 * D])
        k.wkv1 = sb("wkv1", [P, C, 2 * D])
        k.wfx = sb("wfx", [P, C, 2 * D])
        k.wxs = sb("wxs", [P, C, 2 * D])
        k.rT = sb("rT", [P, C, EXPERTS])
        k.rb = sb("rb", [P, EXPERTS])
        k.wout = sb("wout", [SDIM, HEADS, D])
        k.wslice = sb("wslice", [SDIM, SDIM])
        k.wsq = sb("wsq", [SDIM, SDIM])
        k.wsk = sb("wsk", [SDIM, SDIM])
        k.wsv = sb("wsv", [SDIM, SDIM])
        k.bkv0 = sb("bkv0", [P, 2 * D])
        k.bkv1 = sb("bkv1", [P, 2 * D])
        k.bxs = sb("bxs", [P, 2 * D])
        k.bk1row = sb("bk1row", [P, D])
        k.bg1 = sb("bg1", [P, D])
        k.bg2 = sb("bg2", [P, D])
        k.bout = sb("bout", [P, D])
        k.bmq = sb("bmq", [P, D])
        k.bfx = sb("bfx", [1, HS])
        k.bslice_row = sb("bslice_row", [P, SLICES])
        k.temp = sb("temp", [P, HEADS])
        k.rtemp = sb("rtemp", [P, HEADS])
        k.epsw = sb("epsw", [P, 1])
        k.g1c = sb("g1c", [P, C])
        k.be1c = sb("be1c", [P, C])
        k.ghc = sb("ghc", [P, C])
        k.behc = sb("behc", [P, C])
        k.bqc = sb("bqc", [P, C])
        k.boc = sb("boc", [P, C])
        k.gmc = sb("gmc", [P, C])
        k.bemc = sb("bemc", [P, C])
        k.bq1c = sb("bq1c", [P, C])
        k.bk1c = sb("bk1c", [P, C])
        k.s1 = sb("s1", [P, C])
        k.t1 = sb("t1", [P, C])
        k.s2 = sb("s2", [P, C])
        k.t2 = sb("t2", [P, C])
        k.ks = sb("ks", [P, C, P])
        k.mout = sb("mout", [P, HS // P, D])
        k.wdeg = sb("wdeg", [P, NTILE + 1])
        k.flag = sb("flag", [1, 1], I32)
        k.dst_f = sb("dst_f", [P, NET])
        k.rank_f = sb("rank_f", [P, NET])
        k.ew_f = sb("ew_f", [P, NET])
        k.fd_f = sb("fd_f", [P, NET])
        k.src_i = sb("src_i", [P, NET], I32)
        k.dst_i = sb("dst_i", [P, NET], I32)
        k.ext = sb("ext", [P, NET, 3])
        stage_setup(nc, k, a, d)
        stage_front(nc, k, a, d)
        stage_aggregate(nc, k, a, d, d.xn)
        with ExitStack() as middle:
            k.zT = middle.enter_context(nc.sbuf_tensor("zT", [P, C, N], F32))
            k.nbc = middle.enter_context(nc.sbuf_tensor("nbc", [P, N], F32))
            stage_gnn_first(nc, k, a, d)
            stage_gnn_second(nc, k, a, d)
            stage_gnn_mix(nc, k, a, d)
        stage_experts(nc, k, a, d)
        stage_second_front(nc, k, a, d)
        stage_lambda(nc, k, a, d)
        stage_aggregate(nc, k, a, d, d.t1)
        stage_conv_between(nc, k, a, d)
        stage_aggregate(nc, k, a, d, d.t2)
        stage_layer_end(nc, k, a, d)
        stage_slices(nc, k, a, d)
        stage_out(nc, k, a, d, out)


def kernel(**inputs):
    import numpy as np
    import concourse.bacc as bacc
    from concourse.bass_utils import run_bass_kernel_spmd

    nc = bacc.Bacc("TRN2", target_bir_lowering=False, num_devices=1)
    arrays, args = {}, {}
    for name, x in inputs.items():
        x = np.ascontiguousarray(x)
        arrays[f"in_{name}"] = x
        args[name] = nc.dram_tensor(f"in_{name}", x.shape, mybir.dt.from_np(x.dtype), kind="ExternalInput").ap()
    out = nc.dram_tensor("out_0", (N, D), F32, kind="ExternalOutput").ap()
    build(nc, args, out)
    return run_bass_kernel_spmd(nc, [arrays], core_ids=[0]).results[0]["out_0"]
```

```python
from contextlib import ExitStack

import concourse.bass as bass
from concourse import mybir

F32 = mybir.dt.float32
I32 = mybir.dt.int32
ALU = mybir.AluOpType
ACT = mybir.ActivationFunctionType
AX = mybir.AxisListType

N, E, D = 6250, 100000, 256
P = 128
C = D // P
BODY = 2 * P
FULL = N // BODY
LAST = N - FULL * BODY
NTILE = 2 * FULL + 1
GT = 8
GE = GT * P
NG = -(-E // GE)
NET = NG * GT
AW = D + 3
FAR = 65536.0
HEADS, EXPERTS, HID = 8, 32, 64
SLICES, SDIM = 64, 64
SORTED = (N + EXPERTS * (P - 1)) // P
LN_EPS = 1e-5
POOL_DMA = ("stored", "xstored", "scattered")


def wait(eng, sem, value, gate=None):
    if isinstance(value, int):
        if value > 0:
            eng.wait_ge(sem, value)
        return
    eng.wait_ge(sem, value)
    if gate is not None:
        eng.sem_inc(gate, 1)


def bodies(eng, body):
    body(0, (P, P))
    with eng.Fori(1, FULL) as i:
        body(i, (P, P))
    body(FULL, (LAST,))


def rows(ap, i, tiles, width=None):
    if len(tiles) == 2:
        return ap[bass.ds(i * BODY, BODY), :].rearrange("(j p) d -> p j d", p=P)
    return ap[FULL * BODY:N, :].rearrange("(j p) d -> p j d", j=1)


def bcast_rows(ap, n):
    return bass.AP(tensor=ap.tensor, offset=ap.offset, ap=[[0, P], [1, n]])


class Kit:
    pass


class Stage:

    def __init__(self, nc, kit):
        self.nc, self.kit, self.ctx, self.sems = nc, kit, ExitStack(), []
        kit.stages += 1
        self.tag = f"_{kit.stages}"

    def __enter__(self):
        return self

    def __exit__(self, *exc):
        if exc[0] is None and self.sems:
            with self.nc.Block() as block:
                @block.gpsimd
                def _(pool):
                    for s in self.sems:
                        pool.sem_clear(s)
        self.ctx.close()

    def sem(self, name):
        if name in POOL_DMA:
            return self.pool_dma(name)
        s = self.ctx.enter_context(self.nc.semaphore(name + self.tag))
        self.sems.append(s)
        return s

    def pool_dma(self, name):
        return self.kit.ctx.enter_context(self.nc.semaphore(name + self.tag))

    def sb(self, name, shape, dt=F32):
        return self.ctx.enter_context(self.nc.sbuf_tensor(name + self.tag, shape, dt))


class Norm:

    def __init__(self, st, tag, src, src_ready, src_step=1):
        self.src, self.src_ready, self.src_step = src, src_ready, src_step
        self.stat = st.sb(f"stat{tag}", [P, 2, 6])
        self.mv = st.sb(f"mv{tag}", [P, 2, 2])
        self.sd = st.sb(f"sd{tag}", [P, 2])
        self.rs = st.sb(f"rs{tag}", [P, 2])
        self.xn = st.sb(f"xn{tag}", [P, 2, D])
        self.stats_done = st.sem(f"stats_done{tag}")
        self.moments_done = st.sem(f"moments_done{tag}")
        self.sd_done = st.sem(f"sd_done{tag}")
        self.rs_done = st.sem(f"rs_done{tag}")
        self.xn_done = st.sem(f"xn_done{tag}")
        self.gate = st.sem(f"gate{tag}")
        self.kit = st.kit

    def dve_moments(self, eng, i, tiles):
        wait(eng, self.src_ready, (i + 1) * self.src_step)
        for j, w in enumerate(tiles):
            ins = eng.bn_stats(self.stat[0:w, j, :], self.src[0:w, j, :])
        ins.then_inc(self.stats_done, 1)
        wait(eng, self.stats_done, i + 1)
        wait(eng, self.sd_done, i)
        wait(eng, self.xn_done, i, self.gate)
        for j, w in enumerate(tiles):
            ins = eng.bn_aggr(self.mv[0:w, j, :], self.stat[0:w, j, :])
        ins.then_inc(self.moments_done, 1)

    def act_sd(self, eng, i, tiles):
        w, n = tiles[0], len(tiles)
        wait(eng, self.moments_done, i + 1)
        wait(eng, self.rs_done, i)
        eng.activation(self.sd[0:w, 0:n], self.mv[0:w, 0:n, 1], ACT.Sqrt,
                       bias=self.kit.eps[0:w, :]).then_inc(self.sd_done, 1)

    def dve_normalise(self, eng, i, tiles, used=()):
        w, n = tiles[0], len(tiles)
        wait(eng, self.sd_done, i + 1)
        wait(eng, self.xn_done, i)
        eng.reciprocal(self.rs[0:w, 0:n], self.sd[0:w, 0:n]).then_inc(self.rs_done, 1)
        wait(eng, self.rs_done, i + 1)
        for sem, step in used:
            wait(eng, sem, i * step)
        for j, w in enumerate(tiles):
            ins = eng.tensor_scalar(self.xn[0:w, j, :], self.src[0:w, j, :], self.mv[0:w, j, 0:1],
                                    self.rs[0:w, j:j + 1], ALU.subtract, ALU.mult)
        ins.then_inc(self.xn_done, 1)


def pe_turn(kit, eng, bank, src, tiles, done):
    for j, w in enumerate(tiles):
        for c in range(C):
            ins = eng.transpose(bank[:, c * BODY + j * P:c * BODY + j * P + w],
                                src[0:w, j, c * P:(c + 1) * P], kit.ident[0:w, 0:w])
    ins.then_inc(done, 1)


def halves(ap):
    return ap.rearrange("p (c n) -> p c n", c=C)


def project(eng, out, wT, x, w, m=None, n=D):
    for c in range(C):
        ins = eng.matmul(out, x(c), w(c), start=(c == 0), stop=(c == C - 1))
    return ins


def stage_setup(nc, kit, a, d):
    k = kit
    with Stage(nc, kit) as st:
        raw = {n: st.sb("raw_" + n, [P, C, D]) for n in ("L0_gnn_w1", "L0_gnn_w2", "L1_q")}
        wx = st.sb("wx", [P, C, 2 * D])
        bxb = st.sb("bxb", [SDIM, HEADS, P])
        wxT = st.sb("wxT", [SDIM, HEADS, D])
        bxc = st.sb("bxc", [SDIM, HEADS])
        src_f = st.sb("src_f", [P, NET])
        rraw = st.sb("rraw", [EXPERTS, D])
        epad_i = st.sb("epad_i", [P, 2, GE], I32)
        esrc = st.sb("esrc", [P, GE])
        edst = st.sb("edst", [P, GE])
        eew = st.sb("eew", [P, GE])
        chg = st.sb("chg", [P, GE])
        zed = st.sb("zed", [P, GE])
        rank = st.sb("rank", [P, GE])
        fd = st.sb("fd", [P, GE])
        tmp = st.sb("tmp", [P, GE])
        okc = st.sb("okc", [P, 4])
        mset, cst, idn = st.sem("mset"), st.sem("cst"), st.sem("idn")
        wld, eld = st.sem("wld"), st.sem("eld")
        step = st.sem("step")
        tdone, cdone = st.sem("tdone"), st.sem("cdone")
        nload = [0]

        with nc.Block() as block:
            @block.sync
            def _(sp):
                def load(dst, src):
                    sp.dma_start(dst, src, allow_slow_non_contiguous=True).then_inc(wld, 16)
                    nload[0] += 1
                full, rest = E // GE, E % GE
                sp.wait_ge(mset, 1)
                for n, name in enumerate(("src", "dst")):
                    sp.dma_start(epad_i[0:full, n, :], a[name][0:full * GE].rearrange("(g e) -> g e", e=GE)).then_inc(eld, 16)
                    sp.dma_start(epad_i[full:full + 1, n, 0:rest], a[name][full * GE:E].rearrange("(g e) -> g e", g=1)).then_inc(eld, 16)
                sp.dma_start(eew[0:full, :], a["edge_weight"][0:full * GE].rearrange("(g e) -> g e", e=GE)).then_inc(eld, 16)
                sp.dma_start(eew[full:full + 1, 0:rest], a["edge_weight"][full * GE:E].rearrange("(g e) -> g e", g=1)).then_inc(eld, 16)
                sp.wait_ge(eld, 96)
                sq = lambda ap: ap.rearrange("(c p) n -> p c n", p=P)
                load(raw["L0_gnn_w1"][:], sq(a["L0_gnn_w1"]))
                load(raw["L0_gnn_w2"][:], sq(a["L0_gnn_w2"]))
                load(raw["L1_q"][:], sq(a["L1_mix_W_qk"][0]))
                load(rraw[:], a["L0_ffn_router_w"])
                load(k.wq0[:], sq(a["L0_mix_wq"]))
                load(k.wkv0[:, :, 0:D], sq(a["L0_mix_wk"]))
                load(k.wkv0[:, :, D:2 * D], sq(a["L0_mix_wv"]))
                load(k.wo0[:], sq(a["L0_mix_wo"]))
                for j in range(2):
                    load(k.rb2[:, j, :], bcast_rows(a["L0_ffn_router_b"], EXPERTS))
                load(k.wg1[:], sq(a["L1_gnn_W1"]))
                load(k.wg2[:], sq(a["L1_gnn_W2"]))
                load(k.wkv1[:, :, 0:D], sq(a["L1_mix_W_qk"][1]))
                load(k.wkv1[:, :, D:2 * D], sq(a["L1_mix_W_v"]))
                load(k.wfx[:], sq(a["L1_ffn_W_fx"]))
                load(wx[:], sq(a["L1_ffn_W_x"]))
                load(k.wout[:], a["L1_ffn_W_out"].rearrange("(h c) n -> c h n", c=SDIM))
                for dst, name in ((k.wslice, "L1_ffn_W_slice"), (k.wsq, "L1_ffn_W_q"), (k.wsk, "L1_ffn_W_k"), (k.wsv, "L1_ffn_W_v")):
                    load(dst[:], a[name])
                load(k.bkv0[:, 0:D], bcast_rows(a["L0_mix_bk"], D))
                load(k.bkv0[:, D:2 * D], bcast_rows(a["L0_mix_bv"], D))
                load(k.bk1row[:], bcast_rows(a["L1_mix_b_qk"][1], D))
                load(k.bkv1[:, D:2 * D], bcast_rows(a["L1_mix_b_v"], D))
                load(k.bg1[:], bcast_rows(a["L1_gnn_b1"], D))
                load(k.bg2[:], bcast_rows(a["L1_gnn_b2"], D))
                load(k.bout[:], bcast_rows(a["L1_ffn_b_out"], D))
                load(k.bfx[:], a["L1_ffn_b_fx"].rearrange("(a n) -> a n", a=1))
                load(k.bslice_row[:], bcast_rows(a["L1_ffn_b_slice"], SLICES))
                load(k.temp[:], bcast_rows(a["L1_ffn_temperature"].rearrange("a h b c -> (a h b c)"), HEADS))
                load(k.epsw[:], bcast_rows(a["L0_gnn_eps_weight"], 1))
                cols = ((k.g1c, "L0_gnn_gamma1"), (k.be1c, "L0_gnn_beta1"), (k.ghc, "L0_gnn_gamma_h"), (k.behc, "L0_gnn_beta_h"),
                        (k.bqc, "L0_mix_bq"), (k.boc, "L0_mix_bo"), (k.gmc, "L1_mix_gamma"), (k.bemc, "L1_mix_beta"))
                for dst, name in cols:
                    load(dst[:], a[name].rearrange("(c p) -> p c", p=P))
                load(k.bq1c[:], a["L1_mix_b_qk"][0].rearrange("(c p) -> p c", p=P))
                load(k.bk1c[:], a["L1_mix_b_qk"][1].rearrange("(c p) -> p c", p=P))
                load(bxc[:], a["L1_ffn_b_x"].rearrange("(h c) -> c h", c=SDIM))
                sp.dma_start(d.dst.rearrange("(g e) -> g e", e=GE), epad_i[0:NG, 1, :]).then_inc(eld, 16)
                sp.wait_ge(eld, 112)
                sp.wait_ge(wld, 16 * nload[0])

            @block.gpsimd
            def _(pool):
                pool.memset(epad_i[:, 0, :], 0).then_inc(cst, 1)
                pool.memset(epad_i[:, 1, :], N).then_inc(cst, 1)
                pool.memset(eew[:], 0.0).then_inc(cst, 1)
                pool.wait_ge(cst, 3)
                pool.sem_inc(mset, 1)
                pool.memset(k.ident[:], 0.0).then_inc(idn, 1)
                pool.wait_ge(idn, 1)
                pool.memset(k.tri[:], 1.0).then_inc(idn, 1)
                pool.wait_ge(idn, 2)
                pool.memset(k.hmask[:], 0.0).then_inc(idn, 1)
                pool.wait_ge(idn, 3)
                pool.memset(k.upper[:], 1.0).then_inc(idn, 1)
                pool.wait_ge(idn, 4)
                pool.affine_select(out=k.ident[:], in_=k.ident[:], compare_op=ALU.not_equal, fill=1.0, base=0,
                                   pattern=[[-1, P]], channel_multiplier=1).then_inc(idn, 1)
                pool.wait_ge(idn, 5)
                pool.affine_select(out=k.tri[:], in_=k.tri[:], compare_op=ALU.is_gt, fill=0.0, base=0,
                                   pattern=[[-1, P]], channel_multiplier=1).then_inc(idn, 1)
                pool.wait_ge(idn, 6)
                for h in range(4):
                    pool.memset(k.hmask[32 * h:32 * h + 32, 32 * h:32 * h + 32], 1.0).then_inc(idn, 1)
                    pool.wait_ge(idn, 7 + h)
                pool.affine_select(out=k.upper[:], in_=k.upper[:], compare_op=ALU.is_gt, fill=0.0, base=0,
                                   pattern=[[1, P]], channel_multiplier=-1).then_inc(idn, 1)
                pool.wait_ge(idn, 11)
                pool.iota(k.iota_i[:], [[1, P]], base=0, channel_multiplier=0).then_inc(idn, 1)
                pool.wait_ge(idn, 12)
                pool.memset(k.ones[:], 1.0).then_inc(idn, 1)
                pool.wait_ge(idn, 13)
                pool.memset(k.zeros[:], 0.0).then_inc(idn, 1)
                pool.wait_ge(idn, 14)
                pool.memset(k.eps[:], LN_EPS).then_inc(idn, 1)
                pool.wait_ge(idn, 15)
                pool.memset(zed[:], 0.0).then_inc(idn, 1)
                pool.wait_ge(idn, 16)

            @block.vector
            def _(dve):
                n = [0]

                def then(ins):
                    n[0] += 1
                    ins.then_inc(step, 1)
                    dve.wait_ge(step, n[0])
                dve.wait_ge(idn, 16)
                then(dve.tensor_copy(k.iota[:], k.iota_i[:]))
                dve.wait_ge(eld, 96)
                then(dve.tensor_copy(esrc[0:NG, :], epad_i[0:NG, 0, :]))
                then(dve.tensor_copy(edst[0:NG, :], epad_i[0:NG, 1, :]))
                then(dve.memset(chg[:], 0.0))
                then(dve.tensor_tensor(chg[0:NG, 1:GE], edst[0:NG, 1:GE], edst[0:NG, 0:GE - 1], ALU.not_equal))
                then(dve.tensor_tensor_scan(rank[0:NG, :], chg[0:NG, :], zed[0:NG, :], 0.0, ALU.add, ALU.add))
                then(dve.memset(tmp[:], 0.0))
                then(dve.tensor_tensor(tmp[0:NG, 1:GE], edst[0:NG, 1:GE], edst[0:NG, 0:GE - 1], ALU.subtract))
                then(dve.tensor_reduce(okc[0:NG, 0:1], tmp[0:NG, :], AX.X, ALU.min))
                then(dve.tensor_scalar(okc[0:NG, 1:2], okc[0:NG, 0:1], 0.0, None, ALU.is_ge))
                then(dve.tensor_scalar(okc[0:NG, 2:3], rank[0:NG, GE - 1:GE], float(P - 1), None, ALU.is_le))
                then(dve.tensor_tensor(okc[0:NG, 3:4], okc[0:NG, 1:2], okc[0:NG, 2:3], ALU.mult))
                then(dve.memset(chg[:, 0:1], 1.0))
                then(dve.scalar_tensor_tensor(out=fd[0:NG, :], in0=edst[0:NG, :], scalar=-FAR, in1=chg[0:NG, :], op0=ALU.add, op1=ALU.mult))
                then(dve.memset(k.ext[:], 1.0))
                dst = ((src_f, esrc), (k.dst_f, edst), (k.rank_f, rank), (k.ew_f, eew), (k.fd_f, fd))
                kk = 0
                for out, _ in dst:
                    for u in range(GT):
                        dve.wait_ge(tdone, kk + 1)
                        dve.tensor_copy(out[:].rearrange("p (g u) -> p g u", u=GT)[:, :, u], k.bank[kk % 2][:, 0:NG]).then_inc(cdone, 1)
                        kk += 1
                dve.wait_ge(cdone, kk)
                then(dve.tensor_copy(k.src_i[:], src_f[:]))
                then(dve.tensor_copy(k.dst_i[:], k.dst_f[:]))
                then(dve.tensor_copy(k.ext[:, :, 0], k.ew_f[:]))
                then(dve.tensor_copy(k.ext[:, :, 2], k.fd_f[:]))
                dve.wait_ge(tdone, kk + 1)
                dve.tensor_scalar(k.flag[0:1, :], k.bank[kk % 2][0:1, 0:1], float(NG), None, ALU.is_equal).then_inc(cdone, 1)
                kk += 1
                for out in (k.w1T, k.w2T, k.wq1T):
                    for c in range(C):
                        dve.wait_ge(tdone, kk + 1)
                        dve.tensor_copy(out[:, c, :], k.bank[kk % 2][:, 0:D]).then_inc(cdone, 1)
                        kk += 1
                for c in range(C):
                    dve.wait_ge(tdone, kk + 1)
                    dve.tensor_copy(k.rT[:, c, :], k.bank[kk % 2][:, 0:EXPERTS]).then_inc(cdone, 1)
                    kk += 1
                dve.wait_ge(wld, 16 * nload[0])
                then(dve.memset(k.wdeg[:], 1.0))
                then(dve.tensor_scalar(k.temp[:], k.temp[:], 0.1, 5.0, ALU.max, ALU.min))
                then(dve.reciprocal(k.rtemp[:], k.temp[:]))
                for h in range(HEADS):
                    dve.wait_ge(tdone, kk + 1)
                    dve.tensor_copy(wxT[:, h, :], k.bank[kk % 2][0:SDIM, 0:D]).then_inc(cdone, 1)
                    kk += 1
                    for c in range(C):
                        dve.wait_ge(tdone, kk + 1)
                        dve.tensor_scalar(k.wxs[:, c, h * SLICES:(h + 1) * SLICES], k.bank[kk % 2][:, 0:SLICES],
                                          k.rtemp[:, h:h + 1], None, ALU.mult).then_inc(cdone, 1)
                        kk += 1
                    dve.wait_ge(tdone, kk + 1)
                    then(dve.tensor_tensor(k.bxs[:, h * SLICES:(h + 1) * SLICES], k.bank[kk % 2][:, 0:SLICES], k.bslice_row[:], ALU.add))
                    dve.tensor_scalar(k.bxs[:, h * SLICES:(h + 1) * SLICES], k.bxs[:, h * SLICES:(h + 1) * SLICES],
                                      k.rtemp[:, h:h + 1], None, ALU.mult).then_inc(cdone, 1)
                    kk += 1

            @block.scalar
            def _(act):
                act.wait_ge(wld, 16 * nload[0])
                act.wait_ge(idn, 16)
                for h in range(HEADS):
                    act.activation(bxb[:, h, :], k.ones[0:SDIM, :], ACT.Copy, scale=bxc[:, h:h + 1]).then_inc(cst, 1)

            @block.tensor
            def _(pe):
                pe.wait_ge(idn, 16)
                kk = 0

                def go():
                    nonlocal kk
                    if kk >= 2:
                        pe.wait_ge(cdone, kk - 1)
                    kk += 1
                    return k.bank[(kk - 1) % 2]
                pe.wait_ge(step, 14)
                for x in (esrc, edst, rank, eew, fd):
                    for u in range(GT):
                        b = go()
                        pe.transpose(b[:, 0:NG], x[0:NG, u * P:(u + 1) * P], k.ident[0:NG, 0:NG]).then_inc(tdone, 1)
                b = go()
                pe.matmul(b[0:1, 0:1], okc[0:NG, 3:4], k.ones[0:NG, 0:1], start=True, stop=True).then_inc(tdone, 1)
                pe.wait_ge(wld, 16 * nload[0])
                for x in (raw["L0_gnn_w1"], raw["L0_gnn_w2"], raw["L1_q"]):
                    for c in range(C):
                        b = go()
                        for o in range(C):
                            ins = pe.transpose(b[:, o * P:(o + 1) * P], x[:, o, c * P:(c + 1) * P], k.ident[:])
                        ins.then_inc(tdone, 1)
                for c in range(C):
                    b = go()
                    pe.transpose(b[:, 0:EXPERTS], rraw[:, c * P:(c + 1) * P], k.ident[0:EXPERTS, 0:EXPERTS]).then_inc(tdone, 1)
                for h in range(HEADS):
                    b = go()
                    for c in range(C):
                        ins = pe.transpose(b[0:SDIM, c * P:(c + 1) * P], wx[:, c, h * SDIM:(h + 1) * SDIM], k.ident[:])
                    ins.then_inc(tdone, 1)
                    for c in range(C):
                        b = go()
                        if c == 0:
                            pe.wait_ge(cdone, kk - 1)
                        pe.matmul(b[:, 0:SLICES], wxT[:, h, c * P:(c + 1) * P], k.wslice[:], start=True, stop=True).then_inc(tdone, 1)
                    b = go()
                    if h == 0:
                        pe.wait_ge(cst, 3 + HEADS)
                    pe.matmul(b[:, 0:SLICES], bxb[:, h, :], k.wslice[:], start=True, stop=True).then_inc(tdone, 1)


def stage_front(nc, kit, a, d):
    k = kit
    with Stage(nc, kit) as st:
        xt = st.sb("xt", [P, 2, D])
        xnT = st.sb("xnT", [P, C, BODY])
        z = st.sb("z", [P, 2, D])
        mn = st.sb("mn", [P, 2, D])
        kf = st.sb("kf", [P, 2, D])
        v = st.sb("v", [P, 2, D])
        loaded, stored = st.sem("loaded"), st.sem("stored")
        nm = Norm(st, "a", xt, loaded, 16)
        turned, xnT_done = st.sem("turned"), st.sem("xnT_done")
        kv_done, z_done, mn_done, e_done, kf_done, sum_done = (st.sem(s) for s in ("kv_done", "z_done", "mn_done", "e_done", "kf_done", "sum_done"))
        gsp, gpool = st.sem("gsp"), st.sem("gpool")
        with nc.Block() as block:
            @block.sync
            def _(sp):
                def body(i, tiles):
                    wait(sp, nm.xn_done, i, gsp)
                    sp.dma_start(xt[0:tiles[0], 0:len(tiles), :], rows(a["x"], i, tiles)).then_inc(loaded, 16)
                bodies(sp, body)

            @block.gpsimd
            def _(pool):
                def body(i, tiles):
                    wait(pool, nm.xn_done, i + 1, gpool)
                    pool.dma_start(rows(d.xn, i, tiles), nm.xn[0:tiles[0], 0:len(tiles), :]).then_inc(stored, 16)
                bodies(pool, body)
                pool.wait_ge(stored, 16 * (FULL + 1))

            @block.vector
            def _(dve):
                def body(i, tiles):
                    nm.dve_moments(dve, i, tiles)
                    nm.dve_normalise(dve, i, tiles, [(stored, 16), (turned, 1)])
                    wait(dve, kv_done, i + 1)
                    wait(dve, sum_done, i)
                    for j, w in enumerate(tiles):
                        dve.tensor_tensor(v[0:w, j, :], k.bank[1 + j][0:w, D:2 * D], k.bkv0[0:w, D:2 * D], ALU.add)
                        ins = dve.tensor_tensor(z[0:w, j, :], k.bank[1 + j][0:w, 0:D], k.bkv0[0:w, 0:D], ALU.add)
                    ins.then_inc(z_done, 1)
                    wait(dve, z_done, i + 1)
                    w, n = tiles[0], len(tiles)
                    dve.tensor_scalar(mn[0:w, 0:n, :], z[0:w, 0:n, :], 0.0, None, ALU.min).then_inc(mn_done, 1)
                    wait(dve, e_done, i + 1)
                    dve.scalar_tensor_tensor(out=kf[0:w, 0:n, :], in0=z[0:w, 0:n, :], scalar=0.0, in1=mn[0:w, 0:n, :],
                                             op0=ALU.max, op1=ALU.add).then_inc(kf_done, 1)
                bodies(dve, body)

            @block.scalar
            def _(act):
                def body(i, tiles):
                    w, n = tiles[0], len(tiles)
                    nm.act_sd(act, i, tiles)
                    wait(act, turned, i + 1)
                    wait(act, kv_done, i)
                    for c in range(C):
                        ins = act.activation(xnT[:, c, 0:sum(tiles)], k.bank[0][:, c * BODY:c * BODY + sum(tiles)], ACT.Copy)
                    ins.then_inc(xnT_done, 1)
                    wait(act, mn_done, i + 1)
                    act.activation(mn[0:w, 0:n, :], mn[0:w, 0:n, :], ACT.Exp).then_inc(e_done, 1)
                bodies(act, body)

            @block.tensor
            def _(pe):
                def body(i, tiles):
                    wait(pe, nm.xn_done, i + 1)
                    wait(pe, xnT_done, i)
                    pe_turn(k, pe, k.bank[0], nm.xn, tiles, turned)
                    wait(pe, xnT_done, i + 1)
                    wait(pe, z_done, i)
                    for j, w in enumerate(tiles):
                        for c in range(C):
                            ins = pe.matmul(k.bank[1 + j][0:w, :], xnT[:, c, j * P:j * P + w], k.wkv0[:, c, :], start=(c == 0), stop=(c == C - 1))
                    ins.then_inc(kv_done, 1)
                    wait(pe, kf_done, i + 1)
                    first, last = isinstance(i, int) and i == 0, isinstance(i, int) and i == FULL
                    for j, w in enumerate(tiles):
                        for c in range(C):
                            f = slice(c * P, (c + 1) * P)
                            pe.matmul(k.bank[3 + c][:, 0:P], v[0:w, j, f], kf[0:w, j, f], start=first and j == 0, stop=last)
                            ins = pe.matmul(k.bank[5 + c][:, 0:1], kf[0:w, j, f], k.ones[0:w, 0:1], start=first and j == 0, stop=last)
                    ins.then_inc(sum_done, 1)
                bodies(pe, body)
        kvm = st.sb("kvm", [P, C, P])
        s1, s2, s3 = st.sem("masked"), st.sem("m0_done"), st.sem("m0_out")
        with nc.Block() as block:
            @block.vector
            def _(dve):
                for c in range(C):
                    dve.tensor_tensor(kvm[:, c, :], k.bank[3 + c][:, 0:P], k.hmask[:], ALU.mult)
                    dve.tensor_scalar(k.ks[:, c, :], k.hmask[:], k.bank[5 + c][:, 0:1], None, ALU.mult).then_inc(s1, 1)
                for c in range(C):
                    dve.wait_ge(s2, c + 1)
                    dve.tensor_copy(k.m0[:, c, :], k.bank[c][:, 0:D]).then_inc(s3, 1)

            @block.tensor
            def _(pe):
                pe.wait_ge(s1, C)
                for c in range(C):
                    pe.matmul(k.bank[c][:, 0:D], kvm[:, c, :], k.wo0[:, c, :], start=True, stop=True).then_inc(s2, 1)


def stage_clear(nc, kit, d):
    with Stage(nc, kit) as st:
        done = st.sem("cleared")
        with nc.Block() as block:
            @block.sync
            def _(sp):
                for n in range(7):
                    r = NTILE * P // 7
                    sp.dma_start(d.acc[n * r:(n + 1) * r, :].rearrange("(p t) w -> p (t w)", p=P), kit.zeros[:]).then_inc(done, 16)
                sp.wait_ge(done, 7 * 16)


def width(i):
    return N - (NTILE - 1) * P if isinstance(i, int) and i == NTILE - 1 else P


def tile_rows(ap, i, w):
    return ap[bass.ds(i * P, w), :]


def chunks(ap):
    return ap[:, 0:C * P].rearrange("p (c n) -> p c n", c=C)


class Side:

    def __init__(self, st, a, d):
        self.st, self.k, self.a, self.d = st, st.kit, a, d
        self.xn = st.sb("side_xn", [P, D])
        self.xnT = st.sb("side_xnT", [P, C, P])
        self.loaded, self.turned, self.xnT_done = st.sem("side_loaded"), st.sem("side_turned"), st.sem("side_xnT_done")
        self.gsp, self.gact, self.gdve = st.sem("side_gsp"), st.sem("side_gact"), st.sem("side_gdve")
        self.sp, self.act, self.dve, self.pe = {"move": self.move}, {2: self.copy_xnT}, {}, {1: self.turn}
        self.make()

    def engine(self, sp=None, act=None, dve=None, pe=None):
        self.e_sp, self.e_act, self.e_dve, self.e_pe = sp, act, dve, pe

    def turn(self, i, w):
        pe, k = self.e_pe, self.k
        wait(pe, self.loaded, self.loads * 16 * (i + 1))
        wait(pe, self.xnT_done, i)
        for c in range(C):
            ins = pe.transpose(k.bank[2][:, c * P:c * P + w], self.xn[0:w, c * P:(c + 1) * P], k.ident[0:w, 0:w])
        ins.then_inc(self.turned, 1)

    def copy_xnT(self, i, w):
        act = self.e_act
        wait(act, self.turned, i + 1)
        wait(act, self.xnT_read, i)
        act.activation(self.xnT[:, :, 0:w], chunks(self.k.bank[2])[:, :, 0:w], ACT.Copy).then_inc(self.xnT_done, 1)

    def sp_end(self, sp):
        pass


class LinearAttention(Side):

    def make(self):
        st = self.st
        self.loads = 2
        self.x = st.sb("side_x", [P, D])
        self.e = st.sb("side_e", [P, C, P])
        self.q = st.sb("side_q", [P, C, P])
        self.nr = st.sb("side_nr", [P, C, P])
        self.s = st.sb("side_s", [P, C, P])
        self.xm = st.sb("side_xm", [P, D])
        (self.q_psum, self.e_done, self.zr_done, self.q_done, self.nrm_psum, self.nr_done, self.qn_done, self.mix_psum,
         self.s_done, self.back, self.half, self.xm_done, self.sent) = (
            st.sem("side_" + n) for n in "q_psum e_done zr_done q_done nrm_psum nr_done qn_done mix_psum s_done back half xm_done sent".split())
        self.xnT_read = self.q_psum
        self.pe.update({4: self.query, 9: self.norms, 12: self.mix, 14: self.turn_back})
        self.act.update({5: self.exp, 13: self.add_bias})
        self.dve.update({"early": self.features, "late": self.normalise_and_sum})

    def move(self, i, w):
        sp, d = self.e_sp, self.d
        if not (isinstance(i, int) and i == 0):
            wait(sp, self.xm_done, i, self.gsp)
            sp.dma_start(tile_rows(d.xm, i - 1, P), self.xm[:]).then_inc(self.sent, 16)
        sp.dma_start(self.xn[0:w, :], tile_rows(d.xn, i, w)).then_inc(self.loaded, 16)
        sp.dma_start(self.x[0:w, :], tile_rows(self.a["x"], i, w)).then_inc(self.loaded, 16)

    def sp_end(self, sp):
        w = width(NTILE - 1)
        sp.wait_ge(self.xm_done, NTILE)
        sp.dma_start(tile_rows(self.d.xm, NTILE - 1, w), self.xm[0:w, :]).then_inc(self.sent, 16)
        sp.wait_ge(self.sent, 16 * NTILE)

    def query(self, i, w):
        pe, k = self.e_pe, self.k
        wait(pe, self.xnT_done, i + 1)
        wait(pe, self.zr_done, i)
        for o in range(C):
            for c in range(C):
                ins = pe.matmul(k.bank[3][:, o * P:o * P + w], k.wq0[:, c, o * P:(o + 1) * P], self.xnT[:, c, 0:w], start=(c == 0), stop=(c == C - 1))
        ins.then_inc(self.q_psum, 1)

    def exp(self, i, w):
        act, k = self.e_act, self.k
        wait(act, self.q_psum, i + 1)
        wait(act, self.q_done, i)
        for c in range(C):
            ins = act.activation(self.e[:, c, 0:w], k.bank[3][:, c * P:c * P + w], ACT.Exp, bias=k.bqc[:, c:c + 1])
        ins.then_inc(self.e_done, 1)

    def features(self, i, w):
        dve, k = self.e_dve, self.k
        wait(dve, self.e_done, i + 1)
        wait(dve, self.mix_psum, i)
        for c in range(C):
            ins = dve.tensor_scalar(self.q[:, c, 0:w], k.bank[3][:, c * P:c * P + w], k.bqc[:, c:c + 1], 0.0, ALU.add, ALU.max)
        ins.then_inc(self.zr_done, 1)
        wait(dve, self.zr_done, i + 1)
        dve.scalar_tensor_tensor(out=self.q[:, :, 0:w], in0=self.e[:, :, 0:w], scalar=1.0, in1=self.q[:, :, 0:w], op0=ALU.min, op1=ALU.add).then_inc(self.q_done, 1)

    def norms(self, i, w):
        pe, k = self.e_pe, self.k
        wait(pe, self.q_done, i + 1)
        wait(pe, self.nr_done, 2 * i)
        for c in range(C):
            ins = pe.matmul(k.bank[4][:, c * P:c * P + w], k.ks[:, c, :], self.q[:, c, 0:w], start=True, stop=True)
        ins.then_inc(self.nrm_psum, 1)

    def mix(self, i, w):
        pe, k = self.e_pe, self.k
        wait(pe, self.qn_done, i + 1)
        wait(pe, self.s_done, i)
        for o in range(C):
            for c in range(C):
                ins = pe.matmul(k.bank[5][:, o * P:o * P + w], k.m0[:, c, o * P:(o + 1) * P], self.q[:, c, 0:w], start=(c == 0), stop=(c == C - 1))
        ins.then_inc(self.mix_psum, 1)

    def add_bias(self, i, w):
        act, k = self.e_act, self.k
        wait(act, self.mix_psum, i + 1)
        wait(act, self.back, i)
        for c in range(C):
            ins = act.activation(self.s[:, c, 0:w], k.bank[5][:, c * P:c * P + w], ACT.Identity, bias=k.boc[:, c:c + 1])
        ins.then_inc(self.s_done, 1)

    def turn_back(self, i, w):
        pe, k = self.e_pe, self.k
        wait(pe, self.s_done, i + 1)
        wait(pe, self.half, i)
        for c in range(C):
            ins = pe.transpose(k.bank[6][0:w, c * P:(c + 1) * P], self.s[:, c, 0:w], k.ident[:])
        ins.then_inc(self.back, 1)

    def normalise_and_sum(self, i, w):
        dve, k = self.e_dve, self.k
        wait(dve, self.nrm_psum, i + 1)
        dve.tensor_scalar(self.nr[:, :, 0:w], chunks(k.bank[4])[:, :, 0:w], 1e-6, None, ALU.add).then_inc(self.nr_done, 1)
        wait(dve, self.nr_done, 2 * i + 1)
        dve.reciprocal(self.nr[:, :, 0:w], self.nr[:, :, 0:w]).then_inc(self.nr_done, 1)
        wait(dve, self.nr_done, 2 * i + 2)
        dve.tensor_tensor(self.q[:, :, 0:w], self.q[:, :, 0:w], self.nr[:, :, 0:w], ALU.mult).then_inc(self.qn_done, 1)
        wait(dve, self.back, i + 1)
        wait(dve, self.loaded, 32 * (i + 1))
        wait(dve, self.sent, 16 * i)
        dve.tensor_tensor(self.xm[0:w, :], k.bank[6][0:w, 0:D], self.x[0:w, :], ALU.add).then_inc(self.half, 1)
        wait(dve, self.half, i + 1)
        dve.tensor_tensor(self.xm[0:w, :], self.xm[0:w, :], self.xn[0:w, :], ALU.add).then_inc(self.xm_done, 1)


class KeySums(Side):

    def make(self):
        st = self.st
        self.loads = 1
        self.z = st.sb("side_z", [P, D])
        self.v = st.sb("side_v", [P, D + 1])
        (self.kv_psum, self.z_done, self.e_done, self.summed, self.one) = (st.sem("side_" + n) for n in "kv_psum z_done e_done summed one".split())
        self.xnT_read = self.kv_psum
        self.pe.update({4: self.keys_values, 12: self.sum})
        self.act.update({8: self.exp})
        self.dve.update({"early": self.add_bias})

    def engine(self, sp=None, act=None, dve=None, pe=None):
        Side.engine(self, sp, act, dve, pe)
        if dve is not None:
            dve.memset(self.v[:, D:D + 1], 1.0).then_inc(self.one, 1)

    def move(self, i, w):
        sp = self.e_sp
        wait(sp, self.turned, i, self.gsp)
        sp.dma_start(self.xn[0:w, :], tile_rows(self.d.xn, i, w)).then_inc(self.loaded, 16)

    def keys_values(self, i, w):
        pe, k = self.e_pe, self.k
        wait(pe, self.xnT_done, i + 1)
        wait(pe, self.z_done, i)
        for c in range(C):
            ins = pe.matmul(k.bank[3][0:w, :], self.xnT[:, c, 0:w], k.wkv1[:, c, :], start=(c == 0), stop=(c == C - 1))
        ins.then_inc(self.kv_psum, 1)

    def add_bias(self, i, w):
        dve, k = self.e_dve, self.k
        wait(dve, self.kv_psum, i + 1)
        wait(dve, self.summed, i)
        dve.tensor_tensor(self.z[0:w, :], k.bank[3][0:w, 0:D], k.bkv1[0:w, 0:D], ALU.add)
        dve.tensor_tensor(self.v[0:w, 0:D], k.bank[3][0:w, D:2 * D], k.bkv1[0:w, D:2 * D], ALU.add).then_inc(self.z_done, 1)

    def exp(self, i, w):
        act = self.e_act
        wait(act, self.z_done, i + 1)
        act.activation(self.z[0:w, :], self.z[0:w, :], ACT.Exp).then_inc(self.e_done, 1)

    def sum(self, i, w):
        pe, k = self.e_pe, self.k
        first, last = isinstance(i, int) and i == 0, isinstance(i, int) and i == NTILE - 1
        if first:
            pe.wait_ge(self.one, 1)
        wait(pe, self.e_done, i + 1)
        for c in range(C):
            ins = pe.matmul(k.bank[4 + c][:, 0:D + 1], self.z[0:w, c * P:(c + 1) * P], self.v[0:w, :], start=first, stop=last)
        ins.then_inc(self.summed, 1)


class QueryMix(Side):

    def make(self):
        st = self.st
        self.loads = 2
        self.x = st.sb("side_x", [P, D])
        self.xm = st.sb("side_xm", [P, D])
        (self.q_psum, self.half, self.xm_done, self.sent) = (st.sem("side_" + n) for n in "q_psum half xm_done sent".split())
        self.xnT_read = self.q_psum
        self.pe.update({4: self.query})
        self.dve.update({"early": self.add})

    def move(self, i, w):
        sp, d = self.e_sp, self.d
        if not (isinstance(i, int) and i == 0):
            wait(sp, self.xm_done, i, self.gsp)
            sp.dma_start(tile_rows(d.xm, i - 1, P), self.xm[:]).then_inc(self.sent, 16)
        sp.dma_start(self.xn[0:w, :], tile_rows(d.xn, i, w)).then_inc(self.loaded, 16)
        sp.dma_start(self.x[0:w, :], tile_rows(d.x2, i, w)).then_inc(self.loaded, 16)

    sp_end = LinearAttention.sp_end

    def query(self, i, w):
        pe, k = self.e_pe, self.k
        wait(pe, self.xnT_done, i + 1)
        wait(pe, self.half, i)
        for c in range(C):
            ins = pe.matmul(k.bank[3][0:w, 0:D], self.xnT[:, c, 0:w], k.mq[:, c, :], start=(c == 0), stop=(c == C - 1))
        ins.then_inc(self.q_psum, 1)

    def add(self, i, w):
        dve, k = self.e_dve, self.k
        wait(dve, self.q_psum, i + 1)
        wait(dve, self.loaded, 32 * (i + 1))
        wait(dve, self.sent, 16 * i)
        dve.tensor_tensor(self.xm[0:w, :], k.bank[3][0:w, 0:D], k.bmq[0:w, :], ALU.add).then_inc(self.half, 1)
        wait(dve, self.half, i + 1)
        dve.tensor_tensor(self.xm[0:w, :], self.xm[0:w, :], self.x[0:w, :], ALU.add).then_inc(self.xm_done, 1)


def stage_aggregate(nc, kit, a, d, table, side_of):
    k = kit
    stage_clear(nc, kit, d)
    with Stage(nc, kit) as st:
        side = side_of(st, a, d)
        fast = st.ctx.enter_context(ExitStack())

        def sb(name, shape, dt=F32):
            return fast.enter_context(nc.sbuf_tensor(name + st.tag, shape, dt))
        gidx = [sb(f"gidx{h}", [P, GT], I32) for h in range(2)]
        sidx = [sb(f"sidx{h}", [P, 1], I32) for h in range(2)]
        g = [sb(f"g{u}", [P, D]) for u in range(2 * GT)]
        gw = [sb(f"gw{h}", [P, GT, AW]) for h in range(2)]
        m = [sb(f"m{u}", [P, P]) for u in range(2 * GT)]
        r = [sb(f"r{h}", [P, AW]) for h in range(2)]
        gathered = [st.pool_dma(f"gathered{u}") for u in range(2 * GT)]
        idx_done, ext_done, m_done, weighted, multiplied, row_done, scattered = (
            st.sem(s) for s in ("idx_done", "ext_done", "m_done", "weighted", "multiplied", "row_done", "scattered"))
        gpool, gact = st.sem("gpool"), st.sem("gact")
        NB = NG // 2
        drow = sb("drow", [P, P], I32)
        dup = sb("dup", [P, P])
        ndup = sb("ndup", [P, 1])
        row_loaded, dup_done = st.sem("row_loaded"), st.sem("dup_done")
        gsp = st.sem("gsp")

        def loop(eng, body):
            body(0)
            with eng.Fori(1, NB - 1) as i:
                body(i)
            body(NB - 1)

        def along(fns, name, i):
            if name in fns:
                fns[name](i, width(i))

        def fast_pool(pool):
            def scatter(i, h):
                grp = 2 * i + h
                wait(pool, row_done, grp + 1, gpool)
                wait(pool, scattered, 16 * grp, gpool)
                pool.indirect_dma_start(d.acc, bass.IndirectOffsetOnAxis(ap=sidx[h][:], axis=0), r[h][:], None,
                                        bounds_check=N - 1, oob_is_err=False, compute_op=ALU.add).then_inc(scattered, 16)

            def body(i):
                for h in range(2):
                    wait(pool, idx_done, 2 * i + h + 1, gpool)
                    for u in range(GT):
                        s = h * GT + u
                        wait(pool, weighted, 16 * i + s - 15, gpool)
                        pool.indirect_dma_start(g[s][:], None, table, bass.IndirectOffsetOnAxis(ap=gidx[h][:, u:u + 1], axis=0)).then_inc(gathered[s], 16)
                    if h == 1:
                        scatter(i, 0)
                    elif not (isinstance(i, int) and i == 0):
                        scatter(i - 1, 1)
            loop(pool, body)
            scatter(NB - 1, 1)
            pool.wait_ge(scattered, 16 * NG)

        def fast_act(act):
            def body(i):
                for s in range(2 * GT):
                    wait(act, multiplied, 16 * i + s - 15, gact)
                    wait(act, gathered[s], 16 * (i + 1), gact)
                    act.activation(gw[s // GT][:, s % GT, 0:D], g[s][:], ACT.Copy, scale=k.ew_f[:, bass.ds(i * 16 + s, 1)]).then_inc(weighted, 1)
                    along(side.act, s, i)
            loop(act, body)

        def fast_dve(dve):
            def prepare(i, h):
                wait(dve, weighted, 16 * i + 8 * h - 8)
                dve.tensor_copy(gidx[h][:], k.src_i[:, bass.ds(i * 16 + h * 8, 8)]).then_inc(idx_done, 1)
                wait(dve, multiplied, 16 * i + 8 * h - 8)
                dve.tensor_copy(gw[h][:, :, D:AW], k.ext[:, bass.ds(i * 16 + h * 8, 8), :]).then_inc(ext_done, 1)
                for u in range(GT):
                    dve.tensor_scalar(m[h * GT + u][:], k.iota[:], k.rank_f[:, bass.ds(i * 16 + h * 8 + u, 1)], None, ALU.is_equal).then_inc(m_done, 1)

            def finish(i, h):
                wait(dve, multiplied, 16 * i + 8 * h + 8)
                wait(dve, scattered, 16 * (2 * i + h - 1))
                dve.tensor_scalar(sidx[h][:], k.bank[h][:, AW - 1:AW], FAR, None, ALU.add)
                dve.tensor_copy(r[h][:], k.bank[h][:, 0:AW]).then_inc(row_done, 1)

            def body(i):
                prepare(i, 0)
                if not (isinstance(i, int) and i == 0):
                    along(side.dve, "late", i - 1)
                    finish(i - 1, 1)
                prepare(i, 1)
                along(side.dve, "early", i)
                finish(i, 0)
            loop(dve, body)
            along(side.dve, "late", NB - 1)
            finish(NB - 1, 1)

        def fast_pe(pe):
            def body(i):
                for s in range(2 * GT):
                    h, u = s // GT, s % GT
                    if u == 0:
                        wait(pe, ext_done, 2 * i + h + 1)
                        wait(pe, row_done, 2 * i + h - 1)
                    wait(pe, m_done, 16 * i + s + 1)
                    wait(pe, weighted, 16 * i + s + 1)
                    pe.matmul(k.bank[h][:, 0:AW], m[s][:], gw[h][:, u, :], start=(u == 0), stop=(u == GT - 1)).then_inc(multiplied, 1)
                    along(side.pe, s, i)
            loop(pe, body)

        def tiles_of_edges(eng, body):
            body(0)
            with eng.Fori(1, NET) as t:
                body(t)

        def general_sp(sp):
            def body(t):
                wait(sp, m_done, t, gsp)
                wait(sp, dup_done, 2 * t, gsp)
                sp.dma_start(drow[:], bass.AP(tensor=d.dst.tensor, offset=t * P, ap=[[0, P], [1, P]])).then_inc(row_loaded, 16)
            tiles_of_edges(sp, body)

        def general_pool(pool):
            def body(t):
                wait(pool, idx_done, t + 1, gpool)
                wait(pool, weighted, t, gpool)
                pool.indirect_dma_start(g[0][:], None, table, bass.IndirectOffsetOnAxis(ap=gidx[0][:, 0:1], axis=0)).then_inc(gathered[0], 16)
                wait(pool, row_done, t + 1, gpool)
                wait(pool, scattered, 16 * t, gpool)
                pool.indirect_dma_start(d.acc, bass.IndirectOffsetOnAxis(ap=sidx[0][:], axis=0), r[0][:], None,
                                        bounds_check=N - 1, oob_is_err=False, compute_op=ALU.add).then_inc(scattered, 16)
            tiles_of_edges(pool, body)
            pool.wait_ge(scattered, 16 * NET)

        def general_act(act):
            def body(t):
                wait(act, multiplied, t, gact)
                wait(act, gathered[0], 16 * (t + 1), gact)
                act.activation(gw[0][:, 0, 0:D], g[0][:], ACT.Copy, scale=k.ew_f[:, bass.ds(t, 1)]).then_inc(weighted, 1)
            tiles_of_edges(act, body)

        def general_dve(dve):
            def body(t):
                wait(dve, weighted, t)
                dve.tensor_copy(gidx[0][:, 0:1], k.src_i[:, bass.ds(t, 1)]).then_inc(idx_done, 1)
                wait(dve, multiplied, t)
                dve.tensor_copy(gw[0][:, 0:1, D:AW], k.ext[:, bass.ds(t, 1), :]).then_inc(ext_done, 1)
                wait(dve, row_loaded, 16 * (t + 1))
                dve.tensor_scalar(m[0][:], drow[:], k.dst_f[:, bass.ds(t, 1)], None, ALU.is_equal).then_inc(m_done, 1)
                wait(dve, dup_done, 2 * t)
                wait(dve, m_done, t + 1)
                dve.tensor_tensor(dup[:], m[0][:], k.tri[:], ALU.mult).then_inc(dup_done, 1)
                wait(dve, dup_done, 2 * t + 1)
                wait(dve, row_done, t)
                dve.tensor_reduce(ndup[:], dup[:], AX.X, ALU.add).then_inc(dup_done, 1)
                wait(dve, dup_done, 2 * t + 2)
                wait(dve, scattered, 16 * t)
                dve.scalar_tensor_tensor(out=sidx[0][:], in0=ndup[:], scalar=FAR, in1=k.dst_f[:, bass.ds(t, 1)], op0=ALU.mult, op1=ALU.add)
                wait(dve, multiplied, t + 1)
                dve.tensor_copy(r[0][:], k.bank[0][:, 0:AW]).then_inc(row_done, 1)
            tiles_of_edges(dve, body)

        def general_pe(pe):
            def body(t):
                wait(pe, ext_done, t + 1)
                wait(pe, row_done, t)
                wait(pe, m_done, t + 1)
                wait(pe, weighted, t + 1)
                pe.matmul(k.bank[0][:, 0:AW], m[0][:], gw[0][:, 0, :], start=True, stop=True).then_inc(multiplied, 1)
            tiles_of_edges(pe, body)

        def either(eng, fast_path, general_path, steps):
            grouped = eng.value_load(k.flag[0:1, 0:1])
            with eng.If(grouped == 1):
                fast_path(eng)
            with eng.Else():
                if general_path:
                    general_path(eng)
                loop(eng, lambda i: [along(steps, name, i) for name in steps])

        with nc.Block() as block:
            @block.sync
            def _(sp):
                side.engine(sp=sp)
                either(sp, lambda eng: loop(eng, lambda i: side.sp["move"](i, width(i))), general_sp, side.sp)
                side.sp_end(sp)

            @block.gpsimd
            def _(pool):
                either(pool, fast_pool, general_pool, {})

            @block.scalar
            def _(act):
                side.engine(act=act)
                either(act, fast_act, general_act, side.act)

            @block.vector
            def _(dve):
                side.engine(dve=dve)
                either(dve, fast_dve, general_dve, side.dve)

            @block.tensor
            def _(pe):
                side.engine(pe=pe)
                either(pe, fast_pe, general_pe, side.pe)


def coefficients(nc, st, kit, stats, gamma, beta, scale, shift, tag):
    mv = st.sb("bmv" + tag, [P, C, 2])
    sd = st.sb("bsd" + tag, [P, C])
    s1, s2, s3 = st.sem("bm" + tag), st.sem("bs" + tag), st.sem("bc" + tag)
    with nc.Block() as block:
        @block.vector
        def _(dve):
            for c in range(C):
                ins = dve.bn_aggr(mv[:, c, :], stats[:, c, :, :].rearrange("p i s -> p (i s)"))
            ins.then_inc(s1, 1)
            dve.wait_ge(s2, 1)
            dve.reciprocal(sd[:], sd[:]).then_inc(s3, 1)
            dve.wait_ge(s3, 1)
            dve.tensor_tensor(scale[:], sd[:], gamma[:], ALU.mult).then_inc(s3, 1)
            dve.wait_ge(s3, 2)
            dve.tensor_tensor(sd[:], mv[:, :, 0], scale[:], ALU.mult).then_inc(s3, 1)
            dve.wait_ge(s3, 3)
            dve.tensor_tensor(shift[:], beta[:], sd[:], ALU.subtract).then_inc(s3, 1)

        @block.scalar
        def _(act):
            act.wait_ge(s1, 1)
            act.activation(sd[:], mv[:, :, 1], ACT.Sqrt, bias=kit.eps[:]).then_inc(s2, 1)


def stage_gnn_first(nc, kit, a, d):
    k = kit
    with Stage(nc, kit) as st:
        at = st.sb("at", [P, 2, AW])
        xn = st.sb("xnb", [P, 2, D])
        y = st.sb("y", [P, 2, D])
        yT = st.sb("yT", [P, C, BODY])
        cnt = st.sb("cnt", [P, 2])
        nnb = st.sb("nnb", [P, 2, P])
        stats = st.sb("stats", [P, C, FULL + 1, 6])
        loaded, y_done, cnt_done, root_done, rn_done, nnb_done, turned, yT_done, z_done, kept, nbc_done, nkept, stat_done, wd_done = (
            st.sem(s) for s in ("loaded", "y_done", "cnt_done", "root_done", "rn_done", "nnb_done", "turned", "yT_done", "z_done", "kept", "nbc_done", "nkept", "stat_done", "wd_done"))
        gsp, gact, gdve = st.sem("gsp"), st.sem("gact"), st.sem("gdve")
        with nc.Block() as block:
            @block.sync
            def _(sp):
                def body(i, tiles):
                    w, n = tiles[0], len(tiles)
                    wait(sp, y_done, i, gsp)
                    wait(sp, wd_done, i, gsp)
                    sp.dma_start(at[0:w, 0:n, :], rows(d.acc, i, tiles)).then_inc(loaded, 16)
                    sp.dma_start(xn[0:w, 0:n, :], rows(d.xn, i, tiles)).then_inc(loaded, 16)
                bodies(sp, body)

            @block.vector
            def _(dve):
                def body(i, tiles):
                    w, n, wt = tiles[0], len(tiles), sum(tiles)
                    wait(dve, loaded, 32 * (i + 1))
                    wait(dve, nnb_done, i)
                    dve.tensor_scalar(cnt[0:w, 0:n], at[0:w, 0:n, D + 1], 1.0, None, ALU.max).then_inc(cnt_done, 1)
                    dve.tensor_copy(k.wdeg[0:w, bass.ds(i * 2, n)], at[0:w, 0:n, D]).then_inc(wd_done, 1)
                    wait(dve, turned, i)
                    dve.scalar_tensor_tensor(out=y[0:w, 0:n, :], in0=xn[0:w, 0:n, :], scalar=k.epsw[0:w, :], in1=at[0:w, 0:n, 0:D],
                                             op0=ALU.mult, op1=ALU.add).then_inc(y_done, 1)
                    wait(dve, root_done, i + 1)
                    dve.reciprocal(cnt[0:w, 0:n], cnt[0:w, 0:n]).then_inc(rn_done, 1)
                    wait(dve, rn_done, i + 1)
                    wait(dve, nbc_done, i)
                    for j in range(n):
                        ins = dve.tensor_scalar(nnb[0:w, j, :], k.ones[0:w, :], cnt[0:w, j:j + 1], None, ALU.mult)
                    ins.then_inc(nnb_done, 1)
                    wait(dve, kept, i + 1, gdve)
                    for c in range(C):
                        ins = dve.bn_stats(stats[:, c, i, :] if isinstance(i, int) else stats[:, c, bass.ds(i, 1), :].rearrange("p a s -> p (a s)"),
                                           k.bank[1 + c][:, 0:wt])
                    ins.then_inc(stat_done, 1)
                bodies(dve, body)

            @block.scalar
            def _(act):
                def body(i, tiles):
                    w, n, wt = tiles[0], len(tiles), sum(tiles)
                    wait(act, cnt_done, i + 1)
                    act.activation(cnt[0:w, 0:n], cnt[0:w, 0:n], ACT.Sqrt).then_inc(root_done, 1)
                    wait(act, turned, i + 1)
                    wait(act, z_done, i)
                    act.activation(yT[:, :, 0:wt], halves(k.bank[0][:])[:, :, 0:wt], ACT.Copy).then_inc(yT_done, 1)
                    wait(act, z_done, i + 1, gact)
                    for c in range(C):
                        ins = act.activation(k.zT[:, c, bass.ds(i * BODY, wt)], k.bank[1 + c][:, 0:wt], ACT.Copy)
                    ins.then_inc(kept, 1)
                    wait(act, nbc_done, i + 1, gact)
                    act.activation(k.nbc[:, bass.ds(i * BODY, wt)], k.bank[3][:, 0:wt], ACT.Copy).then_inc(nkept, 1)
                bodies(act, body)

            @block.tensor
            def _(pe):
                def body(i, tiles):
                    wt = sum(tiles)
                    wait(pe, y_done, i + 1)
                    wait(pe, yT_done, i)
                    pe_turn(k, pe, k.bank[0], y, tiles, turned)
                    wait(pe, yT_done, i + 1)
                    wait(pe, kept, i)
                    wait(pe, stat_done, i)
                    for o in range(C):
                        for c in range(C):
                            ins = pe.matmul(k.bank[1 + o][:, 0:wt], k.w1T[:, c, o * P:(o + 1) * P], yT[:, c, 0:wt], start=(c == 0), stop=(c == C - 1))
                    ins.then_inc(z_done, 1)
                    wait(pe, nnb_done, i + 1)
                    wait(pe, nkept, i)
                    for j, w in enumerate(tiles):
                        ins = pe.matmul(k.bank[3][:, j * P:j * P + w], nnb[0:w, j, :], k.ident[0:w, 0:w], start=True, stop=True)
                    ins.then_inc(nbc_done, 1)
                bodies(pe, body)
        coefficients(nc, st, kit, stats, k.g1c, k.be1c, k.s1, k.t1, "1")
        c1, c2 = st.sem("dg"), st.sem("dgs")
        pos = st.sb("pos", [P, NTILE + 1])
        with nc.Block() as block:
            @block.vector
            def _(dve):
                dve.tensor_scalar(k.wdeg[:], k.wdeg[:], 1.0, None, ALU.add).then_inc(c1, 1)
                dve.wait_ge(c1, 1)
                dve.tensor_scalar(pos[:], k.wdeg[:], 0.0, None, ALU.is_gt).then_inc(c1, 1)
                dve.wait_ge(c1, 2)
                dve.tensor_scalar(k.wdeg[:], k.wdeg[:], 1e-30, None, ALU.max).then_inc(c1, 1)
                dve.wait_ge(c2, 1)
                dve.reciprocal(k.wdeg[:], k.wdeg[:]).then_inc(c1, 1)
                dve.wait_ge(c1, 4)
                dve.tensor_tensor(k.wdeg[:], k.wdeg[:], pos[:], ALU.mult).then_inc(c1, 1)

            @block.scalar
            def _(act):
                act.wait_ge(c1, 3)
                act.activation(k.wdeg[:], k.wdeg[:], ACT.Sqrt).then_inc(c2, 1)


def stage_gnn_second(nc, kit, a, d):
    k = kit
    with Stage(nc, kit) as st:
        hT = st.sb("hT", [P, C, BODY])
        stats = st.sb("stats", [P, C, FULL + 1, 6])
        h_done, u_done, kept, stat_done = (st.sem(s) for s in ("h_done", "u_done", "kept", "stat_done"))
        gact, gdve = st.sem("gact"), st.sem("gdve")
        with nc.Block() as block:
            @block.scalar
            def _(act):
                def body(i, tiles):
                    wt = sum(tiles)
                    wait(act, u_done, i, gact)
                    for c in range(C):
                        ins = act.activation(hT[:, c, 0:wt], k.zT[:, c, bass.ds(i * BODY, wt)], ACT.Relu, bias=k.t1[:, c:c + 1], scale=k.s1[:, c:c + 1])
                    ins.then_inc(h_done, 1)
                bodies(act, body)

            @block.vector
            def _(dve):
                def body(i, tiles):
                    wt = sum(tiles)
                    wait(dve, u_done, i + 1, gdve)
                    for c in range(C):
                        ins = dve.tensor_tensor(k.zT[:, c, bass.ds(i * BODY, wt)], k.bank[c][:, 0:wt], k.nbc[:, bass.ds(i * BODY, wt)], ALU.mult)
                    ins.then_inc(kept, 1)
                    wait(dve, kept, i + 1, gdve)
                    for c in range(C):
                        ins = dve.bn_stats(stats[:, c, i, :] if isinstance(i, int) else stats[:, c, bass.ds(i, 1), :].rearrange("p a s -> p (a s)"),
                                           k.zT[:, c, bass.ds(i * BODY, wt)])
                    ins.then_inc(stat_done, 1)
                bodies(dve, body)

            @block.tensor
            def _(pe):
                def body(i, tiles):
                    wt = sum(tiles)
                    wait(pe, h_done, i + 1)
                    wait(pe, kept, i)
                    for o in range(C):
                        for c in range(C):
                            ins = pe.matmul(k.bank[o][:, 0:wt], k.w2T[:, c, o * P:(o + 1) * P], hT[:, c, 0:wt], start=(c == 0), stop=(c == C - 1))
                    ins.then_inc(u_done, 1)
                bodies(pe, body)
        coefficients(nc, st, kit, stats, k.ghc, k.behc, k.s2, k.t2, "2")


def stage_combine(nc, kit, a, d):
    k = kit
    with Stage(nc, kit) as st:
        xm = st.sb("xm", [P, 2, D])
        rT = st.sb("reluT", [P, C, BODY])
        x1 = st.sb("x1", [P, 2, D])
        loaded, r_done, back_done, x1_done, stored, gsp, gact, gpool = (
            st.sem(n) for n in "loaded r_done back_done x1_done stored gsp gact gpool".split())
        with nc.Block() as block:
            @block.sync
            def _(sp):
                def body(i, tiles):
                    w, n = tiles[0], len(tiles)
                    wait(sp, x1_done, i, gsp)
                    sp.dma_start(xm[0:w, 0:n, :], rows(d.xm, i, tiles)).then_inc(loaded, 16)
                bodies(sp, body)

            @block.gpsimd
            def _(pool):
                def body(i, tiles):
                    w, n = tiles[0], len(tiles)
                    wait(pool, x1_done, i + 1, gpool)
                    pool.dma_start(rows(d.x1, i, tiles), x1[0:w, 0:n, :]).then_inc(stored, 16)
                bodies(pool, body)
                pool.wait_ge(stored, 16 * (FULL + 1))

            @block.scalar
            def _(act):
                def body(i, tiles):
                    wt = sum(tiles)
                    wait(act, back_done, i, gact)
                    for c in range(C):
                        ins = act.activation(rT[:, c, 0:wt], k.zT[:, c, bass.ds(i * BODY, wt)], ACT.Relu, bias=k.t2[:, c:c + 1], scale=k.s2[:, c:c + 1])
                    ins.then_inc(r_done, 1)
                bodies(act, body)

            @block.vector
            def _(dve):
                def body(i, tiles):
                    w, n = tiles[0], len(tiles)
                    wait(dve, loaded, 16 * (i + 1))
                    wait(dve, back_done, i + 1)
                    wait(dve, stored, 16 * i)
                    dve.tensor_tensor(x1[0:w, 0:n, :], k.bank[6][0:w, 0:n * D].rearrange("p (j d) -> p j d", d=D), xm[0:w, 0:n, :], ALU.add).then_inc(x1_done, 1)
                bodies(dve, body)

            @block.tensor
            def _(pe):
                def body(i, tiles):
                    wait(pe, r_done, i + 1)
                    wait(pe, x1_done, i)
                    for j, w in enumerate(tiles):
                        for c in range(C):
                            ins = pe.transpose(k.bank[6][0:w, j * D + c * P:j * D + (c + 1) * P], rT[:, c, j * P:j * P + w], k.ident[:])
                    ins.then_inc(back_done, 1)
                bodies(pe, body)


def stage_route(nc, kit, a, d):
    k = kit
    with Stage(nc, kit) as st:
        xt = st.sb("xt", [P, 2, D])
        xnT = st.sb("xnT", [P, C, BODY])
        lg = st.sb("lg", [P, 2, EXPERTS])
        top = st.sb("top", [P, 2, 8])
        topi = st.sb("topi", [P, 2, 8], mybir.dt.uint32)
        topf = st.sb("topf", [P, 2, 1])
        one = st.sb("one", [P, 2, EXPERTS])
        seen = st.sb("seen", [P, 2, EXPERTS])
        at = st.sb("at", [P, 2, EXPERTS])
        chosen = st.sb("chosen", [P, NTILE + 1, EXPERTS])
        loaded = st.sem("loaded")
        nm = Norm(st, "d", xt, loaded, 16)
        (turned, xnT_done, lg_psum, lg_done, top_done, topi_done, topf_done, one_done, seen_done, place_psum, place_done, pos_done, kept, cleared, stored, zeroed) = (
            st.sem(n) for n in "turned xnT_done lg_psum lg_done top_done topi_done topf_done one_done seen_done place_psum place_done pos_done kept cleared stored zeroed".split())
        gsp, gpool, gdve = st.sem("gsp"), st.sem("gpool"), st.sem("gdve")
        with nc.Block() as block:
            @block.sync
            def _(sp):
                def body(i, tiles):
                    wait(sp, nm.xn_done, i, gsp)
                    sp.dma_start(xt[0:tiles[0], 0:len(tiles), :], rows(d.x1, i, tiles)).then_inc(loaded, 16)
                bodies(sp, body)
                per = SORTED * D // 16
                for n in range(16):
                    sp.dma_start(d.xs.rearrange("(p r) d -> p (r d)", p=P)[:, n * per:(n + 1) * per], k.zeros[:, 0:per]).then_inc(zeroed, 16)
                sp.wait_ge(zeroed, 16 * 16)

            @block.gpsimd
            def _(pool):
                def body(i, tiles):
                    w, n = tiles[0], len(tiles)
                    wait(pool, nm.xn_done, i + 1, gpool)
                    pool.dma_start(rows(d.xn, i, tiles), nm.xn[0:w, 0:n, :]).then_inc(stored, 16)
                bodies(pool, body)
                pool.wait_ge(stored, 16 * (FULL + 1))

            @block.scalar
            def _(act):
                def body(i, tiles):
                    nm.act_sd(act, i, tiles)
                    wait(act, turned, i + 1)
                    wait(act, lg_psum, i)
                    act.activation(xnT[:, :, 0:sum(tiles)], halves(k.bank[0][:])[:, :, 0:sum(tiles)], ACT.Copy).then_inc(xnT_done, 1)
                bodies(act, body)

            @block.vector
            def _(dve):
                dve.memset(chosen[:], 0.0).then_inc(cleared, 1)
                dve.memset(k.pos[:], 0.0).then_inc(cleared, 1)
                dve.memset(seen[:], 0.0).then_inc(cleared, 1)
                dve.wait_ge(cleared, 3)

                def body(i, tiles):
                    w, n = tiles[0], len(tiles)
                    nm.dve_moments(dve, i, tiles)
                    nm.dve_normalise(dve, i, tiles, [(turned, 1), (stored, 16)])
                    wait(dve, lg_psum, i + 1)
                    wait(dve, topi_done, i)
                    dve_all = dve.tensor_tensor(lg[0:w, 0:n, :], k.bank[1][0:w, 0:n * EXPERTS].rearrange("p (j e) -> p j e", e=EXPERTS),
                                                k.rb2[0:w, 0:n, :], ALU.add)
                    dve_all.then_inc(lg_done, 1)
                    wait(dve, lg_done, i + 1, gdve)
                    for j in range(n):
                        ins = dve.max(top[0:w, j, :], lg[0:w, j, :])
                    ins.then_inc(top_done, 1)
                    wait(dve, top_done, i + 1, gdve)
                    for j in range(n):
                        ins = dve.max_index(topi[0:w, j, :], top[0:w, j, :], lg[0:w, j, :])
                    ins.then_inc(topi_done, 1)
                    wait(dve, topi_done, i + 1)
                    dve.tensor_copy(topf[0:w, 0:n, :], topi[0:w, 0:n, 0:1]).then_inc(topf_done, 1)
                    wait(dve, topf_done, i + 1)
                    wait(dve, place_psum, i)
                    wait(dve, kept, i)
                    for j in range(n):
                        ins = dve.tensor_scalar(one[0:w, j, :], k.iota[0:w, 0:EXPERTS], topf[0:w, j, :], None, ALU.is_equal)
                    ins.then_inc(one_done, 1)
                    wait(dve, one_done, i + 1)
                    if n == 2:
                        dve.tensor_tensor(seen[:, 1, :], seen[:, 0, :], one[:, 0, :], ALU.add).then_inc(seen_done, 1)
                    dve.tensor_copy(chosen[0:w, bass.ds(i * 2, n), :], one[0:w, 0:n, :]).then_inc(kept, 1)
                    wait(dve, place_psum, i + 1)
                    wait(dve, pos_done, i)
                    dve.tensor_tensor(at[0:w, 0:n, :], k.bank[2][0:w, 0:n * EXPERTS].rearrange("p (j e) -> p j e", e=EXPERTS), one[0:w, 0:n, :], ALU.mult).then_inc(place_done, 1)
                    dve.tensor_tensor(seen[0:w, 0, :], seen[0:w, n - 1, :], one[0:w, n - 1, :], ALU.add).then_inc(seen_done, 1)
                    wait(dve, seen_done, 2 * (i + 1) if n == 2 else 2 * FULL + 1)
                    wait(dve, place_done, i + 1)
                    dve.tensor_reduce(k.pos[0:w, bass.ds(i * 2, n)], at[0:w, 0:n, :], AX.X, ALU.add).then_inc(pos_done, 1)
                bodies(dve, body)

            @block.tensor
            def _(pe):
                pe.wait_ge(cleared, 3)

                def body(i, tiles):
                    wait(pe, nm.xn_done, i + 1)
                    wait(pe, xnT_done, i)
                    pe_turn(k, pe, k.bank[0], nm.xn, tiles, turned)
                    wait(pe, xnT_done, i + 1)
                    wait(pe, lg_done, i)
                    for j, w in enumerate(tiles):
                        for c in range(C):
                            ins = pe.matmul(k.bank[1][0:w, j * EXPERTS:(j + 1) * EXPERTS], xnT[:, c, j * P:j * P + w], k.rT[:, c, :], start=(c == 0), stop=(c == C - 1))
                    ins.then_inc(lg_psum, 1)
                    wait(pe, one_done, i + 1)
                    wait(pe, seen_done, 2 * i + 1 if len(tiles) == 2 else 2 * i)
                    wait(pe, place_done, i)
                    for j, w in enumerate(tiles):
                        pe.matmul(k.bank[2][0:w, j * EXPERTS:(j + 1) * EXPERTS], k.upper[0:w, 0:w], one[0:w, j, :], start=True, stop=False)
                        ins = pe.matmul(k.bank[2][0:w, j * EXPERTS:(j + 1) * EXPERTS], k.ones[:, 0:w], seen[:, j, :], start=False, stop=True)
                    ins.then_inc(place_psum, 1)
                bodies(pe, body)
        cnt_i = st.sb("cnt_i", [P, EXPERTS], I32)
        cnt = st.sb("cnt", [P, EXPERTS])
        upto = st.sb("upto", [P, EXPERTS])
        base = st.sb("base", [P, EXPERTS])
        zed = st.sb("zed", [P, EXPERTS])
        big = st.sb("big", [P, NTILE + 1, EXPERTS])
        te = st.sb("te", [1, SORTED, EXPERTS])
        tf = st.sb("tf", [1, SORTED])
        s1, s2 = st.sem("s1"), st.sem("s2")
        with nc.Block() as block:
            @block.tensor
            def _(pe):
                pe.matmul(k.bank[3][:, 0:EXPERTS], k.ones[:], seen[:, 0, :], start=True, stop=True).then_inc(s2, 1)

            @block.vector
            def _(dve):
                n = [0]

                def then(ins):
                    n[0] += 1
                    ins.then_inc(s1, 1)
                    dve.wait_ge(s1, n[0])
                then(dve.memset(zed[:], 0.0))
                dve.wait_ge(s2, 1)
                then(dve.tensor_scalar(cnt_i[:], k.bank[3][:, 0:EXPERTS], float(P - 1), None, ALU.add))
                then(dve.tensor_scalar(cnt_i[:], cnt_i[:], 7, None, ALU.arith_shift_right))
                then(dve.tensor_copy(cnt[:], cnt_i[:]))
                then(dve.tensor_tensor_scan(upto[:], cnt[:], zed[:], 0.0, ALU.add, ALU.add))
                then(dve.tensor_tensor(base[:], upto[:], cnt[:], ALU.subtract))
                then(dve.tensor_tensor(big[:], chosen[:], base[:].rearrange("p (a e) -> p a e", a=1).to_broadcast([P, NTILE + 1, EXPERTS]), ALU.mult))
                then(dve.tensor_reduce(k.slot_f[:], big[:], AX.X, ALU.add))
                then(dve.scalar_tensor_tensor(out=k.slot_i[:], in0=k.slot_f[:], scalar=float(P), in1=k.pos[:], op0=ALU.mult, op1=ALU.add))
                then(dve.tensor_tensor(te[:], k.iota[0:1, 0:SORTED].rearrange("p (s a) -> p s a", a=1).to_broadcast([1, SORTED, EXPERTS]),
                                       upto[0:1, :].rearrange("p (a e) -> p a e", a=1).to_broadcast([1, SORTED, EXPERTS]), ALU.is_ge))
                then(dve.tensor_reduce(tf[:], te[:], AX.X, ALU.add))
                then(dve.tensor_scalar(k.tile_expert[:], tf[:], float(EXPERTS - 1), None, ALU.min))
        xb = [st.sb(f"xb{s}", [P, D]) for s in range(4)]
        ix = [st.sb(f"ix{s}", [P, 1], I32) for s in range(4)]
        lds = [st.sem(f"row_loaded{s}") for s in range(4)]
        sent = [st.pool_dma(f"sent{s}") for s in range(4)]
        ixd = st.sem("ix_done")

        def fours(eng, body):
            body(0, range(4), P)
            with eng.Fori(1, NTILE // 4) as i:
                body(i, range(4), P)
            body(NTILE // 4, range(1), width(NTILE - 1))
        with nc.Block() as block:
            @block.sync
            def _(sp):
                def body(i, slots, w):
                    for s in slots:
                        wait(sp, sent[s], 16 * i, gsp)
                        sp.dma_start(xb[s][0:w, :], d.xn[bass.ds(i * 4 * P + s * P, w), :]).then_inc(lds[s], 16)
                fours(sp, body)

            @block.vector
            def _(dve):
                def body(i, slots, w):
                    for s in slots:
                        wait(dve, sent[s], 16 * i)
                        dve.tensor_copy(ix[s][:], k.slot_i[:, bass.ds(i * 4 + s, 1)]).then_inc(ixd, 1)
                fours(dve, body)

            @block.gpsimd
            def _(pool):
                def body(i, slots, w):
                    for s in slots:
                        wait(pool, ixd, 4 * i + s + 1, gpool)
                        wait(pool, lds[s], 16 * (i + 1), gpool)
                        pool.indirect_dma_start(d.xs, bass.IndirectOffsetOnAxis(ap=ix[s][0:w, :], axis=0), xb[s][0:w, :], None).then_inc(sent[s], 16)
                fours(pool, body)
                for s in range(4):
                    pool.wait_ge(sent[s], 16 * (NTILE // 4 + (s == 0)))


def stage_experts(nc, kit, a, d):
    k = kit
    PAIRS = SORTED // 2
    with Stage(nc, kit) as st:
        xt = [st.sb(f"xt{j}", [P, D]) for j in range(2)]
        w1 = [st.sb(f"w1_{j}", [P, C, HID]) for j in range(2)]
        w2 = [st.sb(f"w2_{j}", [HID, D]) for j in range(2)]
        b1 = [st.sb(f"b1_{j}", [1, HID]) for j in range(2)]
        b2 = [st.sb(f"b2_{j}", [1, D]) for j in range(2)]
        xT = [st.sb(f"xT{j}", [P, C, P]) for j in range(2)]
        hT = [st.sb(f"hT{j}", [HID, P]) for j in range(2)]
        y = [st.sb(f"y{j}", [P, D]) for j in range(2)]
        x_loaded = [st.sem(f"x_loaded{j}") for j in range(2)]
        w_loaded = [st.sem(f"w_loaded{j}") for j in range(2)]
        sent = [st.pool_dma(f"y_sent{j}") for j in range(2)]
        turned, xT_done, hid, h_done, out_psum, y_done = (st.sem(n) for n in "turned xT_done hid h_done out_psum y_done".split())
        gsp, gpool = st.sem("gsp"), st.sem("gpool")

        def pairs(eng, *steps):
            def at(p, i=None, j=0):
                for step, lag in steps:
                    if i is None:
                        if 0 <= p - lag < SORTED:
                            step(p - lag, (p - lag) // 2, (p - lag) % 2)
                    else:
                        step(i * 2 + (j - lag), i + (j - lag) // 2, (j - lag) % 2)
            for p in range(4):
                at(p)
            with eng.Fori(2, PAIRS) as i:
                at(0, i, 0)
                at(0, i, 1)
            at(SORTED)
            at(SORTED + 1)
        with nc.Block() as block:
            @block.sync
            def _(sp):
                def load(t, n, j):
                    wait(sp, turned, t - 1, gsp)
                    sp.dma_start(xt[j][:], d.xs[bass.ds(t * P, P), :]).then_inc(x_loaded[j], 16)
                    wait(sp, out_psum, t - 1, gsp)
                    e = sp.value_load(k.tile_expert[0:1, bass.ds(t, 1)], min_val=0, max_val=EXPERTS - 1)
                    sp.dma_start(w1[j][:], a["L0_ffn_W1"][bass.ds(e, 1), :, :].rearrange("a (c p) h -> p (a c) h", p=P)).then_inc(w_loaded[j], 16)
                    sp.dma_start(w2[j][:], a["L0_ffn_W2"][bass.ds(e, 1), :, :].rearrange("a h d -> h (a d)")).then_inc(w_loaded[j], 16)
                    sp.dma_start(b1[j][:], a["L0_ffn_b1"][bass.ds(e, 1), :]).then_inc(w_loaded[j], 16)
                    sp.dma_start(b2[j][:], a["L0_ffn_b2"][bass.ds(e, 1), :]).then_inc(w_loaded[j], 16)
                pairs(sp, (load, 0))

            @block.tensor
            def _(pe):
                def turn(t, n, j):
                    wait(pe, x_loaded[j], 16 * (n + 1))
                    wait(pe, xT_done, t - 1)
                    for c in range(C):
                        ins = pe.transpose(k.bank[j][:, c * P:(c + 1) * P], xt[j][:, c * P:(c + 1) * P], k.ident[:])
                    ins.then_inc(turned, 1)

                def hidden(t, n, j):
                    wait(pe, xT_done, t + 1)
                    wait(pe, w_loaded[j], 64 * (n + 1))
                    wait(pe, h_done, t - 1)
                    for c in range(C):
                        pe.matmul(k.bank[2 + j][0:HID, 0:P], w1[j][:, c, :], xT[j][:, c, :], start=(c == 0), stop=False)
                    pe.matmul(k.bank[2 + j][0:HID, 0:P], b1[j][:], k.ones[0:1, :], start=False, stop=True).then_inc(hid, 1)

                def output(t, n, j):
                    wait(pe, h_done, t + 1)
                    wait(pe, y_done, t - 1)
                    pe.matmul(k.bank[4 + j][:, 0:D], hT[j][:], w2[j][:], start=True, stop=False)
                    pe.matmul(k.bank[4 + j][:, 0:D], k.ones[0:1, :], b2[j][:], start=False, stop=True).then_inc(out_psum, 1)
                pairs(pe, (turn, 0), (output, 1), (hidden, 0))

            @block.vector
            def _(dve):
                def copy_xT(t, n, j):
                    wait(dve, turned, t + 1)
                    wait(dve, hid, t - 1)
                    dve.tensor_copy(xT[j][:], chunks(k.bank[j])).then_inc(xT_done, 1)
                pairs(dve, (copy_xT, 0))

            @block.scalar
            def _(act):
                def relu_h(t, n, j):
                    wait(act, hid, t + 1)
                    wait(act, out_psum, t - 1)
                    act.activation(hT[j][:], k.bank[2 + j][0:HID, 0:P], ACT.Relu).then_inc(h_done, 1)

                def relu_y(t, n, j):
                    wait(act, out_psum, t + 1)
                    wait(act, sent[j], 16 * n)
                    act.activation(y[j][:], k.bank[4 + j][:, 0:D], ACT.Relu).then_inc(y_done, 1)
                pairs(act, (relu_y, 1), (relu_h, 0))

            @block.gpsimd
            def _(pool):
                def send(t, n, j):
                    wait(pool, y_done, t + 1, gpool)
                    pool.dma_start(d.ys[bass.ds(t * P, P), :], y[j][:]).then_inc(sent[j], 16)
                pairs(pool, (send, 1))
                for j in range(2):
                    pool.wait_ge(sent[j], 16 * PAIRS)


def stage_second_front(nc, kit, a, d):
    k = kit
    with Stage(nc, kit) as st:
        xt = st.sb("xt", [P, 2, D])
        xnT = st.sb("xnT", [P, C, BODY])
        t = st.sb("t", [P, 2, D])
        kmax = st.sb("kmax", [P, C, FULL + 1])
        x1 = st.sb("x1", [P, 2, D])
        y = [st.sb(f"y{j}", [P, D]) for j in range(2)]
        gx = [st.sb(f"gx{j}", [P, 1], I32) for j in range(2)]
        loaded, x2_done, gx_done = st.sem("loaded"), st.sem("x2_done"), st.sem("gx_done")
        got = [st.pool_dma(f"got{j}") for j in range(2)]
        x2stored = st.pool_dma("x2stored")
        nm = Norm(st, "e", xt, x2_done)
        turned, xnT_done, t_psum, t_done, stored, xstored, key_psum, max_done = (st.sem(n) for n in "turned xnT_done t_psum t_done stored xstored key_psum max_done".split())
        gsp, gpool, gact, gdve = (st.sem(n) for n in "gsp gpool gact gdve".split())
        with nc.Block() as block:
            @block.sync
            def _(sp):
                def body(i, tiles):
                    wait(sp, x2_done, i, gsp)
                    sp.dma_start(x1[0:tiles[0], 0:len(tiles), :], rows(d.x1, i, tiles)).then_inc(loaded, 16)
                bodies(sp, body)

            @block.gpsimd
            def _(pool):
                def store(i, tiles):
                    w, n = tiles[0], len(tiles)
                    wait(pool, x2_done, i + 1, gpool)
                    pool.dma_start(rows(d.x2, i, tiles), xt[0:w, 0:n, :]).then_inc(x2stored, 16)
                    wait(pool, nm.xn_done, i + 1, gpool)
                    pool.dma_start(rows(d.xn, i, tiles), nm.xn[0:w, 0:n, :]).then_inc(xstored, 16)
                    wait(pool, t_done, i + 1, gpool)
                    pool.dma_start(rows(d.t1, i, tiles), t[0:w, 0:n, :]).then_inc(stored, 16)

                def body(i, tiles):
                    wait(pool, gx_done, i + 1, gpool)
                    for j, w in enumerate(tiles):
                        pool.indirect_dma_start(y[j][0:w, :], None, d.ys, bass.IndirectOffsetOnAxis(ap=gx[j][0:w, :], axis=0)).then_inc(got[j], 16)
                    if not (isinstance(i, int) and i == 0):
                        store(i - 1, (P, P))
                bodies(pool, body)
                store(FULL, (LAST,))
                pool.wait_ge(x2stored, 16 * (FULL + 1))
                pool.wait_ge(stored, 16 * (FULL + 1))
                pool.wait_ge(xstored, 16 * (FULL + 1))

            @block.scalar
            def _(act):
                def body(i, tiles):
                    wt = sum(tiles)
                    nm.act_sd(act, i, tiles)
                    wait(act, turned, i + 1)
                    wait(act, key_psum, i)
                    act.activation(xnT[:, :, 0:wt], halves(k.bank[0][:])[:, :, 0:wt], ACT.Copy).then_inc(xnT_done, 1)
                    wait(act, t_psum, i + 1)
                    wait(act, stored, 16 * i, gact)
                    for j, w in enumerate(tiles):
                        ins = act.activation(t[0:w, j, :], k.bank[1 + j][0:w, 0:D], ACT.Copy, scale=k.wdeg[0:w, bass.ds(i * 2 + j, 1)])
                    ins.then_inc(t_done, 1)
                bodies(act, body)

            @block.vector
            def _(dve):
                for j in range(2):
                    ins = dve.tensor_copy(gx[j][:], k.slot_i[:, j:j + 1])
                ins.then_inc(gx_done, 1)

                def body(i, tiles):
                    wt = sum(tiles)
                    wait(dve, loaded, 16 * (i + 1))
                    wait(dve, x2stored, 16 * i)
                    wait(dve, nm.xn_done, i)
                    for j, w in enumerate(tiles):
                        wait(dve, got[j], 16 * (i + 1))
                        ins = dve.tensor_tensor(xt[0:w, j, :], x1[0:w, j, :], y[j][0:w, :], ALU.add)
                    ins.then_inc(x2_done, 1)
                    if len(tiles) == 2:
                        wait(dve, x2_done, i + 1)
                        for j in range(2):
                            ins = dve.tensor_copy(gx[j][:], k.slot_i[:, bass.ds(i * 2 + 2 + j, 1)])
                        ins.then_inc(gx_done, 1)
                    nm.dve_moments(dve, i, tiles)
                    nm.dve_normalise(dve, i, tiles, [(turned, 1), (xstored, 16)])
                    wait(dve, key_psum, i + 1, gdve)
                    for c in range(C):
                        ins = dve.tensor_reduce(kmax[:, c, bass.ds(i, 1)], k.bank[3 + c][:, 0:wt], AX.X, ALU.max)
                    ins.then_inc(max_done, 1)
                bodies(dve, body)

            @block.tensor
            def _(pe):
                def body(i, tiles):
                    wt = sum(tiles)
                    wait(pe, nm.xn_done, i + 1)
                    wait(pe, xnT_done, i)
                    pe_turn(k, pe, k.bank[0], nm.xn, tiles, turned)
                    wait(pe, xnT_done, i + 1)
                    wait(pe, t_done, i)
                    for j, w in enumerate(tiles):
                        for c in range(C):
                            ins = pe.matmul(k.bank[1 + j][0:w, 0:D], xnT[:, c, j * P:j * P + w], k.wg1[:, c, :], start=(c == 0), stop=(c == C - 1))
                    ins.then_inc(t_psum, 1)
                    wait(pe, max_done, i)
                    for o in range(C):
                        for c in range(C):
                            ins = pe.matmul(k.bank[3 + o][:, 0:wt], k.wkv1[:, c, o * P:(o + 1) * P], xnT[:, c, 0:wt], start=(c == 0), stop=(c == C - 1))
                    ins.then_inc(key_psum, 1)
                bodies(pe, body)
        mx = st.sb("mx", [P, C])
        mb = st.sb("mb", [P, C, P])
        s1, s2 = st.sem("s1"), st.sem("s2")
        with nc.Block() as block:
            @block.vector
            def _(dve):
                dve.tensor_reduce(mx[:], kmax[:], AX.X, ALU.max).then_inc(s1, 1)
                dve.wait_ge(s1, 1)
                dve.tensor_tensor(mx[:], mx[:], k.bk1c[:], ALU.add).then_inc(s1, 1)
                dve.wait_ge(s1, 2)
                for c in range(C):
                    ins = dve.tensor_scalar(mb[:, c, :], k.ones[:], mx[:, c:c + 1], None, ALU.mult)
                ins.then_inc(s1, 1)
                dve.wait_ge(s2, 1)
                dve.tensor_tensor(k.bkv1[:, 0:D], k.bk1row[:], k.bank[0][:, 0:D], ALU.subtract).then_inc(s1, 1)

            @block.tensor
            def _(pe):
                pe.wait_ge(s1, 3)
                for c in range(C):
                    ins = pe.matmul(k.bank[0][:, c * P:(c + 1) * P], mb[:, c, :], k.ident[:], start=True, stop=True)
                ins.then_inc(s2, 1)


def stage_lambda(nc, kit, a, d):
    k = kit
    with Stage(nc, kit) as st:
        lam = st.sb("lam", [P, C, D])
        rs = st.sb("rsum", [P, C])
        stl = st.sb("stl", [P, C, 6])
        mv = st.sb("mvl", [P, C, 2])
        sd = st.sb("sdl", [P, C])
        sc = st.sb("scl", [P, C])
        sh = st.sb("shl", [P, C])
        qb = st.sb("qb", [P, C, P])
        s1, s2, s3 = st.sem("s1"), st.sem("s2"), st.sem("s3")
        with nc.Block() as block:
            @block.vector
            def _(dve):
                n = [0]

                def then(ins):
                    n[0] += 1
                    ins.then_inc(s1, 1)
                    dve.wait_ge(s1, n[0])
                for c in range(C):
                    then(dve.reciprocal(rs[:, c:c + 1], k.bank[4 + c][:, D:D + 1]))
                    then(dve.tensor_scalar(lam[:, c, :], k.bank[4 + c][:, 0:D], rs[:, c:c + 1], None, ALU.mult))
                    then(dve.bn_stats(stl[:, c, :], lam[:, c, :]))
                    then(dve.bn_aggr(mv[:, c, :], stl[:, c, :]))
                dve.wait_ge(s2, 1)
                then(dve.reciprocal(sd[:], sd[:]))
                then(dve.tensor_tensor(sc[:], sd[:], k.gmc[:], ALU.mult))
                then(dve.tensor_tensor(sd[:], mv[:, :, 0], sc[:], ALU.mult))
                then(dve.tensor_tensor(sh[:], k.bemc[:], sd[:], ALU.subtract))
                for c in range(C):
                    then(dve.tensor_scalar(lam[:, c, :], lam[:, c, :], sc[:, c:c + 1], sh[:, c:c + 1], ALU.mult, ALU.add))
                    then(dve.tensor_scalar(qb[:, c, :], k.ones[:], k.bq1c[:, c:c + 1], None, ALU.mult))
                dve.wait_ge(s3, 1)
                for c in range(C):
                    dve.tensor_copy(k.mq[:, c, :], k.bank[c][:, 0:D])
                then(dve.tensor_copy(k.bmq[:], k.bank[2][:, 0:D]))

            @block.scalar
            def _(act):
                act.wait_ge(s1, 8)
                act.activation(sd[:], mv[:, :, 1], ACT.Sqrt, bias=k.eps[:]).then_inc(s2, 1)

            @block.tensor
            def _(pe):
                pe.wait_ge(s1, 16)
                for o in range(C):
                    for c in range(C):
                        pe.matmul(k.bank[o][:, 0:D], k.wq1T[:, c, o * P:(o + 1) * P], lam[:, c, :], start=(c == 0), stop=(c == C - 1))
                for c in range(C):
                    ins = pe.matmul(k.bank[2][:, 0:D], qb[:, c, :], lam[:, c, :], start=(c == 0), stop=(c == C - 1))
                ins.then_inc(s3, 1)


class Convolved:

    def __init__(self, st, d, table, bias):
        self.table, self.bias, self.d, self.kit = table, bias, d, st.kit
        self.at = st.sb("cat", [P, 2, D])
        self.tt = st.sb("ctt", [P, 2, D])
        self.h = st.sb("ch", [P, 2, D])
        self.loaded, self.added, self.scaled, self.h_done = (st.sem(n) for n in ("c_loaded", "c_added", "c_scaled", "c_h_done"))

    def sp_load(self, sp, i, tiles, gate):
        w, n = tiles[0], len(tiles)
        wait(sp, self.added, i, gate)
        sp.dma_start(self.at[0:w, 0:n, :], rows(self.d.acc[:, 0:D], i, tiles)).then_inc(self.loaded, 16)
        sp.dma_start(self.tt[0:w, 0:n, :], rows(self.table, i, tiles)).then_inc(self.loaded, 16)

    def dve(self, dve, i, tiles, used):
        w, n = tiles[0], len(tiles)
        wait(dve, self.loaded, 32 * (i + 1))
        for sem, step in used:
            wait(dve, sem, i * step)
        dve.tensor_tensor(self.h[0:w, 0:n, :], self.at[0:w, 0:n, :], self.tt[0:w, 0:n, :], ALU.add).then_inc(self.added, 1)
        wait(dve, self.added, i + 1)
        for j, wj in enumerate(tiles):
            ins = dve.scalar_tensor_tensor(out=self.h[0:wj, j, :], in0=self.h[0:wj, j, :], scalar=self.kit.wdeg[0:wj, bass.ds(i * 2 + j, 1)],
                                           in1=self.bias[0:wj, :], op0=ALU.mult, op1=ALU.add)
        ins.then_inc(self.scaled, 1)

    def act(self, act, i, tiles):
        w, n = tiles[0], len(tiles)
        wait(act, self.scaled, i + 1)
        act.activation(self.h[0:w, 0:n, :], self.h[0:w, 0:n, :], ACT.Relu).then_inc(self.h_done, 1)


def stage_conv_between(nc, kit, a, d):
    k = kit
    with Stage(nc, kit) as st:
        cv = Convolved(st, d, d.t1, k.bg1)
        hT = st.sb("hT", [P, C, BODY])
        t = st.sb("t", [P, 2, D])
        turned, hT_done, t_psum, t_done, stored, gsp, gpool, gact = (st.sem(n) for n in "turned hT_done t_psum t_done stored gsp gpool gact".split())
        with nc.Block() as block:
            @block.sync
            def _(sp):
                bodies(sp, lambda i, tiles: cv.sp_load(sp, i, tiles, gsp))

            @block.gpsimd
            def _(pool):
                def body(i, tiles):
                    wait(pool, t_done, i + 1, gpool)
                    pool.dma_start(rows(d.t2, i, tiles), t[0:tiles[0], 0:len(tiles), :]).then_inc(stored, 16)
                bodies(pool, body)
                pool.wait_ge(stored, 16 * (FULL + 1))

            @block.vector
            def _(dve):
                bodies(dve, lambda i, tiles: cv.dve(dve, i, tiles, [(turned, 1)]))

            @block.scalar
            def _(act):
                def body(i, tiles):
                    cv.act(act, i, tiles)
                    wt = sum(tiles)
                    wait(act, turned, i + 1)
                    wait(act, t_psum, i)
                    act.activation(hT[:, :, 0:wt], halves(k.bank[0][:])[:, :, 0:wt], ACT.Copy).then_inc(hT_done, 1)
                    wait(act, t_psum, i + 1)
                    wait(act, stored, 16 * i, gact)
                    for j, w in enumerate(tiles):
                        ins = act.activation(t[0:w, j, :], k.bank[1 + j][0:w, 0:D], ACT.Copy, scale=k.wdeg[0:w, bass.ds(i * 2 + j, 1)])
                    ins.then_inc(t_done, 1)
                bodies(act, body)

            @block.tensor
            def _(pe):
                def body(i, tiles):
                    wait(pe, cv.h_done, i + 1)
                    wait(pe, hT_done, i)
                    pe_turn(k, pe, k.bank[0], cv.h, tiles, turned)
                    wait(pe, hT_done, i + 1)
                    wait(pe, t_done, i)
                    for j, w in enumerate(tiles):
                        for c in range(C):
                            ins = pe.matmul(k.bank[1 + j][0:w, 0:D], hT[:, c, j * P:j * P + w], k.wg2[:, c, :], start=(c == 0), stop=(c == C - 1))
                    ins.then_inc(t_psum, 1)
                bodies(pe, body)


def stage_layer_end(nc, kit, a, d):
    k = kit
    with Stage(nc, kit) as st:
        cv = Convolved(st, d, d.t2, k.bg2)
        xt = st.sb("xt", [P, 2, D])
        x3 = st.sb("x3", [P, 2, D])
        loaded, x3_done, stored, gsp, gpool = (st.sem(n) for n in "loaded x3_done stored gsp gpool".split())
        with nc.Block() as block:
            @block.sync
            def _(sp):
                def body(i, tiles):
                    cv.sp_load(sp, i, tiles, gsp)
                    wait(sp, x3_done, i, gsp)
                    sp.dma_start(xt[0:tiles[0], 0:len(tiles), :], rows(d.xm, i, tiles)).then_inc(loaded, 16)
                bodies(sp, body)

            @block.gpsimd
            def _(pool):
                def body(i, tiles):
                    wait(pool, x3_done, i + 1, gpool)
                    pool.dma_start(rows(d.x3, i, tiles), x3[0:tiles[0], 0:len(tiles), :]).then_inc(stored, 16)
                bodies(pool, body)
                pool.wait_ge(stored, 16 * (FULL + 1))

            @block.vector
            def _(dve):
                def body(i, tiles):
                    w, n = tiles[0], len(tiles)
                    cv.dve(dve, i, tiles, [(x3_done, 1)])
                    wait(dve, stored, 16 * i)
                    wait(dve, loaded, 16 * (i + 1))
                    wait(dve, cv.h_done, i + 1)
                    dve.tensor_tensor(x3[0:w, 0:n, :], xt[0:w, 0:n, :], cv.h[0:w, 0:n, :], ALU.add).then_inc(x3_done, 1)
                bodies(dve, body)

            @block.scalar
            def _(act):
                def body(i, tiles):
                    cv.act(act, i, tiles)
                bodies(act, body)


def stage_slices(nc, kit, a, d):
    k = kit
    HS = HEADS * SLICES
    with Stage(nc, kit) as st:
        xt = st.sb("xt", [P, 2, D])
        xnT = st.sb("xnT", [P, C, BODY])
        lg = st.sb("lg", [P, 2, HS])
        mx = st.sb("mxs", [P, 2, HEADS])
        loaded = st.sem("loaded")
        nm = Norm(st, "s", xt, loaded, 16)
        (turned, xnT_done, lg_psum, lg_done, mx_done, sub_done, e_done, sum_done, rec_done, sw_done, acc_done, stored) = (
            st.sem(n) for n in "turned xnT_done lg_psum lg_done mx_done sub_done e_done sum_done rec_done sw_done acc_done stored".split())
        gsp, gpool = st.sem("gsp"), st.sem("gpool")

        def heads(t, j, w):
            return t[0:w, j, :].rearrange("p (h g) -> p h g", g=SLICES)

        def over(t, j, w):
            return t[0:w, j, :].rearrange("p (h a) -> p h a", a=1).to_broadcast([w, HEADS, SLICES])
        with nc.Block() as block:
            @block.sync
            def _(sp):
                def body(i, tiles):
                    wait(sp, nm.xn_done, i, gsp)
                    sp.dma_start(xt[0:tiles[0], 0:len(tiles), :], rows(d.x3, i, tiles)).then_inc(loaded, 16)
                bodies(sp, body)

            @block.gpsimd
            def _(pool):
                def body(i, tiles):
                    wait(pool, sw_done, i + 1, gpool)
                    pool.dma_start(rows(d.sw, i, tiles), lg[0:tiles[0], 0:len(tiles), :]).then_inc(stored, 16)
                bodies(pool, body)
                pool.wait_ge(stored, 16 * (FULL + 1))

            @block.vector
            def _(dve):
                def body(i, tiles):
                    nm.dve_moments(dve, i, tiles)
                    nm.dve_normalise(dve, i, tiles, [(acc_done, 1)])
                    wait(dve, lg_psum, i + 1)
                    wait(dve, stored, 16 * i)
                    for j, w in enumerate(tiles):
                        ins = dve.tensor_tensor(lg[0:w, j, :], k.bank[1 + j][0:w, :], k.bxs[0:w, :], ALU.add)
                    ins.then_inc(lg_done, 1)
                    wait(dve, lg_done, i + 1)
                    for j, w in enumerate(tiles):
                        ins = dve.tensor_reduce(mx[0:w, j, :], heads(lg, j, w), AX.X, ALU.max)
                    ins.then_inc(mx_done, 1)
                    wait(dve, mx_done, i + 1)
                    for j, w in enumerate(tiles):
                        ins = dve.tensor_tensor(heads(lg, j, w), heads(lg, j, w), over(mx, j, w), ALU.subtract)
                    ins.then_inc(sub_done, 1)
                    wait(dve, e_done, i + 1)
                    for j, w in enumerate(tiles):
                        ins = dve.tensor_reduce(mx[0:w, j, :], heads(lg, j, w), AX.X, ALU.add)
                    ins.then_inc(sum_done, 1)
                    wait(dve, sum_done, i + 1)
                    w, n = tiles[0], len(tiles)
                    dve.reciprocal(mx[0:w, 0:n, :], mx[0:w, 0:n, :]).then_inc(rec_done, 1)
                    wait(dve, rec_done, i + 1)
                    for j, w in enumerate(tiles):
                        ins = dve.tensor_tensor(heads(lg, j, w), heads(lg, j, w), over(mx, j, w), ALU.mult)
                    ins.then_inc(sw_done, 1)
                bodies(dve, body)

            @block.scalar
            def _(act):
                def body(i, tiles):
                    w, n, wt = tiles[0], len(tiles), sum(tiles)
                    nm.act_sd(act, i, tiles)
                    wait(act, turned, i + 1)
                    wait(act, lg_psum, i)
                    act.activation(xnT[:, :, 0:wt], halves(k.bank[0][:])[:, :, 0:wt], ACT.Copy).then_inc(xnT_done, 1)
                    wait(act, sub_done, i + 1)
                    act.activation(lg[0:w, 0:n, :], lg[0:w, 0:n, :], ACT.Exp).then_inc(e_done, 1)
                bodies(act, body)

            @block.tensor
            def _(pe):
                def body(i, tiles):
                    wait(pe, nm.xn_done, i + 1)
                    wait(pe, xnT_done, i)
                    pe_turn(k, pe, k.bank[0], nm.xn, tiles, turned)
                    wait(pe, xnT_done, i + 1)
                    wait(pe, lg_done, i)
                    for j, w in enumerate(tiles):
                        for c in range(C):
                            ins = pe.matmul(k.bank[1 + j][0:w, :], xnT[:, c, j * P:j * P + w], k.wxs[:, c, :], start=(c == 0), stop=(c == C - 1))
                    ins.then_inc(lg_psum, 1)
                    wait(pe, sw_done, i + 1)
                    first, last = isinstance(i, int) and i == 0, isinstance(i, int) and i == FULL
                    for j, w in enumerate(tiles):
                        for c in range(C):
                            pe.matmul(k.bank[3 + c][:, :], nm.xn[0:w, j, c * P:(c + 1) * P], lg[0:w, j, :], start=first and j == 0, stop=last)
                        ins = pe.matmul(k.bank[5][0:1, :], k.ones[0:w, 0:1], lg[0:w, j, :], start=first and j == 0, stop=last)
                    ins.then_inc(acc_done, 1)
                bodies(pe, body)
        T = st.sb("T", [P, C, HS])
        norm = st.sb("norm", [1, HS])
        rn = st.sb("rn", [SLICES, 1])
        tok, tokT, qT, kT, vv, at, atT, oT = (st.sb(n, [SLICES, SDIM]) for n in "tok tokT qT kT vv at atT oT".split())
        mo = st.sb("mo", [SLICES, D])
        sm = st.sb("sm", [SLICES, 4])
        vs, ps, as_, ds = st.sem("vs"), st.sem("ps"), st.sem("as_"), st.sem("ds")
        b = k.bank
        with nc.Block() as block:
            @block.vector
            def _(dve):
                n, p = [0], [0]

                def then(ins):
                    n[0] += 1
                    ins.then_inc(vs, 1)
                    dve.wait_ge(vs, n[0])

                def psum():
                    p[0] += 1
                    dve.wait_ge(ps, p[0])
                for c in range(C):
                    then(dve.tensor_copy(T[:, c, :], b[3 + c][:, :]))
                then(dve.tensor_copy(norm[:], b[5][0:1, :]))
                for h in range(HEADS):
                    psum()
                    then(dve.tensor_scalar(rn[:], b[1][0:SLICES, 0:1], 1e-5, None, ALU.add))
                    then(dve.reciprocal(rn[:], rn[:]))
                    then(dve.tensor_scalar(tok[:], b[0][0:SLICES, 0:SDIM], rn[:], None, ALU.mult))
                    psum()
                    then(dve.tensor_copy(tokT[:], b[0][0:SDIM, 0:SLICES]))
                    psum()
                    dve.tensor_copy(qT[:], b[0][0:SDIM, 0:SLICES])
                    dve.tensor_copy(kT[:], b[1][0:SDIM, 0:SLICES])
                    then(dve.tensor_copy(vv[:], b[2][0:SLICES, 0:SDIM]))
                    psum()
                    then(dve.tensor_reduce(sm[:, 0:1], b[0][0:SLICES, 0:SLICES], AX.X, ALU.max))
                    then(dve.tensor_scalar(sm[:, 1:2], sm[:, 0:1], -SDIM ** -0.5, None, ALU.mult))
                    dve.wait_ge(as_, h + 1)
                    then(dve.reciprocal(sm[:, 3:4], sm[:, 2:3]))
                    then(dve.tensor_scalar(at[:], at[:], sm[:, 3:4], None, ALU.mult))
                    psum()
                    then(dve.tensor_copy(atT[:], b[1][0:SLICES, 0:SLICES]))
                    psum()
                    then(dve.tensor_copy(oT[:], b[2][0:SDIM, 0:SLICES]))
                    psum()
                    if h:
                        dve.wait_ge(ds, 16 * h)
                    then(dve.tensor_copy(mo[:], b[0][0:SLICES, 0:D]))

            @block.scalar
            def _(act):
                for h in range(HEADS):
                    act.wait_ge(vs, 3 + 12 * h + 7)
                    act.activation(at[:], b[0][0:SLICES, 0:SLICES], ACT.Exp, bias=sm[:, 1:2], scale=SDIM ** -0.5,
                                   accum_out=sm[:, 2:3]).then_inc(as_, 1)

            @block.sync
            def _(sp):
                for h in range(HEADS):
                    sp.wait_ge(vs, 3 + 12 * (h + 1))
                    sp.dma_start(k.mout[(h % 2) * SLICES:(h % 2 + 1) * SLICES, h // 2, :], mo[:]).then_inc(ds, 16)
                sp.wait_ge(ds, 16 * HEADS)

            @block.tensor
            def _(pe):
                for h in range(HEADS):
                    hs = slice(h * SLICES, (h + 1) * SLICES)
                    o = 3 + 12 * h
                    pe.wait_ge(vs, o)
                    for c in range(C):
                        pe.matmul(b[0][0:SLICES, 0:SDIM], T[:, c, hs], k.wfx[:, c, hs], start=(c == 0), stop=False)
                    pe.matmul(b[0][0:SLICES, 0:SDIM], norm[:, hs], k.bfx[:, hs], start=False, stop=True)
                    pe.matmul(b[1][0:SLICES, 0:1], norm[:, hs], k.ones[0:1, 0:1], start=True, stop=True).then_inc(ps, 1)
                    pe.wait_ge(vs, o + 3)
                    pe.transpose(b[0][0:SDIM, 0:SLICES], tok[:], k.ident[0:SLICES, 0:SLICES]).then_inc(ps, 1)
                    pe.wait_ge(vs, o + 4)
                    pe.matmul(b[0][0:SDIM, 0:SLICES], k.wsq[:], tokT[:], start=True, stop=True)
                    pe.matmul(b[1][0:SDIM, 0:SLICES], k.wsk[:], tokT[:], start=True, stop=True)
                    pe.matmul(b[2][0:SLICES, 0:SDIM], tokT[:], k.wsv[:], start=True, stop=True).then_inc(ps, 1)
                    pe.wait_ge(vs, o + 5)
                    pe.matmul(b[0][0:SLICES, 0:SLICES], qT[:], kT[:], start=True, stop=True).then_inc(ps, 1)
                    pe.wait_ge(vs, o + 9)
                    pe.transpose(b[1][0:SLICES, 0:SLICES], at[:], k.ident[0:SLICES, 0:SLICES]).then_inc(ps, 1)
                    pe.wait_ge(vs, o + 10)
                    pe.matmul(b[2][0:SDIM, 0:SLICES], vv[:], atT[:], start=True, stop=True).then_inc(ps, 1)
                    pe.wait_ge(vs, o + 11)
                    pe.matmul(b[0][0:SLICES, 0:D], oT[:], k.wout[:, h, :], start=True, stop=True).then_inc(ps, 1)


def stage_out(nc, kit, a, d, out):
    k = kit
    HS = HEADS * SLICES
    NC4 = HS // P
    with Stage(nc, kit) as st:
        sw = st.sb("sw", [P, 2, HS])
        xt = st.sb("xt", [P, 2, D])
        swT = st.sb("swT", [P, 2, NC4, P])
        y = st.sb("y", [P, 2, D])
        loaded, turned, swT_done, y_psum, a_done, y_done, stored, gsp, gpool = (st.sem(n) for n in "loaded turned swT_done y_psum a_done y_done stored gsp gpool".split())
        with nc.Block() as block:
            @block.sync
            def _(sp):
                def body(i, tiles):
                    w, n = tiles[0], len(tiles)
                    wait(sp, y_done, i, gsp)
                    sp.dma_start(sw[0:w, 0:n, :], rows(d.sw, i, tiles)).then_inc(loaded, 16)
                    sp.dma_start(xt[0:w, 0:n, :], rows(d.x3, i, tiles)).then_inc(loaded, 16)
                bodies(sp, body)

            @block.gpsimd
            def _(pool):
                def body(i, tiles):
                    wait(pool, y_done, i + 1, gpool)
                    pool.dma_start(rows(out, i, tiles), y[0:tiles[0], 0:len(tiles), :]).then_inc(stored, 16)
                bodies(pool, body)
                pool.wait_ge(stored, 16 * (FULL + 1))

            @block.scalar
            def _(act):
                def body(i, tiles):
                    wait(act, turned, i + 1)
                    wait(act, y_psum, i)
                    for j, w in enumerate(tiles):
                        ins = act.activation(swT[:, j, :, 0:w], k.bank[j][:].rearrange("p (c n) -> p c n", c=NC4)[:, :, 0:w], ACT.Copy)
                    ins.then_inc(swT_done, 1)
                bodies(act, body)

            @block.vector
            def _(dve):
                def body(i, tiles):
                    w, n = tiles[0], len(tiles)
                    wait(dve, y_psum, i + 1)
                    wait(dve, stored, 16 * i)
                    for j, wj in enumerate(tiles):
                        ins = dve.tensor_tensor(y[0:wj, j, :], k.bank[2 + j][0:wj, 0:D], k.bout[0:wj, :], ALU.add)
                    ins.then_inc(a_done, 1)
                    wait(dve, a_done, i + 1)
                    dve.tensor_tensor(y[0:w, 0:n, :], y[0:w, 0:n, :], xt[0:w, 0:n, :], ALU.add).then_inc(y_done, 1)
                bodies(dve, body)

            @block.tensor
            def _(pe):
                def body(i, tiles):
                    wait(pe, loaded, 32 * (i + 1))
                    wait(pe, swT_done, i)
                    for j, w in enumerate(tiles):
                        for c in range(NC4):
                            ins = pe.transpose(k.bank[j][:, c * P:c * P + w], sw[0:w, j, c * P:(c + 1) * P], k.ident[0:w, 0:w])
                    ins.then_inc(turned, 1)
                    wait(pe, swT_done, i + 1)
                    wait(pe, a_done, i)
                    for j, w in enumerate(tiles):
                        for c in range(NC4):
                            ins = pe.matmul(k.bank[2 + j][0:w, 0:D], swT[:, j, c, 0:w], k.mout[:, c, :], start=(c == 0), stop=(c == NC4 - 1))
                    ins.then_inc(y_psum, 1)
                bodies(pe, body)


def build(nc, a, out):
    HS = HEADS * SLICES
    with ExitStack() as ctx:
        k, d = Kit(), Kit()
        k.ctx, k.stages = ctx, 0

        def sb(name, shape, dt=F32):
            return ctx.enter_context(nc.sbuf_tensor(name, shape, dt))

        def dram(name, shape, dt=F32):
            return nc.dram_tensor("d_" + name, shape, dt).ap()
        k.bank = [ctx.enter_context(nc.psum_tensor(f"bank{b}", [P, 512], F32)) for b in range(8)]
        d.xn = dram("xn", [N, D])
        d.xm = dram("xm", [N, D])
        d.xs = dram("xs", [SORTED * P, D])
        d.ys = dram("ys", [SORTED * P, D])
        d.x1 = dram("x1", [N, D])
        d.t1 = dram("t1", [N, D])
        d.t2 = dram("t2", [N, D])
        d.x2 = dram("x2", [N, D])
        d.x3 = dram("x3", [N, D])
        d.dst = dram("dst", [NG * GE], I32)
        d.sw = dram("sw", [N, HS], F32)
        d.acc = dram("acc", [NTILE * P, AW], F32)
        k.ident = sb("ident", [P, P])
        k.tri = sb("tri", [P, P])
        k.hmask = sb("hmask", [P, P])
        k.ones = sb("ones", [P, P])
        k.iota_i = sb("iota_i", [P, P], I32)
        k.iota = sb("iota", [P, P])
        k.eps = sb("eps", [P, 1])
        k.zeros = sb("zeros", [P, 7 * AW])
        k.wq0 = sb("wq0", [P, C, D])
        k.wo0 = sb("wo0", [P, C, D])
        k.wg1 = sb("wg1", [P, C, D])
        k.wg2 = sb("wg2", [P, C, D])
        k.w1T = sb("w1T", [P, C, D])
        k.w2T = sb("w2T", [P, C, D])
        k.wq1T = sb("wq1T", [P, C, D])
        k.m0 = sb("m0", [P, C, D])
        k.mq = sb("mq", [P, C, D])
        k.wkv0 = sb("wkv0", [P, C, 2 * D])
        k.wkv1 = sb("wkv1", [P, C, 2 * D])
        k.wfx = sb("wfx", [P, C, 2 * D])
        k.wxs = sb("wxs", [P, C, 2 * D])
        k.rT = sb("rT", [P, C, EXPERTS])
        k.rb2 = sb("rb2", [P, 2, EXPERTS])
        k.pos = sb("pos", [P, NTILE + 1])
        k.slot_f = sb("slot_f", [P, NTILE + 1])
        k.slot_i = sb("slot_i", [P, NTILE + 1], I32)
        k.tile_expert = sb("tile_expert", [1, SORTED], I32)
        k.upper = sb("upper", [P, P])
        k.wout = sb("wout", [SDIM, HEADS, D])
        k.wslice = sb("wslice", [SDIM, SDIM])
        k.wsq = sb("wsq", [SDIM, SDIM])
        k.wsk = sb("wsk", [SDIM, SDIM])
        k.wsv = sb("wsv", [SDIM, SDIM])
        k.bkv0 = sb("bkv0", [P, 2 * D])
        k.bkv1 = sb("bkv1", [P, 2 * D])
        k.bxs = sb("bxs", [P, 2 * D])
        k.bk1row = sb("bk1row", [P, D])
        k.bg1 = sb("bg1", [P, D])
        k.bg2 = sb("bg2", [P, D])
        k.bout = sb("bout", [P, D])
        k.bmq = sb("bmq", [P, D])
        k.bfx = sb("bfx", [1, HS])
        k.bslice_row = sb("bslice_row", [P, SLICES])
        k.temp = sb("temp", [P, HEADS])
        k.rtemp = sb("rtemp", [P, HEADS])
        k.epsw = sb("epsw", [P, 1])
        k.g1c = sb("g1c", [P, C])
        k.be1c = sb("be1c", [P, C])
        k.ghc = sb("ghc", [P, C])
        k.behc = sb("behc", [P, C])
        k.bqc = sb("bqc", [P, C])
        k.boc = sb("boc", [P, C])
        k.gmc = sb("gmc", [P, C])
        k.bemc = sb("bemc", [P, C])
        k.bq1c = sb("bq1c", [P, C])
        k.bk1c = sb("bk1c", [P, C])
        k.s1 = sb("s1", [P, C])
        k.t1 = sb("t1", [P, C])
        k.s2 = sb("s2", [P, C])
        k.t2 = sb("t2", [P, C])
        k.ks = sb("ks", [P, C, P])
        k.mout = sb("mout", [P, HS // P, D])
        k.wdeg = sb("wdeg", [P, NTILE + 1])
        k.flag = sb("flag", [1, 1], I32)
        k.dst_f = sb("dst_f", [P, NET])
        k.rank_f = sb("rank_f", [P, NET])
        k.ew_f = sb("ew_f", [P, NET])
        k.fd_f = sb("fd_f", [P, NET])
        k.src_i = sb("src_i", [P, NET], I32)
        k.dst_i = sb("dst_i", [P, NET], I32)
        k.ext = sb("ext", [P, NET, 3])
        stage_setup(nc, k, a, d)
        stage_front(nc, k, a, d)
        stage_aggregate(nc, k, a, d, d.xn, LinearAttention)
        with ExitStack() as middle:
            k.zT = middle.enter_context(nc.sbuf_tensor("zT", [P, C, N], F32))
            k.nbc = middle.enter_context(nc.sbuf_tensor("nbc", [P, N], F32))
            stage_gnn_first(nc, k, a, d)
            stage_gnn_second(nc, k, a, d)
            stage_combine(nc, k, a, d)
        stage_route(nc, k, a, d)
        stage_experts(nc, k, a, d)
        stage_second_front(nc, k, a, d)
        stage_aggregate(nc, k, a, d, d.t1, KeySums)
        stage_lambda(nc, k, a, d)
        stage_conv_between(nc, k, a, d)
        stage_aggregate(nc, k, a, d, d.t2, QueryMix)
        stage_layer_end(nc, k, a, d)
        stage_slices(nc, k, a, d)
        stage_out(nc, k, a, d, out)


def kernel(**inputs):
    import numpy as np
    import concourse.bacc as bacc
    from concourse.bass_utils import run_bass_kernel_spmd

    nc = bacc.Bacc("TRN2", target_bir_lowering=False, num_devices=1)
    arrays, args = {}, {}
    for name, x in inputs.items():
        x = np.ascontiguousarray(x)
        arrays[f"in_{name}"] = x
        args[name] = nc.dram_tensor(f"in_{name}", x.shape, mybir.dt.from_np(x.dtype), kind="ExternalInput").ap()
    out = nc.dram_tensor("out_0", (N, D), F32, kind="ExternalOutput").ap()
    build(nc, args, out)
    return run_bass_kernel_spmd(nc, [arrays], core_ids=[0]).results[0]["out_0"]
```

```python
from contextlib import ExitStack

import concourse.bass as bass
from concourse import mybir

F32 = mybir.dt.float32
I32 = mybir.dt.int32
ALU = mybir.AluOpType
ACT = mybir.ActivationFunctionType
AX = mybir.AxisListType

N, E, D = 6250, 100000, 256
P = 128
C = D // P
BODY = 2 * P
FULL = N // BODY
LAST = N - FULL * BODY
NTILE = 2 * FULL + 1
GT = 8
GE = GT * P
NG = -(-E // GE)
NET = NG * GT
AW = D + 3
FAR = 65536.0
HEADS, EXPERTS, HID = 8, 32, 64
SLICES, SDIM = 64, 64
SORTED = (N + EXPERTS * (P - 1)) // P
LN_EPS = 1e-5
POOL_DMA = ("stored", "xstored", "scattered")


def wait(eng, sem, value, gate=None):
    if isinstance(value, int):
        if value > 0:
            eng.wait_ge(sem, value)
        return
    eng.wait_ge(sem, value)
    if gate is not None:
        eng.sem_inc(gate, 1)


def bodies(eng, body):
    body(0, (P, P))
    with eng.Fori(1, FULL) as i:
        body(i, (P, P))
    body(FULL, (LAST,))


def rows(ap, i, tiles, width=None):
    if len(tiles) == 2:
        return ap[bass.ds(i * BODY, BODY), :].rearrange("(j p) d -> p j d", p=P)
    return ap[FULL * BODY:N, :].rearrange("(j p) d -> p j d", j=1)


def bcast_rows(ap, n):
    return bass.AP(tensor=ap.tensor, offset=ap.offset, ap=[[0, P], [1, n]])


class Kit:
    pass


class Stage:

    def __init__(self, nc, kit):
        self.nc, self.kit, self.ctx, self.sems = nc, kit, ExitStack(), []
        kit.stages += 1
        self.tag = f"_{kit.stages}"

    def __enter__(self):
        return self

    def __exit__(self, *exc):
        if exc[0] is None and self.sems:
            with self.nc.Block() as block:
                @block.gpsimd
                def _(pool):
                    for s in self.sems:
                        pool.sem_clear(s)
        self.ctx.close()

    def sem(self, name):
        if name in POOL_DMA:
            return self.pool_dma(name)
        s = self.ctx.enter_context(self.nc.semaphore(name + self.tag))
        self.sems.append(s)
        return s

    def pool_dma(self, name):
        return self.kit.ctx.enter_context(self.nc.semaphore(name + self.tag))

    def sb(self, name, shape, dt=F32):
        return self.ctx.enter_context(self.nc.sbuf_tensor(name + self.tag, shape, dt))


class Norm:

    def __init__(self, st, tag, src, src_ready, src_step=1):
        self.src, self.src_ready, self.src_step = src, src_ready, src_step
        self.stat = st.sb(f"stat{tag}", [P, 2, 6])
        self.mv = st.sb(f"mv{tag}", [P, 2, 2])
        self.sd = st.sb(f"sd{tag}", [P, 2])
        self.rs = st.sb(f"rs{tag}", [P, 2])
        self.xn = st.sb(f"xn{tag}", [P, 2, D])
        self.stats_done = st.sem(f"stats_done{tag}")
        self.moments_done = st.sem(f"moments_done{tag}")
        self.sd_done = st.sem(f"sd_done{tag}")
        self.rs_done = st.sem(f"rs_done{tag}")
        self.xn_done = st.sem(f"xn_done{tag}")
        self.gate = st.sem(f"gate{tag}")
        self.kit = st.kit

    def dve_moments(self, eng, i, tiles):
        wait(eng, self.src_ready, (i + 1) * self.src_step)
        for j, w in enumerate(tiles):
            ins = eng.bn_stats(self.stat[0:w, j, :], self.src[0:w, j, :])
        ins.then_inc(self.stats_done, 1)
        wait(eng, self.stats_done, i + 1)
        wait(eng, self.sd_done, i)
        wait(eng, self.xn_done, i, self.gate)
        for j, w in enumerate(tiles):
            ins = eng.bn_aggr(self.mv[0:w, j, :], self.stat[0:w, j, :])
        ins.then_inc(self.moments_done, 1)

    def act_sd(self, eng, i, tiles):
        w, n = tiles[0], len(tiles)
        wait(eng, self.moments_done, i + 1)
        wait(eng, self.rs_done, i)
        eng.activation(self.sd[0:w, 0:n], self.mv[0:w, 0:n, 1], ACT.Sqrt,
                       bias=self.kit.eps[0:w, :]).then_inc(self.sd_done, 1)

    def dve_normalise(self, eng, i, tiles, used=()):
        w, n = tiles[0], len(tiles)
        wait(eng, self.sd_done, i + 1)
        wait(eng, self.xn_done, i)
        eng.reciprocal(self.rs[0:w, 0:n], self.sd[0:w, 0:n]).then_inc(self.rs_done, 1)
        wait(eng, self.rs_done, i + 1)
        for sem, step in used:
            wait(eng, sem, i * step)
        for j, w in enumerate(tiles):
            ins = eng.tensor_scalar(self.xn[0:w, j, :], self.src[0:w, j, :], self.mv[0:w, j, 0:1],
                                    self.rs[0:w, j:j + 1], ALU.subtract, ALU.mult)
        ins.then_inc(self.xn_done, 1)


def pe_turn(kit, eng, bank, src, tiles, done):
    for j, w in enumerate(tiles):
        for c in range(C):
            ins = eng.transpose(bank[:, c * BODY + j * P:c * BODY + j * P + w],
                                src[0:w, j, c * P:(c + 1) * P], kit.ident[0:w, 0:w])
    ins.then_inc(done, 1)


def halves(ap):
    return ap.rearrange("p (c n) -> p c n", c=C)

SLOTS = 3


class Unit:

    def __init__(self, c, i=None):
        self.j = c % SLOTS
        if i is None:
            self.n, self.r = c, c // SLOTS
        else:
            self.n, self.r = i * SLOTS + c, i + c // SLOTS
        self.first = i is None and c == 0
        self.last = i is None and c == FULL
        self.tiles = (LAST,) if self.last else (P, P)
        self.w, self.k, self.wt = self.tiles[0], len(self.tiles), sum(self.tiles)


def pipeline(eng, *steps):
    def at(p, i=None):
        for step, lag in steps:
            if i is not None or 0 <= p - lag <= FULL:
                step(Unit(p - lag, i))
    for p in range(2 * SLOTS):
        at(p)
    with eng.Fori(2, FULL // SLOTS) as i:
        for p in range(SLOTS):
            at(p, i)
    for p in range(FULL, FULL + 1 + max(lag for _, lag in steps)):
        at(p)


def free(eng, sem, u, step=1, gate=None):
    wait(eng, sem, (u.n - (SLOTS - 1)) * step, gate)


class Slots:

    def __init__(self, st, name, shape, dt=F32, dma=None):
        self.buf = [st.sb(f"{name}{j}", shape, dt) for j in range(SLOTS)]
        if dma:
            self.sem = [(st.pool_dma if dma == "pool" else st.sem)(f"{name}_dma{j}") for j in range(SLOTS)]

    def __getitem__(self, u):
        return self.buf[u.j]

    def part(self, u):
        return self.buf[u.j][0:u.w, 0:u.k, :]

    def load(self, eng, u, src):
        eng.dma_start(self.part(u), rows(src, u.n, u.tiles)).then_inc(self.sem[u.j], 16)

    def store(self, eng, u, dst, width=None):
        eng.dma_start(rows(dst, u.n, u.tiles), self.part(u) if width is None else self.buf[u.j][0:u.w, 0:u.k, 0:width]).then_inc(self.sem[u.j], 16)

    def landed(self, eng, u, gate=None, of=1):
        wait(eng, self.sem[u.j], 16 * of * (u.r + 1), gate)

    def sent(self, eng, u, gate=None):
        wait(eng, self.sem[u.j], 16 * u.r, gate)

    def all_sent(self, eng):
        for j in range(SLOTS):
            eng.wait_ge(self.sem[j], 16 * ((FULL + SLOTS - j) // SLOTS))


class PipedNorm:

    def __init__(self, st, tag, src, width=D, dma="pool"):
        self.src, self.k = src, st.kit
        self.stat = Slots(st, f"stat{tag}", [P, 2, 6])
        self.mv = Slots(st, f"mv{tag}", [P, 2, 2])
        self.ve = Slots(st, f"ve{tag}", [P, 2])
        self.rs = Slots(st, f"rs{tag}", [P, 2])
        self.xn = Slots(st, f"pxn{tag}", [P, 2, width], dma=dma)
        self.stats_done, self.moments_done, self.ve_done, self.rs_done, self.xn_done = (
            st.sem(n + tag) for n in ("stats_done", "moments_done", "ve_done", "rs_done", "xn_done"))
        self.gate = st.sem("norm_gate" + tag)

    def moments(self, dve, u):
        for j, w in enumerate(u.tiles):
            ins = dve.bn_stats(self.stat[u][0:w, j, :], self.src[u][0:w, j, :])
        ins.then_inc(self.stats_done, 1)
        free(dve, self.xn_done, u)
        wait(dve, self.stats_done, u.n + 1, self.gate)
        for j, w in enumerate(u.tiles):
            ins = dve.bn_aggr(self.mv[u][0:w, j, :], self.stat[u][0:w, j, :])
        ins.then_inc(self.moments_done, 1)
        wait(dve, self.moments_done, u.n + 1)
        dve.tensor_scalar(self.ve[u][0:u.w, 0:u.k], self.mv[u][0:u.w, 0:u.k, 1], LN_EPS, None, ALU.add).then_inc(self.ve_done, 1)

    def root(self, pool, u, gate):
        wait(pool, self.ve_done, u.n + 1, gate)
        free(pool, self.xn_done, u, gate=gate)
        pool.tensor_tensor(self.rs[u][0:u.w, 0:u.k], self.ve[u][0:u.w, 0:u.k], self.k.mhalf[0:u.w, 0:u.k], ALU.pow).then_inc(self.rs_done, 1)

    def normalise(self, dve, u):
        wait(dve, self.rs_done, u.n + 1)
        for j, w in enumerate(u.tiles):
            ins = dve.tensor_scalar(self.xn[u][0:w, j, 0:D], self.src[u][0:w, j, :], self.mv[u][0:w, j, 0:1],
                                    self.rs[u][0:w, j:j + 1], ALU.subtract, ALU.mult)
        ins.then_inc(self.xn_done, 1)



def clear_acc(sp, d, kit, done):
    for n in range(7):
        r = NTILE * P // 7
        sp.dma_start(d.acc[n * r:(n + 1) * r, :].rearrange("(p t) w -> p (t w)", p=P), kit.zeros[:]).then_inc(done, 16)


def stage_setup(nc, kit, a, d):
    k = kit
    with Stage(nc, kit) as st:
        raw = {n: st.sb("raw_" + n, [P, C, D]) for n in ("L0_gnn_w1", "L0_gnn_w2", "L1_q")}
        wx = st.sb("wx", [P, C, 2 * D])
        bxb = st.sb("bxb", [SDIM, HEADS, P])
        wxT = st.sb("wxT", [SDIM, HEADS, D])
        bxc = st.sb("bxc", [SDIM, HEADS])
        src_f = st.sb("src_f", [P, NET])
        rraw = st.sb("rraw", [EXPERTS, D])
        epad_i = st.sb("epad_i", [P, 2, GE], I32)
        esrc = st.sb("esrc", [P, GE])
        edst = st.sb("edst", [P, GE])
        eew = st.sb("eew", [P, GE])
        chg = st.sb("chg", [P, GE])
        zed = st.sb("zed", [P, GE])
        rank = st.sb("rank", [P, GE])
        fd = st.sb("fd", [P, GE])
        tmp = st.sb("tmp", [P, GE])
        okc = st.sb("okc", [P, 4])
        acc_cleared = st.sem("acc_cleared")
        mset, cst, idn = st.sem("mset"), st.sem("cst"), st.sem("idn")
        wld, eld = st.sem("wld"), st.sem("eld")
        step = st.sem("step")
        tdone, cdone = st.sem("tdone"), st.sem("cdone")
        nload = [0]

        with nc.Block() as block:
            @block.sync
            def _(sp):
                def load(dst, src):
                    sp.dma_start(dst, src, allow_slow_non_contiguous=True).then_inc(wld, 16)
                    nload[0] += 1
                full, rest = E // GE, E % GE
                sp.wait_ge(mset, 1)
                for n, name in enumerate(("src", "dst")):
                    sp.dma_start(epad_i[0:full, n, :], a[name][0:full * GE].rearrange("(g e) -> g e", e=GE)).then_inc(eld, 16)
                    sp.dma_start(epad_i[full:full + 1, n, 0:rest], a[name][full * GE:E].rearrange("(g e) -> g e", g=1)).then_inc(eld, 16)
                sp.dma_start(eew[0:full, :], a["edge_weight"][0:full * GE].rearrange("(g e) -> g e", e=GE)).then_inc(eld, 16)
                sp.dma_start(eew[full:full + 1, 0:rest], a["edge_weight"][full * GE:E].rearrange("(g e) -> g e", g=1)).then_inc(eld, 16)
                sp.wait_ge(eld, 96)
                sq = lambda ap: ap.rearrange("(c p) n -> p c n", p=P)
                load(raw["L0_gnn_w1"][:], sq(a["L0_gnn_w1"]))
                load(raw["L0_gnn_w2"][:], sq(a["L0_gnn_w2"]))
                load(raw["L1_q"][:], sq(a["L1_mix_W_qk"][0]))
                load(rraw[:], a["L0_ffn_router_w"])
                load(k.wq0[:], sq(a["L0_mix_wq"]))
                load(k.wkv0[:, :, 0:D], sq(a["L0_mix_wk"]))
                load(k.wkv0[:, :, D:2 * D], sq(a["L0_mix_wv"]))
                load(k.wo0[:], sq(a["L0_mix_wo"]))
                for j in range(2):
                    load(k.rb2[:, j, :], bcast_rows(a["L0_ffn_router_b"], EXPERTS))
                load(k.wg1[:], sq(a["L1_gnn_W1"]))
                load(k.wg2[:], sq(a["L1_gnn_W2"]))
                load(k.wkv1[:, :, 0:D], sq(a["L1_mix_W_qk"][1]))
                load(k.wkv1[:, :, D:2 * D], sq(a["L1_mix_W_v"]))
                load(k.wfx[:], sq(a["L1_ffn_W_fx"]))
                load(wx[:], sq(a["L1_ffn_W_x"]))
                load(k.wout[:], a["L1_ffn_W_out"].rearrange("(h c) n -> c h n", c=SDIM))
                for dst, name in ((k.wslice, "L1_ffn_W_slice"), (k.wsq, "L1_ffn_W_q"), (k.wsk, "L1_ffn_W_k"), (k.wsv, "L1_ffn_W_v")):
                    load(dst[:], a[name])
                load(k.bkv0[:, 0:D], bcast_rows(a["L0_mix_bk"], D))
                load(k.bkv0[:, D:2 * D], bcast_rows(a["L0_mix_bv"], D))
                load(k.bk1row[:], bcast_rows(a["L1_mix_b_qk"][1], D))
                load(k.bkv1[:, D:2 * D], bcast_rows(a["L1_mix_b_v"], D))
                load(k.bg1[:], bcast_rows(a["L1_gnn_b1"], D))
                load(k.bg2[:], bcast_rows(a["L1_gnn_b2"], D))
                load(k.bout[:], bcast_rows(a["L1_ffn_b_out"], D))
                load(k.bfx[:], a["L1_ffn_b_fx"].rearrange("(a n) -> a n", a=1))
                load(k.bslice_row[:], bcast_rows(a["L1_ffn_b_slice"], SLICES))
                load(k.temp[:], bcast_rows(a["L1_ffn_temperature"].rearrange("a h b c -> (a h b c)"), HEADS))
                load(k.epsw[:], bcast_rows(a["L0_gnn_eps_weight"], 1))
                cols = ((k.g1c, "L0_gnn_gamma1"), (k.be1c, "L0_gnn_beta1"), (k.ghc, "L0_gnn_gamma_h"), (k.behc, "L0_gnn_beta_h"),
                        (k.bqc, "L0_mix_bq"), (k.boc, "L0_mix_bo"), (k.gmc, "L1_mix_gamma"), (k.bemc, "L1_mix_beta"))
                for dst, name in cols:
                    load(dst[:], a[name].rearrange("(c p) -> p c", p=P))
                load(k.bq1c[:], a["L1_mix_b_qk"][0].rearrange("(c p) -> p c", p=P))
                load(k.bk1c[:], a["L1_mix_b_qk"][1].rearrange("(c p) -> p c", p=P))
                load(bxc[:], a["L1_ffn_b_x"].rearrange("(h c) -> c h", c=SDIM))
                sp.wait_ge(idn, 17)
                clear_acc(sp, d, k, acc_cleared)
                sp.wait_ge(acc_cleared, 7 * 16)
                sp.dma_start(d.dst.rearrange("(g e) -> g e", e=GE), epad_i[0:NG, 1, :]).then_inc(eld, 16)
                sp.wait_ge(eld, 112)
                sp.wait_ge(wld, 16 * nload[0])

            @block.gpsimd
            def _(pool):
                pool.memset(epad_i[:, 0, :], 0).then_inc(cst, 1)
                pool.memset(epad_i[:, 1, :], N).then_inc(cst, 1)
                pool.memset(eew[:], 0.0).then_inc(cst, 1)
                pool.wait_ge(cst, 3)
                pool.sem_inc(mset, 1)
                pool.memset(k.ident[:], 0.0).then_inc(idn, 1)
                pool.wait_ge(idn, 1)
                pool.memset(k.tri[:], 1.0).then_inc(idn, 1)
                pool.wait_ge(idn, 2)
                pool.memset(k.hmask[:], 0.0).then_inc(idn, 1)
                pool.wait_ge(idn, 3)
                pool.memset(k.upper[:], 1.0).then_inc(idn, 1)
                pool.wait_ge(idn, 4)
                pool.affine_select(out=k.ident[:], in_=k.ident[:], compare_op=ALU.not_equal, fill=1.0, base=0,
                                   pattern=[[-1, P]], channel_multiplier=1).then_inc(idn, 1)
                pool.wait_ge(idn, 5)
                pool.affine_select(out=k.tri[:], in_=k.tri[:], compare_op=ALU.is_gt, fill=0.0, base=0,
                                   pattern=[[-1, P]], channel_multiplier=1).then_inc(idn, 1)
                pool.wait_ge(idn, 6)
                for h in range(4):
                    pool.memset(k.hmask[32 * h:32 * h + 32, 32 * h:32 * h + 32], 1.0).then_inc(idn, 1)
                    pool.wait_ge(idn, 7 + h)
                pool.affine_select(out=k.upper[:], in_=k.upper[:], compare_op=ALU.is_gt, fill=0.0, base=0,
                                   pattern=[[1, P]], channel_multiplier=-1).then_inc(idn, 1)
                pool.wait_ge(idn, 11)
                pool.iota(k.iota_i[:], [[1, P]], base=0, channel_multiplier=0).then_inc(idn, 1)
                pool.wait_ge(idn, 12)
                pool.memset(k.ones[:], 1.0).then_inc(idn, 1)
                pool.wait_ge(idn, 13)
                pool.memset(k.zeros[:], 0.0).then_inc(idn, 1)
                pool.wait_ge(idn, 14)
                pool.memset(k.eps[:], LN_EPS).then_inc(idn, 1)
                pool.wait_ge(idn, 15)
                pool.memset(k.mhalf[:], -0.5).then_inc(idn, 1)
                pool.wait_ge(idn, 16)
                pool.memset(zed[:], 0.0).then_inc(idn, 1)
                pool.wait_ge(idn, 17)

            @block.vector
            def _(dve):
                n = [0]

                def then(ins):
                    n[0] += 1
                    ins.then_inc(step, 1)
                    dve.wait_ge(step, n[0])
                dve.wait_ge(idn, 17)
                then(dve.tensor_copy(k.iota[:], k.iota_i[:]))
                dve.wait_ge(eld, 96)
                then(dve.tensor_copy(esrc[0:NG, :], epad_i[0:NG, 0, :]))
                then(dve.tensor_copy(edst[0:NG, :], epad_i[0:NG, 1, :]))
                then(dve.memset(chg[:], 0.0))
                then(dve.tensor_tensor(chg[0:NG, 1:GE], edst[0:NG, 1:GE], edst[0:NG, 0:GE - 1], ALU.not_equal))
                then(dve.tensor_tensor_scan(rank[0:NG, :], chg[0:NG, :], zed[0:NG, :], 0.0, ALU.add, ALU.add))
                then(dve.memset(tmp[:], 0.0))
                then(dve.tensor_tensor(tmp[0:NG, 1:GE], edst[0:NG, 1:GE], edst[0:NG, 0:GE - 1], ALU.subtract))
                then(dve.tensor_reduce(okc[0:NG, 0:1], tmp[0:NG, :], AX.X, ALU.min))
                then(dve.tensor_scalar(okc[0:NG, 1:2], okc[0:NG, 0:1], 0.0, None, ALU.is_ge))
                then(dve.tensor_scalar(okc[0:NG, 2:3], rank[0:NG, GE - 1:GE], float(P - 1), None, ALU.is_le))
                then(dve.tensor_tensor(okc[0:NG, 3:4], okc[0:NG, 1:2], okc[0:NG, 2:3], ALU.mult))
                then(dve.memset(chg[:, 0:1], 1.0))
                then(dve.scalar_tensor_tensor(out=fd[0:NG, :], in0=edst[0:NG, :], scalar=-FAR, in1=chg[0:NG, :], op0=ALU.add, op1=ALU.mult))
                then(dve.memset(k.ext[:], 1.0))
                dst = ((src_f, esrc), (k.dst_f, edst), (k.rank_f, rank), (k.ew_f, eew), (k.fd_f, fd))
                kk = 0
                for out, _ in dst:
                    for u in range(GT):
                        dve.wait_ge(tdone, kk + 1)
                        dve.tensor_copy(out[:].rearrange("p (g u) -> p g u", u=GT)[:, :, u], k.bank[kk % 2][:, 0:NG]).then_inc(cdone, 1)
                        kk += 1
                dve.wait_ge(cdone, kk)
                then(dve.tensor_copy(k.src_i[:], src_f[:]))
                then(dve.tensor_copy(k.dst_i[:], k.dst_f[:]))
                then(dve.tensor_copy(k.ext[:, :, 0], k.ew_f[:]))
                then(dve.tensor_copy(k.ext[:, :, 2], k.fd_f[:]))
                dve.wait_ge(tdone, kk + 1)
                dve.tensor_scalar(k.flag[0:1, :], k.bank[kk % 2][0:1, 0:1], float(NG), None, ALU.is_equal).then_inc(cdone, 1)
                kk += 1
                for out in (k.w1T, k.w2T, k.wq1T):
                    for c in range(C):
                        dve.wait_ge(tdone, kk + 1)
                        dve.tensor_copy(out[:, c, :], k.bank[kk % 2][:, 0:D]).then_inc(cdone, 1)
                        kk += 1
                for c in range(C):
                    dve.wait_ge(tdone, kk + 1)
                    dve.tensor_copy(k.rT[:, c, :], k.bank[kk % 2][:, 0:EXPERTS]).then_inc(cdone, 1)
                    kk += 1
                dve.wait_ge(wld, 16 * nload[0])
                then(dve.memset(k.wdeg[:], 1.0))
                then(dve.tensor_scalar(k.temp[:], k.temp[:], 0.1, 5.0, ALU.max, ALU.min))
                then(dve.reciprocal(k.rtemp[:], k.temp[:]))
                for h in range(HEADS):
                    dve.wait_ge(tdone, kk + 1)
                    dve.tensor_copy(wxT[:, h, :], k.bank[kk % 2][0:SDIM, 0:D]).then_inc(cdone, 1)
                    kk += 1
                    for c in range(C):
                        dve.wait_ge(tdone, kk + 1)
                        dve.tensor_scalar(k.wxs[:, c, h * SLICES:(h + 1) * SLICES], k.bank[kk % 2][:, 0:SLICES],
                                          k.rtemp[:, h:h + 1], None, ALU.mult).then_inc(cdone, 1)
                        kk += 1
                    dve.wait_ge(tdone, kk + 1)
                    then(dve.tensor_tensor(k.bxs[:, h * SLICES:(h + 1) * SLICES], k.bank[kk % 2][:, 0:SLICES], k.bslice_row[:], ALU.add))
                    dve.tensor_scalar(k.bxs[:, h * SLICES:(h + 1) * SLICES], k.bxs[:, h * SLICES:(h + 1) * SLICES],
                                      k.rtemp[:, h:h + 1], None, ALU.mult).then_inc(cdone, 1)
                    kk += 1

            @block.scalar
            def _(act):
                act.wait_ge(wld, 16 * nload[0])
                act.wait_ge(idn, 17)
                for h in range(HEADS):
                    act.activation(bxb[:, h, :], k.ones[0:SDIM, :], ACT.Copy, scale=bxc[:, h:h + 1]).then_inc(cst, 1)

            @block.tensor
            def _(pe):
                pe.wait_ge(idn, 17)
                kk = 0

                def go():
                    nonlocal kk
                    if kk >= 2:
                        pe.wait_ge(cdone, kk - 1)
                    kk += 1
                    return k.bank[(kk - 1) % 2]
                pe.wait_ge(step, 14)
                for x in (esrc, edst, rank, eew, fd):
                    for u in range(GT):
                        b = go()
                        pe.transpose(b[:, 0:NG], x[0:NG, u * P:(u + 1) * P], k.ident[0:NG, 0:NG]).then_inc(tdone, 1)
                b = go()
                pe.matmul(b[0:1, 0:1], okc[0:NG, 3:4], k.ones[0:NG, 0:1], start=True, stop=True).then_inc(tdone, 1)
                pe.wait_ge(wld, 16 * nload[0])
                for x in (raw["L0_gnn_w1"], raw["L0_gnn_w2"], raw["L1_q"]):
                    for c in range(C):
                        b = go()
                        for o in range(C):
                            ins = pe.transpose(b[:, o * P:(o + 1) * P], x[:, o, c * P:(c + 1) * P], k.ident[:])
                        ins.then_inc(tdone, 1)
                for c in range(C):
                    b = go()
                    pe.transpose(b[:, 0:EXPERTS], rraw[:, c * P:(c + 1) * P], k.ident[0:EXPERTS, 0:EXPERTS]).then_inc(tdone, 1)
                for h in range(HEADS):
                    b = go()
                    for c in range(C):
                        ins = pe.transpose(b[0:SDIM, c * P:(c + 1) * P], wx[:, c, h * SDIM:(h + 1) * SDIM], k.ident[:])
                    ins.then_inc(tdone, 1)
                    for c in range(C):
                        b = go()
                        if c == 0:
                            pe.wait_ge(cdone, kk - 1)
                        pe.matmul(b[:, 0:SLICES], wxT[:, h, c * P:(c + 1) * P], k.wslice[:], start=True, stop=True).then_inc(tdone, 1)
                    b = go()
                    if h == 0:
                        pe.wait_ge(cst, 3 + HEADS)
                    pe.matmul(b[:, 0:SLICES], bxb[:, h, :], k.wslice[:], start=True, stop=True).then_inc(tdone, 1)


def stage_front(nc, kit, a, d):
    k = kit
    with Stage(nc, kit) as st:
        x = Slots(st, "x", [P, 2, D], dma="sp")
        xnT = Slots(st, "xnT", [P, C, BODY])
        z = Slots(st, "z", [P, 2, D])
        e = Slots(st, "e", [P, 2, D])
        kf = Slots(st, "kf", [P, 2, D])
        nm = PipedNorm(st, "a", x, D + 1)
        one_done, turned, xnT_done, key_psum, z_done, e_done, kf_done, sum_done, gsp, gpool = (
            st.sem(n) for n in "one_done turned xnT_done key_psum z_done e_done kf_done sum_done gsp gpool".split())
        with nc.Block() as block:
            @block.sync
            def _(sp):
                def load(u):
                    free(sp, nm.xn_done, u, gate=gsp)
                    x.load(sp, u, a["x"])
                pipeline(sp, (load, 0))

            @block.gpsimd
            def _(pool):
                def store(u):
                    wait(pool, nm.xn_done, u.n + 1, gpool)
                    nm.xn.store(pool, u, d.xn, D)
                pipeline(pool, (lambda u: nm.root(pool, u, gpool), 0), (store, 1))
                nm.xn.all_sent(pool)

            @block.vector
            def _(dve):
                for b in nm.xn.buf:
                    dve.memset(b[:, :, D:D + 1], 1.0).then_inc(one_done, 1)

                def moments(u):
                    x.landed(dve, u)
                    nm.moments(dve, u)

                def normalise(u):
                    free(dve, sum_done, u)
                    nm.xn.sent(dve, u)
                    nm.normalise(dve, u)

                def add_bias(u):
                    wait(dve, key_psum, u.n + 1)
                    free(dve, kf_done, u)
                    for j, w in enumerate(u.tiles):
                        ins = dve.tensor_tensor(z[u][0:w, j, :], k.bank[1][0:w, j * D:(j + 1) * D], k.bkv0[0:w, 0:D], ALU.add)
                    ins.then_inc(z_done, 1)

                def features(u):
                    wait(dve, e_done, u.n + 1)
                    free(dve, sum_done, u)
                    dve.scalar_tensor_tensor(out=kf.part(u), in0=e.part(u), scalar=1.0, in1=z.part(u), op0=ALU.min, op1=ALU.add).then_inc(kf_done, 1)
                pipeline(dve, (features, 3), (normalise, 1), (add_bias, 2), (moments, 0))

            @block.scalar
            def _(act):
                def copy_xnT(u):
                    wait(act, turned, u.n + 1)
                    free(act, key_psum, u)
                    act.activation(xnT[u][:, :, 0:u.wt], halves(k.bank[0][:])[:, :, 0:u.wt], ACT.Copy).then_inc(xnT_done, 1)

                def exp(u):
                    wait(act, z_done, u.n + 1)
                    free(act, kf_done, u)
                    act.activation(e.part(u), z.part(u), ACT.Exp)
                    act.activation(z.part(u), z.part(u), ACT.Relu).then_inc(e_done, 1)
                pipeline(act, (copy_xnT, 1), (exp, 2))

            @block.tensor
            def _(pe):
                pe.wait_ge(one_done, SLOTS)

                def turn(u):
                    wait(pe, nm.xn_done, u.n + 1)
                    wait(pe, xnT_done, u.n)
                    pe_turn(k, pe, k.bank[0], nm.xn[u], u.tiles, turned)

                def sums(u):
                    wait(pe, kf_done, u.n + 1)
                    for j, w in enumerate(u.tiles):
                        for c in range(C):
                            ins = pe.matmul(k.bank[3 + c][:, 0:D + 1], kf[u][0:w, j, c * P:(c + 1) * P], nm.xn[u][0:w, j, :],
                                            start=u.first and j == 0, stop=u.last)
                    ins.then_inc(sum_done, 1)

                def keys(u):
                    wait(pe, xnT_done, u.n + 1)
                    wait(pe, z_done, u.n)
                    for j, w in enumerate(u.tiles):
                        for c in range(C):
                            ins = pe.matmul(k.bank[1][0:w, j * D:(j + 1) * D], xnT[u][:, c, j * P:j * P + w], k.wkv0[:, c, 0:D], start=(c == 0), stop=(c == C - 1))
                    ins.then_inc(key_psum, 1)
                pipeline(pe, (turn, 1), (sums, 3), (keys, 1))
        A = st.sb("A", [P, C, D + 1])
        AT = st.sb("AT", [P, C, D])
        srow = st.sb("srow", [1, C, P])
        kvm = st.sb("kvm", [P, C, P])
        a_read, a_turned, at_done, kv_psum, masked, m0_psum, m0_done = (st.sem(n) for n in "a_read a_turned at_done kv_psum masked m0_psum m0_out".split())
        with nc.Block() as block:
            @block.vector
            def _(dve):
                for c in range(C):
                    ins = dve.tensor_copy(A[:, c, :], k.bank[3 + c][:, 0:D + 1])
                ins.then_inc(a_read, 1)
                dve.wait_ge(a_read, 1)
                for c in range(C):
                    dve.tensor_scalar(k.ks[:, c, :], k.hmask[:], A[:, c, D:D + 1], None, ALU.mult)
                dve.wait_ge(a_turned, 1)
                for c in range(C):
                    dve.tensor_copy(AT[:, c, :], k.bank[c][:, 0:D])
                dve.tensor_copy(srow[:], k.bank[2][0:1, 0:C * P].rearrange("p (c n) -> p c n", c=C)).then_inc(at_done, 1)
                dve.wait_ge(kv_psum, 1)
                for c in range(C):
                    ins = dve.tensor_tensor(kvm[:, c, :], k.bank[5][:, c * P:(c + 1) * P], k.hmask[:], ALU.mult)
                ins.then_inc(masked, 1)
                dve.wait_ge(m0_psum, 1)
                for c in range(C):
                    ins = dve.tensor_copy(k.m0[:, c, :], k.bank[6][:, c * D:(c + 1) * D])
                ins.then_inc(m0_done, 1)

            @block.tensor
            def _(pe):
                pe.wait_ge(a_read, 1)
                for c in range(C):
                    for o in range(C):
                        pe.transpose(k.bank[o][:, c * P:(c + 1) * P], A[:, c, o * P:(o + 1) * P], k.ident[:])
                    ins = pe.transpose(k.bank[2][0:1, c * P:(c + 1) * P], A[:, c, D:D + 1], k.ident[:])
                ins.then_inc(a_turned, 1)
                pe.wait_ge(at_done, 1)
                for c in range(C):
                    v = slice(D + c * P, D + (c + 1) * P)
                    for o in range(C):
                        pe.matmul(k.bank[5][:, c * P:(c + 1) * P], k.wkv0[:, o, v], AT[:, o, c * P:(c + 1) * P], start=(o == 0), stop=False)
                    ins = pe.matmul(k.bank[5][:, c * P:(c + 1) * P], k.bkv0[0:1, v], srow[:, c, :], start=False, stop=True)
                ins.then_inc(kv_psum, 1)
                pe.wait_ge(masked, 1)
                for c in range(C):
                    ins = pe.matmul(k.bank[6][:, c * D:(c + 1) * D], kvm[:, c, :], k.wo0[:, c, :], start=True, stop=True)
                ins.then_inc(m0_psum, 1)


def width(i):
    return N - (NTILE - 1) * P if isinstance(i, int) and i == NTILE - 1 else P


def tile_rows(ap, i, w):
    return ap[bass.ds(i * P, w), :]


def chunks(ap):
    return ap[:, 0:C * P].rearrange("p (c n) -> p c n", c=C)


class Side:

    def __init__(self, st, a, d):
        self.st, self.k, self.a, self.d = st, st.kit, a, d
        self.xn = st.sb("side_xn", [P, D])
        self.xnT = st.sb("side_xnT", [P, C, P])
        self.loaded, self.turned, self.xnT_done = st.sem("side_loaded"), st.sem("side_turned"), st.sem("side_xnT_done")
        self.gsp, self.gact, self.gdve = st.sem("side_gsp"), st.sem("side_gact"), st.sem("side_gdve")
        self.sp, self.act, self.dve, self.pe = {"move": self.move}, {2: self.copy_xnT}, {}, {1: self.turn}
        self.make()

    def engine(self, sp=None, act=None, dve=None, pe=None):
        self.e_sp, self.e_act, self.e_dve, self.e_pe = sp, act, dve, pe

    def turn(self, i, w):
        pe, k = self.e_pe, self.k
        wait(pe, self.loaded, self.loads * 16 * (i + 1))
        wait(pe, self.xnT_done, i)
        for c in range(C):
            ins = pe.transpose(k.bank[2][:, c * P:c * P + w], self.xn[0:w, c * P:(c + 1) * P], k.ident[0:w, 0:w])
        ins.then_inc(self.turned, 1)

    def copy_xnT(self, i, w):
        act = self.e_act
        wait(act, self.turned, i + 1)
        wait(act, self.xnT_read, i)
        act.activation(self.xnT[:, :, 0:w], chunks(self.k.bank[2])[:, :, 0:w], ACT.Copy).then_inc(self.xnT_done, 1)

    def sp_start(self, sp):
        pass

    def sp_end(self, sp):
        pass


class LinearAttention(Side):

    def make(self):
        st = self.st
        self.loads = 2
        self.x = st.sb("side_x", [P, D])
        self.e = st.sb("side_e", [P, C, P])
        self.q = st.sb("side_q", [P, C, P])
        self.nr = st.sb("side_nr", [P, C, P])
        self.s = st.sb("side_s", [P, C, P])
        self.xm = st.sb("side_xm", [P, D])
        (self.q_psum, self.e_done, self.zr_done, self.q_done, self.nrm_psum, self.nr_done, self.qn_done, self.mix_psum,
         self.s_done, self.back, self.half, self.xm_done, self.sent) = (
            st.sem("side_" + n) for n in "q_psum e_done zr_done q_done nrm_psum nr_done qn_done mix_psum s_done back half xm_done sent".split())
        self.zeroed = st.sem("zeroed")
        self.xnT_read = self.q_psum
        self.pe.update({4: self.query, 9: self.norms, 12: self.mix, 14: self.turn_back})
        self.act.update({5: self.exp, 13: self.add_bias})
        self.dve.update({"early": self.features, "late": self.normalise_and_sum})

    def move(self, i, w):
        sp, d = self.e_sp, self.d
        if not (isinstance(i, int) and i == 0):
            wait(sp, self.xm_done, i, self.gsp)
            sp.dma_start(tile_rows(d.xm, i - 1, P), self.xm[:]).then_inc(self.sent, 16)
        sp.dma_start(self.xn[0:w, :], tile_rows(d.xn, i, w)).then_inc(self.loaded, 16)
        sp.dma_start(self.x[0:w, :], tile_rows(self.a["x"], i, w)).then_inc(self.loaded, 16)

    def sp_start(self, sp):
        per = SORTED * D // 16
        for n in range(16):
            sp.dma_start(self.d.xs.rearrange("(p r) d -> p (r d)", p=P)[:, n * per:(n + 1) * per], self.k.zeros[:, 0:per]).then_inc(self.zeroed, 16)

    def sp_end(self, sp):
        sp.wait_ge(self.zeroed, 16 * 16)
        self.send_last(sp)

    def send_last(self, sp):
        w = width(NTILE - 1)
        sp.wait_ge(self.xm_done, NTILE)
        sp.dma_start(tile_rows(self.d.xm, NTILE - 1, w), self.xm[0:w, :]).then_inc(self.sent, 16)
        sp.wait_ge(self.sent, 16 * NTILE)

    def query(self, i, w):
        pe, k = self.e_pe, self.k
        wait(pe, self.xnT_done, i + 1)
        wait(pe, self.zr_done, i)
        for o in range(C):
            for c in range(C):
                ins = pe.matmul(k.bank[3][:, o * P:o * P + w], k.wq0[:, c, o * P:(o + 1) * P], self.xnT[:, c, 0:w], start=(c == 0), stop=(c == C - 1))
        ins.then_inc(self.q_psum, 1)

    def exp(self, i, w):
        act, k = self.e_act, self.k
        wait(act, self.q_psum, i + 1)
        wait(act, self.q_done, i)
        for c in range(C):
            ins = act.activation(self.e[:, c, 0:w], k.bank[3][:, c * P:c * P + w], ACT.Exp, bias=k.bqc[:, c:c + 1])
        ins.then_inc(self.e_done, 1)

    def features(self, i, w):
        dve, k = self.e_dve, self.k
        wait(dve, self.e_done, i + 1)
        wait(dve, self.mix_psum, i)
        for c in range(C):
            ins = dve.tensor_scalar(self.q[:, c, 0:w], k.bank[3][:, c * P:c * P + w], k.bqc[:, c:c + 1], 0.0, ALU.add, ALU.max)
        ins.then_inc(self.zr_done, 1)
        wait(dve, self.zr_done, i + 1)
        dve.scalar_tensor_tensor(out=self.q[:, :, 0:w], in0=self.e[:, :, 0:w], scalar=1.0, in1=self.q[:, :, 0:w], op0=ALU.min, op1=ALU.add).then_inc(self.q_done, 1)

    def norms(self, i, w):
        pe, k = self.e_pe, self.k
        wait(pe, self.q_done, i + 1)
        wait(pe, self.nr_done, 2 * i)
        for c in range(C):
            ins = pe.matmul(k.bank[4][:, c * P:c * P + w], k.ks[:, c, :], self.q[:, c, 0:w], start=True, stop=True)
        ins.then_inc(self.nrm_psum, 1)

    def mix(self, i, w):
        pe, k = self.e_pe, self.k
        wait(pe, self.qn_done, i + 1)
        wait(pe, self.s_done, i)
        for o in range(C):
            for c in range(C):
                ins = pe.matmul(k.bank[5][:, o * P:o * P + w], k.m0[:, c, o * P:(o + 1) * P], self.q[:, c, 0:w], start=(c == 0), stop=(c == C - 1))
        ins.then_inc(self.mix_psum, 1)

    def add_bias(self, i, w):
        act, k = self.e_act, self.k
        wait(act, self.mix_psum, i + 1)
        wait(act, self.back, i)
        for c in range(C):
            ins = act.activation(self.s[:, c, 0:w], k.bank[5][:, c * P:c * P + w], ACT.Identity, bias=k.boc[:, c:c + 1])
        ins.then_inc(self.s_done, 1)

    def turn_back(self, i, w):
        pe, k = self.e_pe, self.k
        wait(pe, self.s_done, i + 1)
        wait(pe, self.half, i)
        for c in range(C):
            ins = pe.transpose(k.bank[6][0:w, c * P:(c + 1) * P], self.s[:, c, 0:w], k.ident[:])
        ins.then_inc(self.back, 1)

    def normalise_and_sum(self, i, w):
        dve, k = self.e_dve, self.k
        wait(dve, self.nrm_psum, i + 1)
        dve.tensor_scalar(self.nr[:, :, 0:w], chunks(k.bank[4])[:, :, 0:w], 1e-6, None, ALU.add).then_inc(self.nr_done, 1)
        wait(dve, self.nr_done, 2 * i + 1)
        dve.reciprocal(self.nr[:, :, 0:w], self.nr[:, :, 0:w]).then_inc(self.nr_done, 1)
        wait(dve, self.nr_done, 2 * i + 2)
        dve.tensor_tensor(self.q[:, :, 0:w], self.q[:, :, 0:w], self.nr[:, :, 0:w], ALU.mult).then_inc(self.qn_done, 1)
        wait(dve, self.back, i + 1)
        wait(dve, self.loaded, 32 * (i + 1))
        wait(dve, self.sent, 16 * i)
        dve.tensor_tensor(self.xm[0:w, :], k.bank[6][0:w, 0:D], self.x[0:w, :], ALU.add).then_inc(self.half, 1)
        wait(dve, self.half, i + 1)
        dve.tensor_tensor(self.xm[0:w, :], self.xm[0:w, :], self.xn[0:w, :], ALU.add).then_inc(self.xm_done, 1)


class KeySums(Side):

    def make(self):
        st = self.st
        self.loads = 1
        self.z = st.sb("side_z", [P, D])
        self.v = st.sb("side_v", [P, D + 1])
        (self.kv_psum, self.z_done, self.e_done, self.summed, self.one) = (st.sem("side_" + n) for n in "kv_psum z_done e_done summed one".split())
        self.xnT_read = self.kv_psum
        self.pe.update({4: self.keys_values, 12: self.sum})
        self.act.update({8: self.exp})
        self.dve.update({"early": self.add_bias})

    def engine(self, sp=None, act=None, dve=None, pe=None):
        Side.engine(self, sp, act, dve, pe)
        if dve is not None:
            dve.memset(self.v[:, D:D + 1], 1.0).then_inc(self.one, 1)

    def move(self, i, w):
        sp = self.e_sp
        wait(sp, self.turned, i, self.gsp)
        sp.dma_start(self.xn[0:w, :], tile_rows(self.d.xn, i, w)).then_inc(self.loaded, 16)

    def keys_values(self, i, w):
        pe, k = self.e_pe, self.k
        wait(pe, self.xnT_done, i + 1)
        wait(pe, self.z_done, i)
        for c in range(C):
            ins = pe.matmul(k.bank[3][0:w, :], self.xnT[:, c, 0:w], k.wkv1[:, c, :], start=(c == 0), stop=(c == C - 1))
        ins.then_inc(self.kv_psum, 1)

    def add_bias(self, i, w):
        dve, k = self.e_dve, self.k
        wait(dve, self.kv_psum, i + 1)
        wait(dve, self.summed, i)
        dve.tensor_tensor(self.z[0:w, :], k.bank[3][0:w, 0:D], k.bkv1[0:w, 0:D], ALU.add)
        dve.tensor_tensor(self.v[0:w, 0:D], k.bank[3][0:w, D:2 * D], k.bkv1[0:w, D:2 * D], ALU.add).then_inc(self.z_done, 1)

    def exp(self, i, w):
        act = self.e_act
        wait(act, self.z_done, i + 1)
        act.activation(self.z[0:w, :], self.z[0:w, :], ACT.Exp).then_inc(self.e_done, 1)

    def sum(self, i, w):
        pe, k = self.e_pe, self.k
        first, last = isinstance(i, int) and i == 0, isinstance(i, int) and i == NTILE - 1
        if first:
            pe.wait_ge(self.one, 1)
        wait(pe, self.e_done, i + 1)
        for c in range(C):
            ins = pe.matmul(k.bank[4 + c][:, 0:D + 1], self.z[0:w, c * P:(c + 1) * P], self.v[0:w, :], start=first, stop=last)
        ins.then_inc(self.summed, 1)


class QueryMix(Side):

    def make(self):
        st = self.st
        self.loads = 2
        self.x = st.sb("side_x", [P, D])
        self.xm = st.sb("side_xm", [P, D])
        (self.q_psum, self.half, self.xm_done, self.sent) = (st.sem("side_" + n) for n in "q_psum half xm_done sent".split())
        self.xnT_read = self.q_psum
        self.pe.update({4: self.query})
        self.dve.update({"early": self.add})

    def move(self, i, w):
        sp, d = self.e_sp, self.d
        if not (isinstance(i, int) and i == 0):
            wait(sp, self.xm_done, i, self.gsp)
            sp.dma_start(tile_rows(d.xm, i - 1, P), self.xm[:]).then_inc(self.sent, 16)
        sp.dma_start(self.xn[0:w, :], tile_rows(d.xn, i, w)).then_inc(self.loaded, 16)
        sp.dma_start(self.x[0:w, :], tile_rows(d.x2, i, w)).then_inc(self.loaded, 16)

    sp_end = LinearAttention.send_last

    def query(self, i, w):
        pe, k = self.e_pe, self.k
        wait(pe, self.xnT_done, i + 1)
        wait(pe, self.half, i)
        for c in range(C):
            ins = pe.matmul(k.bank[3][0:w, 0:D], self.xnT[:, c, 0:w], k.mq[:, c, :], start=(c == 0), stop=(c == C - 1))
        ins.then_inc(self.q_psum, 1)

    def add(self, i, w):
        dve, k = self.e_dve, self.k
        wait(dve, self.q_psum, i + 1)
        wait(dve, self.loaded, 32 * (i + 1))
        wait(dve, self.sent, 16 * i)
        dve.tensor_tensor(self.xm[0:w, :], k.bank[3][0:w, 0:D], k.bmq[0:w, :], ALU.add).then_inc(self.half, 1)
        wait(dve, self.half, i + 1)
        dve.tensor_tensor(self.xm[0:w, :], self.xm[0:w, :], self.x[0:w, :], ALU.add).then_inc(self.xm_done, 1)


def stage_aggregate(nc, kit, a, d, table, side_of):
    k = kit
    with Stage(nc, kit) as st:
        side = side_of(st, a, d)
        fast = st.ctx.enter_context(ExitStack())

        def sb(name, shape, dt=F32):
            return fast.enter_context(nc.sbuf_tensor(name + st.tag, shape, dt))
        gidx = [sb(f"gidx{h}", [P, GT], I32) for h in range(2)]
        sidx = [sb(f"sidx{h}", [P, 1], I32) for h in range(2)]
        g = [sb(f"g{u}", [P, D]) for u in range(2 * GT)]
        gw = [sb(f"gw{h}", [P, GT, AW]) for h in range(2)]
        m = [sb(f"m{u}", [P, P]) for u in range(2 * GT)]
        r = [sb(f"r{h}", [P, AW]) for h in range(2)]
        gathered = [st.pool_dma(f"gathered{u}") for u in range(2 * GT)]
        idx_done, ext_done, m_done, weighted, multiplied, row_done, scattered = (
            st.sem(s) for s in ("idx_done", "ext_done", "m_done", "weighted", "multiplied", "row_done", "scattered"))
        gpool, gact = st.sem("gpool"), st.sem("gact")
        NB = NG // 2
        drow = sb("drow", [P, P], I32)
        dup = sb("dup", [P, P])
        ndup = sb("ndup", [P, 1])
        row_loaded, dup_done = st.sem("row_loaded"), st.sem("dup_done")
        gsp = st.sem("gsp")

        def loop(eng, body):
            body(0)
            with eng.Fori(1, NB - 1) as i:
                body(i)
            body(NB - 1)

        def along(fns, name, i):
            if name in fns:
                fns[name](i, width(i))

        def fast_pool(pool):
            def scatter(i, h):
                grp = 2 * i + h
                wait(pool, row_done, grp + 1, gpool)
                wait(pool, scattered, 16 * grp, gpool)
                pool.indirect_dma_start(d.acc, bass.IndirectOffsetOnAxis(ap=sidx[h][:], axis=0), r[h][:], None,
                                        bounds_check=N - 1, oob_is_err=False, compute_op=ALU.add).then_inc(scattered, 16)

            def body(i):
                for h in range(2):
                    wait(pool, idx_done, 2 * i + h + 1, gpool)
                    for u in range(GT):
                        s = h * GT + u
                        wait(pool, weighted, 16 * i + s - 15, gpool)
                        pool.indirect_dma_start(g[s][:], None, table, bass.IndirectOffsetOnAxis(ap=gidx[h][:, u:u + 1], axis=0)).then_inc(gathered[s], 16)
                    if h == 1:
                        scatter(i, 0)
                    elif not (isinstance(i, int) and i == 0):
                        scatter(i - 1, 1)
            loop(pool, body)
            scatter(NB - 1, 1)
            pool.wait_ge(scattered, 16 * NG)

        def fast_act(act):
            def body(i):
                for s in range(2 * GT):
                    wait(act, multiplied, 16 * i + s - 15, gact)
                    wait(act, gathered[s], 16 * (i + 1), gact)
                    act.activation(gw[s // GT][:, s % GT, 0:D], g[s][:], ACT.Copy, scale=k.ew_f[:, bass.ds(i * 16 + s, 1)]).then_inc(weighted, 1)
                    along(side.act, s, i)
            loop(act, body)

        def fast_dve(dve):
            def prepare(i, h):
                wait(dve, weighted, 16 * i + 8 * h - 8)
                dve.tensor_copy(gidx[h][:], k.src_i[:, bass.ds(i * 16 + h * 8, 8)]).then_inc(idx_done, 1)
                wait(dve, multiplied, 16 * i + 8 * h - 8)
                dve.tensor_copy(gw[h][:, :, D:AW], k.ext[:, bass.ds(i * 16 + h * 8, 8), :]).then_inc(ext_done, 1)
                for u in range(GT):
                    dve.tensor_scalar(m[h * GT + u][:], k.iota[:], k.rank_f[:, bass.ds(i * 16 + h * 8 + u, 1)], None, ALU.is_equal).then_inc(m_done, 1)

            def finish(i, h):
                wait(dve, multiplied, 16 * i + 8 * h + 8)
                wait(dve, scattered, 16 * (2 * i + h - 1))
                dve.tensor_scalar(sidx[h][:], k.bank[h][:, AW - 1:AW], FAR, None, ALU.add)
                dve.tensor_copy(r[h][:], k.bank[h][:, 0:AW]).then_inc(row_done, 1)

            def body(i):
                prepare(i, 0)
                if not (isinstance(i, int) and i == 0):
                    along(side.dve, "late", i - 1)
                    finish(i - 1, 1)
                prepare(i, 1)
                along(side.dve, "early", i)
                finish(i, 0)
            loop(dve, body)
            along(side.dve, "late", NB - 1)
            finish(NB - 1, 1)

        def fast_pe(pe):
            def body(i):
                for s in range(2 * GT):
                    h, u = s // GT, s % GT
                    if u == 0:
                        wait(pe, ext_done, 2 * i + h + 1)
                        wait(pe, row_done, 2 * i + h - 1)
                    wait(pe, m_done, 16 * i + s + 1)
                    wait(pe, weighted, 16 * i + s + 1)
                    pe.matmul(k.bank[h][:, 0:AW], m[s][:], gw[h][:, u, :], start=(u == 0), stop=(u == GT - 1)).then_inc(multiplied, 1)
                    along(side.pe, s, i)
            loop(pe, body)

        def tiles_of_edges(eng, body):
            body(0)
            with eng.Fori(1, NET) as t:
                body(t)

        def general_sp(sp):
            def body(t):
                wait(sp, m_done, t, gsp)
                wait(sp, dup_done, 2 * t, gsp)
                sp.dma_start(drow[:], bass.AP(tensor=d.dst.tensor, offset=t * P, ap=[[0, P], [1, P]])).then_inc(row_loaded, 16)
            tiles_of_edges(sp, body)

        def general_pool(pool):
            def body(t):
                wait(pool, idx_done, t + 1, gpool)
                wait(pool, weighted, t, gpool)
                pool.indirect_dma_start(g[0][:], None, table, bass.IndirectOffsetOnAxis(ap=gidx[0][:, 0:1], axis=0)).then_inc(gathered[0], 16)
                wait(pool, row_done, t + 1, gpool)
                wait(pool, scattered, 16 * t, gpool)
                pool.indirect_dma_start(d.acc, bass.IndirectOffsetOnAxis(ap=sidx[0][:], axis=0), r[0][:], None,
                                        bounds_check=N - 1, oob_is_err=False, compute_op=ALU.add).then_inc(scattered, 16)
            tiles_of_edges(pool, body)
            pool.wait_ge(scattered, 16 * NET)

        def general_act(act):
            def body(t):
                wait(act, multiplied, t, gact)
                wait(act, gathered[0], 16 * (t + 1), gact)
                act.activation(gw[0][:, 0, 0:D], g[0][:], ACT.Copy, scale=k.ew_f[:, bass.ds(t, 1)]).then_inc(weighted, 1)
            tiles_of_edges(act, body)

        def general_dve(dve):
            def body(t):
                wait(dve, weighted, t)
                dve.tensor_copy(gidx[0][:, 0:1], k.src_i[:, bass.ds(t, 1)]).then_inc(idx_done, 1)
                wait(dve, multiplied, t)
                dve.tensor_copy(gw[0][:, 0:1, D:AW], k.ext[:, bass.ds(t, 1), :]).then_inc(ext_done, 1)
                wait(dve, row_loaded, 16 * (t + 1))
                dve.tensor_scalar(m[0][:], drow[:], k.dst_f[:, bass.ds(t, 1)], None, ALU.is_equal).then_inc(m_done, 1)
                wait(dve, dup_done, 2 * t)
                wait(dve, m_done, t + 1)
                dve.tensor_tensor(dup[:], m[0][:], k.tri[:], ALU.mult).then_inc(dup_done, 1)
                wait(dve, dup_done, 2 * t + 1)
                wait(dve, row_done, t)
                dve.tensor_reduce(ndup[:], dup[:], AX.X, ALU.add).then_inc(dup_done, 1)
                wait(dve, dup_done, 2 * t + 2)
                wait(dve, scattered, 16 * t)
                dve.scalar_tensor_tensor(out=sidx[0][:], in0=ndup[:], scalar=FAR, in1=k.dst_f[:, bass.ds(t, 1)], op0=ALU.mult, op1=ALU.add)
                wait(dve, multiplied, t + 1)
                dve.tensor_copy(r[0][:], k.bank[0][:, 0:AW]).then_inc(row_done, 1)
            tiles_of_edges(dve, body)

        def general_pe(pe):
            def body(t):
                wait(pe, ext_done, t + 1)
                wait(pe, row_done, t)
                wait(pe, m_done, t + 1)
                wait(pe, weighted, t + 1)
                pe.matmul(k.bank[0][:, 0:AW], m[0][:], gw[0][:, 0, :], start=True, stop=True).then_inc(multiplied, 1)
            tiles_of_edges(pe, body)

        def either(eng, fast_path, general_path, steps):
            grouped = eng.value_load(k.flag[0:1, 0:1])
            with eng.If(grouped == 1):
                fast_path(eng)
            with eng.Else():
                if general_path:
                    general_path(eng)
                loop(eng, lambda i: [along(steps, name, i) for name in steps])

        with nc.Block() as block:
            @block.sync
            def _(sp):
                side.engine(sp=sp)
                side.sp_start(sp)
                either(sp, lambda eng: loop(eng, lambda i: side.sp["move"](i, width(i))), general_sp, side.sp)
                side.sp_end(sp)

            @block.gpsimd
            def _(pool):
                either(pool, fast_pool, general_pool, {})

            @block.scalar
            def _(act):
                side.engine(act=act)
                either(act, fast_act, general_act, side.act)

            @block.vector
            def _(dve):
                side.engine(dve=dve)
                either(dve, fast_dve, general_dve, side.dve)

            @block.tensor
            def _(pe):
                side.engine(pe=pe)
                either(pe, fast_pe, general_pe, side.pe)


def coefficients(nc, st, kit, stats, gamma, beta, scale, shift, tag):
    mv = st.sb("bmv" + tag, [P, C, 2])
    sd = st.sb("bsd" + tag, [P, C])
    s1, s2, s3 = st.sem("bm" + tag), st.sem("bs" + tag), st.sem("bc" + tag)
    with nc.Block() as block:
        @block.vector
        def _(dve):
            for c in range(C):
                ins = dve.bn_aggr(mv[:, c, :], stats[:, c, :, :].rearrange("p i s -> p (i s)"))
            ins.then_inc(s1, 1)
            dve.wait_ge(s2, 1)
            dve.reciprocal(sd[:], sd[:]).then_inc(s3, 1)
            dve.wait_ge(s3, 1)
            dve.tensor_tensor(scale[:], sd[:], gamma[:], ALU.mult).then_inc(s3, 1)
            dve.wait_ge(s3, 2)
            dve.tensor_tensor(sd[:], mv[:, :, 0], scale[:], ALU.mult).then_inc(s3, 1)
            dve.wait_ge(s3, 3)
            dve.tensor_tensor(shift[:], beta[:], sd[:], ALU.subtract).then_inc(s3, 1)

        @block.scalar
        def _(act):
            act.wait_ge(s1, 1)
            act.activation(sd[:], mv[:, :, 1], ACT.Sqrt, bias=kit.eps[:]).then_inc(s2, 1)


def stage_gnn_first(nc, kit, a, d):
    k = kit
    with Stage(nc, kit) as st:
        at = st.sb("at", [P, 2, AW])
        xn = st.sb("xnb", [P, 2, D])
        y = st.sb("y", [P, 2, D])
        yT = st.sb("yT", [P, C, BODY])
        cnt = st.sb("cnt", [P, 2])
        nnb = st.sb("nnb", [P, 2, P])
        stats = st.sb("stats", [P, C, FULL + 1, 6])
        loaded, y_done, cnt_done, root_done, rn_done, nnb_done, turned, yT_done, z_done, kept, nbc_done, nkept, stat_done, wd_done = (
            st.sem(s) for s in ("loaded", "y_done", "cnt_done", "root_done", "rn_done", "nnb_done", "turned", "yT_done", "z_done", "kept", "nbc_done", "nkept", "stat_done", "wd_done"))
        gsp, gact, gdve = st.sem("gsp"), st.sem("gact"), st.sem("gdve")
        with nc.Block() as block:
            @block.sync
            def _(sp):
                def body(i, tiles):
                    w, n = tiles[0], len(tiles)
                    wait(sp, y_done, i, gsp)
                    wait(sp, wd_done, i, gsp)
                    sp.dma_start(at[0:w, 0:n, :], rows(d.acc, i, tiles)).then_inc(loaded, 16)
                    sp.dma_start(xn[0:w, 0:n, :], rows(d.xn, i, tiles)).then_inc(loaded, 16)
                bodies(sp, body)

            @block.vector
            def _(dve):
                def body(i, tiles):
                    w, n, wt = tiles[0], len(tiles), sum(tiles)
                    wait(dve, loaded, 32 * (i + 1))
                    wait(dve, nnb_done, i)
                    dve.tensor_scalar(cnt[0:w, 0:n], at[0:w, 0:n, D + 1], 1.0, None, ALU.max).then_inc(cnt_done, 1)
                    dve.tensor_copy(k.wdeg[0:w, bass.ds(i * 2, n)], at[0:w, 0:n, D]).then_inc(wd_done, 1)
                    wait(dve, turned, i)
                    dve.scalar_tensor_tensor(out=y[0:w, 0:n, :], in0=xn[0:w, 0:n, :], scalar=k.epsw[0:w, :], in1=at[0:w, 0:n, 0:D],
                                             op0=ALU.mult, op1=ALU.add).then_inc(y_done, 1)
                    wait(dve, root_done, i + 1)
                    dve.reciprocal(cnt[0:w, 0:n], cnt[0:w, 0:n]).then_inc(rn_done, 1)
                    wait(dve, rn_done, i + 1)
                    wait(dve, nbc_done, i)
                    for j in range(n):
                        ins = dve.tensor_scalar(nnb[0:w, j, :], k.ones[0:w, :], cnt[0:w, j:j + 1], None, ALU.mult)
                    ins.then_inc(nnb_done, 1)
                    wait(dve, kept, i + 1, gdve)
                    for c in range(C):
                        ins = dve.bn_stats(stats[:, c, i, :] if isinstance(i, int) else stats[:, c, bass.ds(i, 1), :].rearrange("p a s -> p (a s)"),
                                           k.bank[1 + c][:, 0:wt])
                    ins.then_inc(stat_done, 1)
                bodies(dve, body)

            @block.scalar
            def _(act):
                def body(i, tiles):
                    w, n, wt = tiles[0], len(tiles), sum(tiles)
                    wait(act, cnt_done, i + 1)
                    act.activation(cnt[0:w, 0:n], cnt[0:w, 0:n], ACT.Sqrt).then_inc(root_done, 1)
                    wait(act, turned, i + 1)
                    wait(act, z_done, i)
                    act.activation(yT[:, :, 0:wt], halves(k.bank[0][:])[:, :, 0:wt], ACT.Copy).then_inc(yT_done, 1)
                    wait(act, z_done, i + 1, gact)
                    for c in range(C):
                        ins = act.activation(k.zT[:, c, bass.ds(i * BODY, wt)], k.bank[1 + c][:, 0:wt], ACT.Copy)
                    ins.then_inc(kept, 1)
                    wait(act, nbc_done, i + 1, gact)
                    act.activation(k.nbc[:, bass.ds(i * BODY, wt)], k.bank[3][:, 0:wt], ACT.Copy).then_inc(nkept, 1)
                bodies(act, body)

            @block.tensor
            def _(pe):
                def body(i, tiles):
                    wt = sum(tiles)
                    wait(pe, y_done, i + 1)
                    wait(pe, yT_done, i)
                    pe_turn(k, pe, k.bank[0], y, tiles, turned)
                    wait(pe, yT_done, i + 1)
                    wait(pe, kept, i)
                    wait(pe, stat_done, i)
                    for o in range(C):
                        for c in range(C):
                            ins = pe.matmul(k.bank[1 + o][:, 0:wt], k.w1T[:, c, o * P:(o + 1) * P], yT[:, c, 0:wt], start=(c == 0), stop=(c == C - 1))
                    ins.then_inc(z_done, 1)
                    wait(pe, nnb_done, i + 1)
                    wait(pe, nkept, i)
                    for j, w in enumerate(tiles):
                        ins = pe.matmul(k.bank[3][:, j * P:j * P + w], nnb[0:w, j, :], k.ident[0:w, 0:w], start=True, stop=True)
                    ins.then_inc(nbc_done, 1)
                bodies(pe, body)
        coefficients(nc, st, kit, stats, k.g1c, k.be1c, k.s1, k.t1, "1")
        c1, c2 = st.sem("dg"), st.sem("dgs")
        pos = st.sb("pos", [P, NTILE + 1])
        with nc.Block() as block:
            @block.vector
            def _(dve):
                dve.tensor_scalar(k.wdeg[:], k.wdeg[:], 1.0, None, ALU.add).then_inc(c1, 1)
                dve.wait_ge(c1, 1)
                dve.tensor_scalar(pos[:], k.wdeg[:], 0.0, None, ALU.is_gt).then_inc(c1, 1)
                dve.wait_ge(c1, 2)
                dve.tensor_scalar(k.wdeg[:], k.wdeg[:], 1e-30, None, ALU.max).then_inc(c1, 1)
                dve.wait_ge(c2, 1)
                dve.reciprocal(k.wdeg[:], k.wdeg[:]).then_inc(c1, 1)
                dve.wait_ge(c1, 4)
                dve.tensor_tensor(k.wdeg[:], k.wdeg[:], pos[:], ALU.mult).then_inc(c1, 1)

            @block.scalar
            def _(act):
                act.wait_ge(c1, 3)
                act.activation(k.wdeg[:], k.wdeg[:], ACT.Sqrt).then_inc(c2, 1)


def stage_gnn_second(nc, kit, a, d):
    k = kit
    with Stage(nc, kit) as st:
        hT = st.sb("hT", [P, C, BODY])
        stats = st.sb("stats", [P, C, FULL + 1, 6])
        h_done, u_done, kept, stat_done = (st.sem(s) for s in ("h_done", "u_done", "kept", "stat_done"))
        gact, gdve = st.sem("gact"), st.sem("gdve")
        with nc.Block() as block:
            @block.scalar
            def _(act):
                def body(i, tiles):
                    wt = sum(tiles)
                    wait(act, u_done, i, gact)
                    for c in range(C):
                        ins = act.activation(hT[:, c, 0:wt], k.zT[:, c, bass.ds(i * BODY, wt)], ACT.Relu, bias=k.t1[:, c:c + 1], scale=k.s1[:, c:c + 1])
                    ins.then_inc(h_done, 1)
                bodies(act, body)

            @block.vector
            def _(dve):
                def body(i, tiles):
                    wt = sum(tiles)
                    wait(dve, u_done, i + 1, gdve)
                    for c in range(C):
                        ins = dve.tensor_tensor(k.zT[:, c, bass.ds(i * BODY, wt)], k.bank[c][:, 0:wt], k.nbc[:, bass.ds(i * BODY, wt)], ALU.mult)
                    ins.then_inc(kept, 1)
                    wait(dve, kept, i + 1, gdve)
                    for c in range(C):
                        ins = dve.bn_stats(stats[:, c, i, :] if isinstance(i, int) else stats[:, c, bass.ds(i, 1), :].rearrange("p a s -> p (a s)"),
                                           k.zT[:, c, bass.ds(i * BODY, wt)])
                    ins.then_inc(stat_done, 1)
                bodies(dve, body)

            @block.tensor
            def _(pe):
                def body(i, tiles):
                    wt = sum(tiles)
                    wait(pe, h_done, i + 1)
                    wait(pe, kept, i)
                    for o in range(C):
                        for c in range(C):
                            ins = pe.matmul(k.bank[o][:, 0:wt], k.w2T[:, c, o * P:(o + 1) * P], hT[:, c, 0:wt], start=(c == 0), stop=(c == C - 1))
                    ins.then_inc(u_done, 1)
                bodies(pe, body)
        coefficients(nc, st, kit, stats, k.ghc, k.behc, k.s2, k.t2, "2")


def stage_combine(nc, kit, a, d):
    k = kit
    with Stage(nc, kit) as st:
        xm = st.sb("xm", [P, 2, D])
        rT = st.sb("reluT", [P, C, BODY])
        x1 = st.sb("x1", [P, 2, D])
        loaded, r_done, back_done, x1_done, stored, gsp, gact, gpool = (
            st.sem(n) for n in "loaded r_done back_done x1_done stored gsp gact gpool".split())
        with nc.Block() as block:
            @block.sync
            def _(sp):
                def body(i, tiles):
                    w, n = tiles[0], len(tiles)
                    wait(sp, x1_done, i, gsp)
                    sp.dma_start(xm[0:w, 0:n, :], rows(d.xm, i, tiles)).then_inc(loaded, 16)
                bodies(sp, body)

            @block.gpsimd
            def _(pool):
                def body(i, tiles):
                    w, n = tiles[0], len(tiles)
                    wait(pool, x1_done, i + 1, gpool)
                    pool.dma_start(rows(d.x1, i, tiles), x1[0:w, 0:n, :]).then_inc(stored, 16)
                bodies(pool, body)
                pool.wait_ge(stored, 16 * (FULL + 1))

            @block.scalar
            def _(act):
                def body(i, tiles):
                    wt = sum(tiles)
                    wait(act, back_done, i, gact)
                    for c in range(C):
                        ins = act.activation(rT[:, c, 0:wt], k.zT[:, c, bass.ds(i * BODY, wt)], ACT.Relu, bias=k.t2[:, c:c + 1], scale=k.s2[:, c:c + 1])
                    ins.then_inc(r_done, 1)
                bodies(act, body)

            @block.vector
            def _(dve):
                def body(i, tiles):
                    w, n = tiles[0], len(tiles)
                    wait(dve, loaded, 16 * (i + 1))
                    wait(dve, back_done, i + 1)
                    wait(dve, stored, 16 * i)
                    dve.tensor_tensor(x1[0:w, 0:n, :], k.bank[6][0:w, 0:n * D].rearrange("p (j d) -> p j d", d=D), xm[0:w, 0:n, :], ALU.add).then_inc(x1_done, 1)
                bodies(dve, body)

            @block.tensor
            def _(pe):
                def body(i, tiles):
                    wait(pe, r_done, i + 1)
                    wait(pe, x1_done, i)
                    for j, w in enumerate(tiles):
                        for c in range(C):
                            ins = pe.transpose(k.bank[6][0:w, j * D + c * P:j * D + (c + 1) * P], rT[:, c, j * P:j * P + w], k.ident[:])
                    ins.then_inc(back_done, 1)
                bodies(pe, body)


def stage_route(nc, kit, a, d):
    k = kit
    with Stage(nc, kit) as st:
        xt = st.sb("xt", [P, 2, D])
        xnT = st.sb("xnT", [P, C, BODY])
        lg = st.sb("lg", [P, 2, EXPERTS])
        top = st.sb("top", [P, 2, 8])
        topi = st.sb("topi", [P, 2, 8], mybir.dt.uint32)
        topf = st.sb("topf", [P, 2, 1])
        one = st.sb("one", [P, 2, EXPERTS])
        seen = st.sb("seen", [P, 2, EXPERTS])
        at = st.sb("at", [P, 2, EXPERTS])
        chosen = st.sb("chosen", [P, NTILE + 1, EXPERTS])
        loaded = st.sem("loaded")
        nm = Norm(st, "d", xt, loaded, 16)
        (turned, xnT_done, lg_psum, lg_done, top_done, topi_done, topf_done, one_done, seen_done, place_psum, place_done, pos_done, kept, cleared, stored) = (
            st.sem(n) for n in "turned xnT_done lg_psum lg_done top_done topi_done topf_done one_done seen_done place_psum place_done pos_done kept cleared stored".split())
        gsp, gpool, gdve = st.sem("gsp"), st.sem("gpool"), st.sem("gdve")
        with nc.Block() as block:
            @block.sync
            def _(sp):
                def body(i, tiles):
                    wait(sp, nm.xn_done, i, gsp)
                    sp.dma_start(xt[0:tiles[0], 0:len(tiles), :], rows(d.x1, i, tiles)).then_inc(loaded, 16)
                bodies(sp, body)

            @block.gpsimd
            def _(pool):
                def body(i, tiles):
                    w, n = tiles[0], len(tiles)
                    wait(pool, nm.xn_done, i + 1, gpool)
                    pool.dma_start(rows(d.xn, i, tiles), nm.xn[0:w, 0:n, :]).then_inc(stored, 16)
                bodies(pool, body)
                pool.wait_ge(stored, 16 * (FULL + 1))

            @block.scalar
            def _(act):
                def body(i, tiles):
                    nm.act_sd(act, i, tiles)
                    wait(act, turned, i + 1)
                    wait(act, lg_psum, i)
                    act.activation(xnT[:, :, 0:sum(tiles)], halves(k.bank[0][:])[:, :, 0:sum(tiles)], ACT.Copy).then_inc(xnT_done, 1)
                bodies(act, body)

            @block.vector
            def _(dve):
                dve.memset(chosen[:], 0.0).then_inc(cleared, 1)
                dve.memset(k.pos[:], 0.0).then_inc(cleared, 1)
                dve.memset(seen[:], 0.0).then_inc(cleared, 1)
                dve.wait_ge(cleared, 3)

                def body(i, tiles):
                    w, n = tiles[0], len(tiles)
                    nm.dve_moments(dve, i, tiles)
                    nm.dve_normalise(dve, i, tiles, [(turned, 1), (stored, 16)])
                    wait(dve, lg_psum, i + 1)
                    wait(dve, topi_done, i)
                    dve_all = dve.tensor_tensor(lg[0:w, 0:n, :], k.bank[1][0:w, 0:n * EXPERTS].rearrange("p (j e) -> p j e", e=EXPERTS),
                                                k.rb2[0:w, 0:n, :], ALU.add)
                    dve_all.then_inc(lg_done, 1)
                    wait(dve, lg_done, i + 1, gdve)
                    for j in range(n):
                        ins = dve.max(top[0:w, j, :], lg[0:w, j, :])
                    ins.then_inc(top_done, 1)
                    wait(dve, top_done, i + 1, gdve)
                    for j in range(n):
                        ins = dve.max_index(topi[0:w, j, :], top[0:w, j, :], lg[0:w, j, :])
                    ins.then_inc(topi_done, 1)
                    wait(dve, topi_done, i + 1)
                    dve.tensor_copy(topf[0:w, 0:n, :], topi[0:w, 0:n, 0:1]).then_inc(topf_done, 1)
                    wait(dve, topf_done, i + 1)
                    wait(dve, place_psum, i)
                    wait(dve, kept, i)
                    for j in range(n):
                        ins = dve.tensor_scalar(one[0:w, j, :], k.iota[0:w, 0:EXPERTS], topf[0:w, j, :], None, ALU.is_equal)
                    ins.then_inc(one_done, 1)
                    wait(dve, one_done, i + 1)
                    if n == 2:
                        dve.tensor_tensor(seen[:, 1, :], seen[:, 0, :], one[:, 0, :], ALU.add).then_inc(seen_done, 1)
                    dve.tensor_copy(chosen[0:w, bass.ds(i * 2, n), :], one[0:w, 0:n, :]).then_inc(kept, 1)
                    wait(dve, place_psum, i + 1)
                    wait(dve, pos_done, i)
                    dve.tensor_tensor(at[0:w, 0:n, :], k.bank[2][0:w, 0:n * EXPERTS].rearrange("p (j e) -> p j e", e=EXPERTS), one[0:w, 0:n, :], ALU.mult).then_inc(place_done, 1)
                    dve.tensor_tensor(seen[0:w, 0, :], seen[0:w, n - 1, :], one[0:w, n - 1, :], ALU.add).then_inc(seen_done, 1)
                    wait(dve, seen_done, 2 * (i + 1) if n == 2 else 2 * FULL + 1)
                    wait(dve, place_done, i + 1)
                    dve.tensor_reduce(k.pos[0:w, bass.ds(i * 2, n)], at[0:w, 0:n, :], AX.X, ALU.add).then_inc(pos_done, 1)
                bodies(dve, body)

            @block.tensor
            def _(pe):
                pe.wait_ge(cleared, 3)

                def body(i, tiles):
                    wait(pe, nm.xn_done, i + 1)
                    wait(pe, xnT_done, i)
                    pe_turn(k, pe, k.bank[0], nm.xn, tiles, turned)
                    wait(pe, xnT_done, i + 1)
                    wait(pe, lg_done, i)
                    for j, w in enumerate(tiles):
                        for c in range(C):
                            ins = pe.matmul(k.bank[1][0:w, j * EXPERTS:(j + 1) * EXPERTS], xnT[:, c, j * P:j * P + w], k.rT[:, c, :], start=(c == 0), stop=(c == C - 1))
                    ins.then_inc(lg_psum, 1)
                    wait(pe, one_done, i + 1)
                    wait(pe, seen_done, 2 * i + 1 if len(tiles) == 2 else 2 * i)
                    wait(pe, place_done, i)
                    for j, w in enumerate(tiles):
                        pe.matmul(k.bank[2][0:w, j * EXPERTS:(j + 1) * EXPERTS], k.upper[0:w, 0:w], one[0:w, j, :], start=True, stop=False)
                        ins = pe.matmul(k.bank[2][0:w, j * EXPERTS:(j + 1) * EXPERTS], k.ones[:, 0:w], seen[:, j, :], start=False, stop=True)
                    ins.then_inc(place_psum, 1)
                bodies(pe, body)
        cnt_i = st.sb("cnt_i", [P, EXPERTS], I32)
        cnt = st.sb("cnt", [P, EXPERTS])
        upto = st.sb("upto", [P, EXPERTS])
        base = st.sb("base", [P, EXPERTS])
        zed = st.sb("zed", [P, EXPERTS])
        big = st.sb("big", [P, NTILE + 1, EXPERTS])
        te = st.sb("te", [1, SORTED, EXPERTS])
        tf = st.sb("tf", [1, SORTED])
        s1, s2 = st.sem("s1"), st.sem("s2")
        with nc.Block() as block:
            @block.tensor
            def _(pe):
                pe.matmul(k.bank[3][:, 0:EXPERTS], k.ones[:], seen[:, 0, :], start=True, stop=True).then_inc(s2, 1)

            @block.vector
            def _(dve):
                n = [0]

                def then(ins):
                    n[0] += 1
                    ins.then_inc(s1, 1)
                    dve.wait_ge(s1, n[0])
                then(dve.memset(zed[:], 0.0))
                dve.wait_ge(s2, 1)
                then(dve.tensor_scalar(cnt_i[:], k.bank[3][:, 0:EXPERTS], float(P - 1), None, ALU.add))
                then(dve.tensor_scalar(cnt_i[:], cnt_i[:], 7, None, ALU.arith_shift_right))
                then(dve.tensor_copy(cnt[:], cnt_i[:]))
                then(dve.tensor_tensor_scan(upto[:], cnt[:], zed[:], 0.0, ALU.add, ALU.add))
                then(dve.tensor_tensor(base[:], upto[:], cnt[:], ALU.subtract))
                then(dve.tensor_tensor(big[:], chosen[:], base[:].rearrange("p (a e) -> p a e", a=1).to_broadcast([P, NTILE + 1, EXPERTS]), ALU.mult))
                then(dve.tensor_reduce(k.slot_f[:], big[:], AX.X, ALU.add))
                then(dve.scalar_tensor_tensor(out=k.slot_i[:], in0=k.slot_f[:], scalar=float(P), in1=k.pos[:], op0=ALU.mult, op1=ALU.add))
                then(dve.tensor_tensor(te[:], k.iota[0:1, 0:SORTED].rearrange("p (s a) -> p s a", a=1).to_broadcast([1, SORTED, EXPERTS]),
                                       upto[0:1, :].rearrange("p (a e) -> p a e", a=1).to_broadcast([1, SORTED, EXPERTS]), ALU.is_ge))
                then(dve.tensor_reduce(tf[:], te[:], AX.X, ALU.add))
                then(dve.tensor_scalar(k.tile_expert[:], tf[:], float(EXPERTS - 1), None, ALU.min))
        xb = [st.sb(f"xb{s}", [P, D]) for s in range(4)]
        ix = [st.sb(f"ix{s}", [P, 1], I32) for s in range(4)]
        lds = [st.sem(f"row_loaded{s}") for s in range(4)]
        sent = [st.pool_dma(f"sent{s}") for s in range(4)]
        ixd = st.sem("ix_done")

        def fours(eng, body):
            body(0, range(4), P)
            with eng.Fori(1, NTILE // 4) as i:
                body(i, range(4), P)
            body(NTILE // 4, range(1), width(NTILE - 1))
        with nc.Block() as block:
            @block.sync
            def _(sp):
                def body(i, slots, w):
                    for s in slots:
                        wait(sp, sent[s], 16 * i, gsp)
                        sp.dma_start(xb[s][0:w, :], d.xn[bass.ds(i * 4 * P + s * P, w), :]).then_inc(lds[s], 16)
                fours(sp, body)

            @block.vector
            def _(dve):
                def body(i, slots, w):
                    for s in slots:
                        wait(dve, sent[s], 16 * i)
                        dve.tensor_copy(ix[s][:], k.slot_i[:, bass.ds(i * 4 + s, 1)]).then_inc(ixd, 1)
                fours(dve, body)

            @block.gpsimd
            def _(pool):
                def body(i, slots, w):
                    for s in slots:
                        wait(pool, ixd, 4 * i + s + 1, gpool)
                        wait(pool, lds[s], 16 * (i + 1), gpool)
                        pool.indirect_dma_start(d.xs, bass.IndirectOffsetOnAxis(ap=ix[s][0:w, :], axis=0), xb[s][0:w, :], None).then_inc(sent[s], 16)
                fours(pool, body)
                for s in range(4):
                    pool.wait_ge(sent[s], 16 * (NTILE // 4 + (s == 0)))


def stage_experts(nc, kit, a, d):
    k = kit
    PAIRS = SORTED // 2
    with Stage(nc, kit) as st:
        xt = [st.sb(f"xt{j}", [P, D]) for j in range(2)]
        w1 = [st.sb(f"w1_{j}", [P, C, HID]) for j in range(2)]
        w2 = [st.sb(f"w2_{j}", [HID, D]) for j in range(2)]
        b1 = [st.sb(f"b1_{j}", [1, HID]) for j in range(2)]
        b2 = [st.sb(f"b2_{j}", [1, D]) for j in range(2)]
        xT = [st.sb(f"xT{j}", [P, C, P]) for j in range(2)]
        hT = [st.sb(f"hT{j}", [HID, P]) for j in range(2)]
        y = [st.sb(f"y{j}", [P, D]) for j in range(2)]
        x_loaded = [st.sem(f"x_loaded{j}") for j in range(2)]
        w_loaded = [st.sem(f"w_loaded{j}") for j in range(2)]
        sent = [st.pool_dma(f"y_sent{j}") for j in range(2)]
        turned, xT_done, hid, h_done, out_psum, y_done = (st.sem(n) for n in "turned xT_done hid h_done out_psum y_done".split())
        gsp, gpool, acc_cleared = st.sem("gsp"), st.sem("gpool"), st.sem("acc_cleared")

        def pairs(eng, *steps):
            def at(p, i=None, j=0):
                for step, lag in steps:
                    if i is None:
                        if 0 <= p - lag < SORTED:
                            step(p - lag, (p - lag) // 2, (p - lag) % 2)
                    else:
                        step(i * 2 + (j - lag), i + (j - lag) // 2, (j - lag) % 2)
            for p in range(4):
                at(p)
            with eng.Fori(2, PAIRS) as i:
                at(0, i, 0)
                at(0, i, 1)
            at(SORTED)
            at(SORTED + 1)
        with nc.Block() as block:
            @block.sync
            def _(sp):
                def load(t, n, j):
                    wait(sp, turned, t - 1, gsp)
                    sp.dma_start(xt[j][:], d.xs[bass.ds(t * P, P), :]).then_inc(x_loaded[j], 16)
                    wait(sp, out_psum, t - 1, gsp)
                    if isinstance(t, int) and t == 1:
                        clear_acc(sp, d, k, acc_cleared)
                    e = sp.value_load(k.tile_expert[0:1, bass.ds(t, 1)], min_val=0, max_val=EXPERTS - 1)
                    sp.dma_start(w1[j][:], a["L0_ffn_W1"][bass.ds(e, 1), :, :].rearrange("a (c p) h -> p (a c) h", p=P)).then_inc(w_loaded[j], 16)
                    sp.dma_start(w2[j][:], a["L0_ffn_W2"][bass.ds(e, 1), :, :].rearrange("a h d -> h (a d)")).then_inc(w_loaded[j], 16)
                    sp.dma_start(b1[j][:], a["L0_ffn_b1"][bass.ds(e, 1), :]).then_inc(w_loaded[j], 16)
                    sp.dma_start(b2[j][:], a["L0_ffn_b2"][bass.ds(e, 1), :]).then_inc(w_loaded[j], 16)
                pairs(sp, (load, 0))
                sp.wait_ge(acc_cleared, 7 * 16)

            @block.tensor
            def _(pe):
                def turn(t, n, j):
                    wait(pe, x_loaded[j], 16 * (n + 1))
                    wait(pe, xT_done, t - 1)
                    for c in range(C):
                        ins = pe.transpose(k.bank[j][:, c * P:(c + 1) * P], xt[j][:, c * P:(c + 1) * P], k.ident[:])
                    ins.then_inc(turned, 1)

                def hidden(t, n, j):
                    wait(pe, xT_done, t + 1)
                    wait(pe, w_loaded[j], 64 * (n + 1))
                    wait(pe, h_done, t - 1)
                    for c in range(C):
                        pe.matmul(k.bank[2 + j][0:HID, 0:P], w1[j][:, c, :], xT[j][:, c, :], start=(c == 0), stop=False)
                    pe.matmul(k.bank[2 + j][0:HID, 0:P], b1[j][:], k.ones[0:1, :], start=False, stop=True).then_inc(hid, 1)

                def output(t, n, j):
                    wait(pe, h_done, t + 1)
                    wait(pe, y_done, t - 1)
                    pe.matmul(k.bank[4 + j][:, 0:D], hT[j][:], w2[j][:], start=True, stop=False)
                    pe.matmul(k.bank[4 + j][:, 0:D], k.ones[0:1, :], b2[j][:], start=False, stop=True).then_inc(out_psum, 1)
                pairs(pe, (turn, 0), (output, 1), (hidden, 0))

            @block.vector
            def _(dve):
                def copy_xT(t, n, j):
                    wait(dve, turned, t + 1)
                    wait(dve, hid, t - 1)
                    dve.tensor_copy(xT[j][:], chunks(k.bank[j])).then_inc(xT_done, 1)
                pairs(dve, (copy_xT, 0))

            @block.scalar
            def _(act):
                def relu_h(t, n, j):
                    wait(act, hid, t + 1)
                    wait(act, out_psum, t - 1)
                    act.activation(hT[j][:], k.bank[2 + j][0:HID, 0:P], ACT.Relu).then_inc(h_done, 1)

                def relu_y(t, n, j):
                    wait(act, out_psum, t + 1)
                    wait(act, sent[j], 16 * n)
                    act.activation(y[j][:], k.bank[4 + j][:, 0:D], ACT.Relu).then_inc(y_done, 1)
                pairs(act, (relu_y, 1), (relu_h, 0))

            @block.gpsimd
            def _(pool):
                def send(t, n, j):
                    wait(pool, y_done, t + 1, gpool)
                    pool.dma_start(d.ys[bass.ds(t * P, P), :], y[j][:]).then_inc(sent[j], 16)
                pairs(pool, (send, 1))
                for j in range(2):
                    pool.wait_ge(sent[j], 16 * PAIRS)


def stage_second_front(nc, kit, a, d):
    k = kit
    with Stage(nc, kit) as st:
        x1 = Slots(st, "x1", [P, 2, D], dma="sp")
        x2 = Slots(st, "x2", [P, 2, D], dma="sp")
        y = [Slots(st, f"y{j}_", [P, D], dma="pool") for j in range(2)]
        slot = [Slots(st, f"slot{j}_", [P, 1], I32) for j in range(2)]
        xnT = Slots(st, "xnT", [P, C, BODY])
        t = Slots(st, "t", [P, 2, D], dma="pool")
        kmax = st.sb("kmax", [P, C, FULL + 1])
        nm = PipedNorm(st, "e", x2, dma="sp")
        slot_done, x2_done, turned, xnT_done, t_psum, t_done, key_psum, max_done, gsp, gpool, gact, gdve = (
            st.sem(n) for n in "slot_done x2_done turned xnT_done t_psum t_done key_psum max_done gsp gpool gact gdve".split())
        with nc.Block() as block:
            @block.sync
            def _(sp):
                def load(u):
                    free(sp, x2_done, u, gate=gsp)
                    x1.load(sp, u, d.x1)

                def store_x2(u):
                    wait(sp, x2_done, u.n + 1, gsp)
                    x2.store(sp, u, d.x2)

                def store_xn(u):
                    wait(sp, nm.xn_done, u.n + 1, gsp)
                    nm.xn.store(sp, u, d.xn)
                pipeline(sp, (load, 0), (store_x2, 2), (store_xn, 3))
                x2.all_sent(sp)
                nm.xn.all_sent(sp)

            @block.gpsimd
            def _(pool):
                def gather(u):
                    wait(pool, slot_done, u.n + 1, gpool)
                    free(pool, x2_done, u, gate=gpool)
                    for j, w in enumerate(u.tiles):
                        pool.indirect_dma_start(y[j][u][0:w, :], None, d.ys, bass.IndirectOffsetOnAxis(ap=slot[j][u][0:w, :], axis=0)).then_inc(y[j].sem[u.j], 16)

                def store(u):
                    wait(pool, t_done, u.n + 1, gpool)
                    t.store(pool, u, d.t1)
                pipeline(pool, (gather, 0), (lambda u: nm.root(pool, u, gpool), 1), (store, 3))
                t.all_sent(pool)

            @block.vector
            def _(dve):
                def slots(u):
                    free(dve, x2_done, u)
                    for j in range(u.k):
                        ins = dve.tensor_copy(slot[j][u][:], k.slot_i[:, bass.ds(u.n * 2 + j, 1)])
                    ins.then_inc(slot_done, 1)

                def add_experts(u):
                    x1.landed(dve, u)
                    x2.sent(dve, u)
                    free(dve, nm.xn_done, u)
                    for j, w in enumerate(u.tiles):
                        y[j].landed(dve, u)
                        ins = dve.tensor_tensor(x2[u][0:w, j, :], x1[u][0:w, j, :], y[j][u][0:w, :], ALU.add)
                    ins.then_inc(x2_done, 1)
                    wait(dve, x2_done, u.n + 1)
                    nm.moments(dve, u)

                def normalise(u):
                    free(dve, turned, u)
                    nm.xn.sent(dve, u)
                    nm.normalise(dve, u)

                def greatest(u):
                    wait(dve, key_psum, u.n + 1, gdve)
                    dve.tensor_reduce(kmax[:, :, bass.ds(u.n, 1)], halves(k.bank[2][:])[:, :, 0:u.wt], AX.X, ALU.max).then_inc(max_done, 1)
                pipeline(dve, (slots, 0), (greatest, 3), (normalise, 2), (add_experts, 1))

            @block.scalar
            def _(act):
                def copy_xnT(u):
                    wait(act, turned, u.n + 1)
                    free(act, key_psum, u)
                    act.activation(xnT[u][:, :, 0:u.wt], halves(k.bank[0][:])[:, :, 0:u.wt], ACT.Copy).then_inc(xnT_done, 1)

                def scale(u):
                    t.sent(act, u)
                    wait(act, t_psum, u.n + 1, gact)
                    for j, w in enumerate(u.tiles):
                        ins = act.activation(t[u][0:w, j, :], k.bank[1][0:w, j * D:(j + 1) * D], ACT.Copy, scale=k.wdeg[0:w, bass.ds(u.n * 2 + j, 1)])
                    ins.then_inc(t_done, 1)
                pipeline(act, (scale, 3), (copy_xnT, 2))

            @block.tensor
            def _(pe):
                def turn(u):
                    wait(pe, nm.xn_done, u.n + 1)
                    wait(pe, xnT_done, u.n)
                    pe_turn(k, pe, k.bank[0], nm.xn[u], u.tiles, turned)

                def products(u):
                    wait(pe, xnT_done, u.n + 1)
                    wait(pe, t_done, u.n)
                    for j, w in enumerate(u.tiles):
                        for c in range(C):
                            ins = pe.matmul(k.bank[1][0:w, j * D:(j + 1) * D], xnT[u][:, c, j * P:j * P + w], k.wg1[:, c, :], start=(c == 0), stop=(c == C - 1))
                    ins.then_inc(t_psum, 1)
                    wait(pe, max_done, u.n)
                    for o in range(C):
                        for c in range(C):
                            ins = pe.matmul(k.bank[2][:, o * BODY:o * BODY + u.wt], k.wkv1[:, c, o * P:(o + 1) * P], xnT[u][:, c, 0:u.wt], start=(c == 0), stop=(c == C - 1))
                    ins.then_inc(key_psum, 1)
                pipeline(pe, (products, 3), (turn, 2))
        mx = st.sb("mx", [P, C])
        mb = st.sb("mb", [P, C, P])
        s1, s2 = st.sem("s1"), st.sem("s2")
        with nc.Block() as block:
            @block.vector
            def _(dve):
                dve.tensor_reduce(mx[:], kmax[:], AX.X, ALU.max).then_inc(s1, 1)
                dve.wait_ge(s1, 1)
                dve.tensor_tensor(mx[:], mx[:], k.bk1c[:], ALU.add).then_inc(s1, 1)
                dve.wait_ge(s1, 2)
                for c in range(C):
                    ins = dve.tensor_scalar(mb[:, c, :], k.ones[:], mx[:, c:c + 1], None, ALU.mult)
                ins.then_inc(s1, 1)
                dve.wait_ge(s2, 1)
                dve.tensor_tensor(k.bkv1[:, 0:D], k.bk1row[:], k.bank[0][:, 0:D], ALU.subtract).then_inc(s1, 1)

            @block.tensor
            def _(pe):
                pe.wait_ge(s1, 3)
                for c in range(C):
                    ins = pe.matmul(k.bank[0][:, c * P:(c + 1) * P], mb[:, c, :], k.ident[:], start=True, stop=True)
                ins.then_inc(s2, 1)


def stage_lambda(nc, kit, a, d):
    k = kit
    with Stage(nc, kit) as st:
        lam = st.sb("lam", [P, C, D])
        rs = st.sb("rsum", [P, C])
        stl = st.sb("stl", [P, C, 6])
        mv = st.sb("mvl", [P, C, 2])
        sd = st.sb("sdl", [P, C])
        sc = st.sb("scl", [P, C])
        sh = st.sb("shl", [P, C])
        qb = st.sb("qb", [P, C, P])
        s1, s2, s3 = st.sem("s1"), st.sem("s2"), st.sem("s3")
        with nc.Block() as block:
            @block.vector
            def _(dve):
                n = [0]

                def then(ins):
                    n[0] += 1
                    ins.then_inc(s1, 1)
                    dve.wait_ge(s1, n[0])
                for c in range(C):
                    then(dve.reciprocal(rs[:, c:c + 1], k.bank[4 + c][:, D:D + 1]))
                    then(dve.tensor_scalar(lam[:, c, :], k.bank[4 + c][:, 0:D], rs[:, c:c + 1], None, ALU.mult))
                    then(dve.bn_stats(stl[:, c, :], lam[:, c, :]))
                    then(dve.bn_aggr(mv[:, c, :], stl[:, c, :]))
                dve.wait_ge(s2, 1)
                then(dve.reciprocal(sd[:], sd[:]))
                then(dve.tensor_tensor(sc[:], sd[:], k.gmc[:], ALU.mult))
                then(dve.tensor_tensor(sd[:], mv[:, :, 0], sc[:], ALU.mult))
                then(dve.tensor_tensor(sh[:], k.bemc[:], sd[:], ALU.subtract))
                for c in range(C):
                    then(dve.tensor_scalar(lam[:, c, :], lam[:, c, :], sc[:, c:c + 1], sh[:, c:c + 1], ALU.mult, ALU.add))
                    then(dve.tensor_scalar(qb[:, c, :], k.ones[:], k.bq1c[:, c:c + 1], None, ALU.mult))
                dve.wait_ge(s3, 1)
                for c in range(C):
                    dve.tensor_copy(k.mq[:, c, :], k.bank[c][:, 0:D])
                then(dve.tensor_copy(k.bmq[:], k.bank[2][:, 0:D]))

            @block.scalar
            def _(act):
                act.wait_ge(s1, 8)
                act.activation(sd[:], mv[:, :, 1], ACT.Sqrt, bias=k.eps[:]).then_inc(s2, 1)

            @block.tensor
            def _(pe):
                pe.wait_ge(s1, 16)
                for o in range(C):
                    for c in range(C):
                        pe.matmul(k.bank[o][:, 0:D], k.wq1T[:, c, o * P:(o + 1) * P], lam[:, c, :], start=(c == 0), stop=(c == C - 1))
                for c in range(C):
                    ins = pe.matmul(k.bank[2][:, 0:D], qb[:, c, :], lam[:, c, :], start=(c == 0), stop=(c == C - 1))
                ins.then_inc(s3, 1)


def stage_conv_between(nc, kit, a, d):
    k = kit
    with Stage(nc, kit) as st:
        at = Slots(st, "at", [P, 2, D], dma="sp")
        tt = Slots(st, "tt", [P, 2, D], dma="sp")
        h = Slots(st, "h", [P, 2, D])
        hT = Slots(st, "hT", [P, C, BODY])
        t = Slots(st, "t", [P, 2, D], dma="pool")
        cleared, added, h_done, turned, hT_done, t_psum, t_done, gsp, gpool, gact = (st.sem(n) for n in "cleared added h_done turned hT_done t_psum t_done gsp gpool gact".split())
        with nc.Block() as block:
            @block.sync
            def _(sp):
                def load(u):
                    free(sp, added, u, gate=gsp)
                    at.load(sp, u, d.acc[:, 0:D])
                    tt.load(sp, u, d.t1)

                def clear(u):
                    at.landed(sp, u, gsp)
                    sp.dma_start(rows(d.acc, u.n, u.tiles), k.zeros[0:u.w, 0:u.k * AW].rearrange("p (j d) -> p j d", d=AW)).then_inc(cleared, 16)
                pipeline(sp, (load, 0), (clear, 2))
                sp.wait_ge(cleared, 16 * (FULL + 1))

            @block.gpsimd
            def _(pool):
                def store(u):
                    wait(pool, t_done, u.n + 1, gpool)
                    t.store(pool, u, d.t2)
                pipeline(pool, (store, 2))
                t.all_sent(pool)

            @block.vector
            def _(dve):
                def convolve(u):
                    at.landed(dve, u)
                    tt.landed(dve, u)
                    free(dve, turned, u)
                    dve.tensor_tensor(h.part(u), at.part(u), tt.part(u), ALU.add).then_inc(added, 1)
                    wait(dve, added, u.n + 1)
                    for j, w in enumerate(u.tiles):
                        ins = dve.scalar_tensor_tensor(out=h[u][0:w, j, :], in0=h[u][0:w, j, :], scalar=k.wdeg[0:w, bass.ds(u.n * 2 + j, 1)],
                                                       in1=k.bg1[0:w, :], op0=ALU.mult, op1=ALU.add)
                    ins.then_inc(h_done, 1)
                pipeline(dve, (convolve, 0))

            @block.scalar
            def _(act):
                def relu_hT(u):
                    wait(act, turned, u.n + 1)
                    free(act, t_psum, u)
                    act.activation(hT[u][:, :, 0:u.wt], halves(k.bank[0][:])[:, :, 0:u.wt], ACT.Relu).then_inc(hT_done, 1)

                def scale(u):
                    t.sent(act, u)
                    wait(act, t_psum, u.n + 1, gact)
                    for j, w in enumerate(u.tiles):
                        ins = act.activation(t[u][0:w, j, :], k.bank[1][0:w, j * D:(j + 1) * D], ACT.Copy, scale=k.wdeg[0:w, bass.ds(u.n * 2 + j, 1)])
                    ins.then_inc(t_done, 1)
                pipeline(act, (relu_hT, 1), (scale, 2))

            @block.tensor
            def _(pe):
                def turn(u):
                    wait(pe, h_done, u.n + 1)
                    wait(pe, hT_done, u.n)
                    pe_turn(k, pe, k.bank[0], h[u], u.tiles, turned)

                def product(u):
                    wait(pe, hT_done, u.n + 1)
                    wait(pe, t_done, u.n)
                    for j, w in enumerate(u.tiles):
                        for c in range(C):
                            ins = pe.matmul(k.bank[1][0:w, j * D:(j + 1) * D], hT[u][:, c, j * P:j * P + w], k.wg2[:, c, :], start=(c == 0), stop=(c == C - 1))
                    ins.then_inc(t_psum, 1)
                pipeline(pe, (turn, 1), (product, 2))


def stage_slices(nc, kit, a, d):
    k = kit
    HS = HEADS * SLICES
    NC4 = HS // P
    with Stage(nc, kit) as st:
        at = Slots(st, "at", [P, 2, D], dma="sp")
        tt = Slots(st, "tt", [P, 2, D], dma="sp")
        xm = Slots(st, "xm", [P, 2, D], dma="sp")
        x3 = Slots(st, "x3", [P, 2, D], dma="pool")
        xnT = Slots(st, "xnT", [P, C, BODY])
        lg = Slots(st, "lg", [P, 2, HS], dma="pool")
        mx = Slots(st, "mx", [P, 2, HEADS])
        nm = PipedNorm(st, "s", x3, D + 1)
        (one_done, added, scaled, x3_done, turned, xnT_done, lg_psum, lg_done, mx_done, sub_done, e_done, sum_done, rec_done, sw_done, acc_done) = (
            st.sem(n) for n in "one_done added scaled x3_done turned xnT_done lg_psum lg_done mx_done sub_done e_done sum_done rec_done sw_done acc_done".split())
        gsp, gpool = st.sem("gsp"), st.sem("gpool")

        def heads(t, j, w):
            return t[0:w, j, :].rearrange("p (h g) -> p h g", g=SLICES)

        def over(t, j, w):
            return t[0:w, j, :].rearrange("p (h a) -> p h a", a=1).to_broadcast([w, HEADS, SLICES])
        with nc.Block() as block:
            @block.sync
            def _(sp):
                def load(u):
                    free(sp, added, u, gate=gsp)
                    at.load(sp, u, d.acc[:, 0:D])
                    tt.load(sp, u, d.t2)
                    free(sp, x3_done, u, gate=gsp)
                    xm.load(sp, u, d.xm)
                pipeline(sp, (load, 0))

            @block.gpsimd
            def _(pool):
                def store_x3(u):
                    wait(pool, x3_done, u.n + 1, gpool)
                    x3.store(pool, u, d.x3)

                def store_sw(u):
                    wait(pool, sw_done, u.n + 1, gpool)
                    lg.store(pool, u, d.sw)
                pipeline(pool, (lambda u: nm.root(pool, u, gpool), 0), (store_x3, 0), (store_sw, 3))
                x3.all_sent(pool)
                lg.all_sent(pool)

            @block.vector
            def _(dve):
                for b in nm.xn.buf:
                    dve.memset(b[:, :, D:D + 1], 1.0).then_inc(one_done, 1)

                def convolve(u):
                    at.landed(dve, u)
                    tt.landed(dve, u)
                    x3.sent(dve, u)
                    free(dve, nm.xn_done, u)
                    dve.tensor_tensor(x3.part(u), at.part(u), tt.part(u), ALU.add).then_inc(added, 1)
                    wait(dve, added, u.n + 1)
                    for j, w in enumerate(u.tiles):
                        ins = dve.scalar_tensor_tensor(out=x3[u][0:w, j, :], in0=x3[u][0:w, j, :], scalar=k.wdeg[0:w, bass.ds(u.n * 2 + j, 1)],
                                                       in1=k.bg2[0:w, :], op0=ALU.mult, op1=ALU.add)
                    ins.then_inc(scaled, 1)
                    wait(dve, scaled, u.n + 1)
                    xm.landed(dve, u)
                    dve.scalar_tensor_tensor(out=x3.part(u), in0=x3.part(u), scalar=0.0, in1=xm.part(u), op0=ALU.max, op1=ALU.add).then_inc(x3_done, 1)
                    wait(dve, x3_done, u.n + 1)
                    nm.moments(dve, u)

                def normalise(u):
                    free(dve, acc_done, u)
                    nm.normalise(dve, u)

                def below_max(u):
                    wait(dve, lg_psum, u.n + 1)
                    lg.sent(dve, u)
                    free(dve, acc_done, u)
                    for j, w in enumerate(u.tiles):
                        ins = dve.tensor_tensor(lg[u][0:w, j, :], k.bank[1 + j][0:w, :], k.bxs[0:w, :], ALU.add)
                    ins.then_inc(lg_done, 1)
                    wait(dve, lg_done, u.n + 1)
                    for j, w in enumerate(u.tiles):
                        ins = dve.tensor_reduce(mx[u][0:w, j, :], heads(lg[u], j, w), AX.X, ALU.max)
                    ins.then_inc(mx_done, 1)
                    wait(dve, mx_done, u.n + 1)
                    for j, w in enumerate(u.tiles):
                        ins = dve.tensor_tensor(heads(lg[u], j, w), heads(lg[u], j, w), over(mx[u], j, w), ALU.subtract)
                    ins.then_inc(sub_done, 1)

                def weights(u):
                    wait(dve, e_done, u.n + 1)
                    for j, w in enumerate(u.tiles):
                        ins = dve.tensor_reduce(mx[u][0:w, j, :], heads(lg[u], j, w), AX.X, ALU.add)
                    ins.then_inc(sum_done, 1)
                    wait(dve, sum_done, u.n + 1)
                    dve.reciprocal(mx.part(u), mx.part(u)).then_inc(rec_done, 1)
                    wait(dve, rec_done, u.n + 1)
                    for j, w in enumerate(u.tiles):
                        ins = dve.tensor_tensor(heads(lg[u], j, w), heads(lg[u], j, w), over(mx[u], j, w), ALU.mult)
                    ins.then_inc(sw_done, 1)
                pipeline(dve, (weights, 3), (normalise, 1), (below_max, 2), (convolve, 0))

            @block.scalar
            def _(act):
                def copy_xnT(u):
                    wait(act, turned, u.n + 1)
                    free(act, lg_psum, u)
                    act.activation(xnT[u][:, :, 0:u.wt], halves(k.bank[0][:])[:, :, 0:u.wt], ACT.Copy).then_inc(xnT_done, 1)

                def exp(u):
                    wait(act, sub_done, u.n + 1)
                    act.activation(lg.part(u), lg.part(u), ACT.Exp).then_inc(e_done, 1)
                pipeline(act, (copy_xnT, 1), (exp, 2))

            @block.tensor
            def _(pe):
                pe.wait_ge(one_done, SLOTS)

                def turn(u):
                    wait(pe, nm.xn_done, u.n + 1)
                    wait(pe, xnT_done, u.n)
                    pe_turn(k, pe, k.bank[0], nm.xn[u], u.tiles, turned)

                def sums(u):
                    wait(pe, sw_done, u.n + 1)
                    for j, w in enumerate(u.tiles):
                        for c in range(NC4):
                            ins = pe.matmul(k.bank[3 + c][:, 0:D + 1], lg[u][0:w, j, c * P:(c + 1) * P], nm.xn[u][0:w, j, :],
                                            start=u.first and j == 0, stop=u.last)
                    ins.then_inc(acc_done, 1)

                def logits(u):
                    wait(pe, xnT_done, u.n + 1)
                    wait(pe, lg_done, u.n)
                    for j, w in enumerate(u.tiles):
                        for c in range(C):
                            ins = pe.matmul(k.bank[1 + j][0:w, :], xnT[u][:, c, j * P:j * P + w], k.wxs[:, c, :], start=(c == 0), stop=(c == C - 1))
                    ins.then_inc(lg_psum, 1)
                pipeline(pe, (turn, 1), (sums, 3), (logits, 1))
        Tt = st.sb("Tt", [P, NC4, D + 1])
        T = st.sb("T", [P, C, HS])
        norm = st.sb("norm", [1, HS])
        t_read, t_turned, t_out = st.sem("t_read"), st.sem("t_turned"), st.sem("t_out")
        with nc.Block() as block:
            @block.vector
            def _(dve):
                for c in range(NC4):
                    ins = dve.tensor_copy(Tt[:, c, :], k.bank[3 + c][:, 0:D + 1])
                ins.then_inc(t_read, 1)
                dve.wait_ge(t_turned, 1)
                for c in range(C):
                    dve.tensor_copy(T[:, c, :], k.bank[c][:])
                dve.tensor_copy(norm[:], k.bank[2][0:1, :]).then_inc(t_out, 1)

            @block.tensor
            def _(pe):
                pe.wait_ge(t_read, 1)
                for c in range(NC4):
                    for o in range(C):
                        pe.transpose(k.bank[o][:, c * P:(c + 1) * P], Tt[:, c, o * P:(o + 1) * P], k.ident[:])
                    ins = pe.transpose(k.bank[2][0:1, c * P:(c + 1) * P], Tt[:, c, D:D + 1], k.ident[:])
                ins.then_inc(t_turned, 1)
        rn = st.sb("rn", [SLICES, 1])
        tok, tokT, qT, kT, vv, at, atT, oT = (st.sb(n, [SLICES, SDIM]) for n in "tok tokT qT kT vv at atT oT".split())
        mo = st.sb("mo", [SLICES, D])
        sm = st.sb("sm", [SLICES, 4])
        vs, ps, as_, ds = st.sem("vs"), st.sem("ps"), st.sem("as_"), st.sem("ds")
        b = k.bank
        with nc.Block() as block:
            @block.vector
            def _(dve):
                n, p = [0], [0]

                def then(ins):
                    n[0] += 1
                    ins.then_inc(vs, 1)
                    dve.wait_ge(vs, n[0])

                def psum():
                    p[0] += 1
                    dve.wait_ge(ps, p[0])
                for h in range(HEADS):
                    psum()
                    then(dve.tensor_scalar(rn[:], b[1][0:SLICES, 0:1], 1e-5, None, ALU.add))
                    then(dve.reciprocal(rn[:], rn[:]))
                    then(dve.tensor_scalar(tok[:], b[0][0:SLICES, 0:SDIM], rn[:], None, ALU.mult))
                    psum()
                    then(dve.tensor_copy(tokT[:], b[0][0:SDIM, 0:SLICES]))
                    psum()
                    dve.tensor_copy(qT[:], b[0][0:SDIM, 0:SLICES])
                    dve.tensor_copy(kT[:], b[1][0:SDIM, 0:SLICES])
                    then(dve.tensor_copy(vv[:], b[2][0:SLICES, 0:SDIM]))
                    psum()
                    then(dve.tensor_reduce(sm[:, 0:1], b[0][0:SLICES, 0:SLICES], AX.X, ALU.max))
                    then(dve.tensor_scalar(sm[:, 1:2], sm[:, 0:1], -SDIM ** -0.5, None, ALU.mult))
                    dve.wait_ge(as_, h + 1)
                    then(dve.reciprocal(sm[:, 3:4], sm[:, 2:3]))
                    then(dve.tensor_scalar(at[:], at[:], sm[:, 3:4], None, ALU.mult))
                    psum()
                    then(dve.tensor_copy(atT[:], b[1][0:SLICES, 0:SLICES]))
                    psum()
                    then(dve.tensor_copy(oT[:], b[2][0:SDIM, 0:SLICES]))
                    psum()
                    if h:
                        dve.wait_ge(ds, 16 * h)
                    then(dve.tensor_copy(mo[:], b[0][0:SLICES, 0:D]))

            @block.scalar
            def _(act):
                for h in range(HEADS):
                    act.wait_ge(vs, 12 * h + 7)
                    act.activation(at[:], b[0][0:SLICES, 0:SLICES], ACT.Exp, bias=sm[:, 1:2], scale=SDIM ** -0.5,
                                   accum_out=sm[:, 2:3]).then_inc(as_, 1)

            @block.sync
            def _(sp):
                for h in range(HEADS):
                    sp.wait_ge(vs, 12 * (h + 1))
                    sp.dma_start(k.mout[(h % 2) * SLICES:(h % 2 + 1) * SLICES, h // 2, :], mo[:]).then_inc(ds, 16)
                sp.wait_ge(ds, 16 * HEADS)

            @block.tensor
            def _(pe):
                for h in range(HEADS):
                    hs = slice(h * SLICES, (h + 1) * SLICES)
                    o = 12 * h
                    if h:
                        pe.wait_ge(vs, o)
                    for c in range(C):
                        pe.matmul(b[0][0:SLICES, 0:SDIM], T[:, c, hs], k.wfx[:, c, hs], start=(c == 0), stop=False)
                    pe.matmul(b[0][0:SLICES, 0:SDIM], norm[:, hs], k.bfx[:, hs], start=False, stop=True)
                    pe.matmul(b[1][0:SLICES, 0:1], norm[:, hs], k.ones[0:1, 0:1], start=True, stop=True).then_inc(ps, 1)
                    pe.wait_ge(vs, o + 3)
                    pe.transpose(b[0][0:SDIM, 0:SLICES], tok[:], k.ident[0:SLICES, 0:SLICES]).then_inc(ps, 1)
                    pe.wait_ge(vs, o + 4)
                    pe.matmul(b[0][0:SDIM, 0:SLICES], k.wsq[:], tokT[:], start=True, stop=True)
                    pe.matmul(b[1][0:SDIM, 0:SLICES], k.wsk[:], tokT[:], start=True, stop=True)
                    pe.matmul(b[2][0:SLICES, 0:SDIM], tokT[:], k.wsv[:], start=True, stop=True).then_inc(ps, 1)
                    pe.wait_ge(vs, o + 5)
                    pe.matmul(b[0][0:SLICES, 0:SLICES], qT[:], kT[:], start=True, stop=True).then_inc(ps, 1)
                    pe.wait_ge(vs, o + 9)
                    pe.transpose(b[1][0:SLICES, 0:SLICES], at[:], k.ident[0:SLICES, 0:SLICES]).then_inc(ps, 1)
                    pe.wait_ge(vs, o + 10)
                    pe.matmul(b[2][0:SDIM, 0:SLICES], vv[:], atT[:], start=True, stop=True).then_inc(ps, 1)
                    pe.wait_ge(vs, o + 11)
                    pe.matmul(b[0][0:SLICES, 0:D], oT[:], k.wout[:, h, :], start=True, stop=True).then_inc(ps, 1)


def stage_out(nc, kit, a, d, out):
    k = kit
    HS = HEADS * SLICES
    NC4 = HS // P
    with Stage(nc, kit) as st:
        sw = Slots(st, "sw", [P, 2, HS], dma="sp")
        x3 = Slots(st, "x3", [P, 2, D], dma="sp")
        swT = Slots(st, "swT", [P, 2, NC4, P])
        y = Slots(st, "y", [P, 2, D], dma="pool")
        turned, copied, swT_done, y_psum, a_done, y_done, gsp, gpool = (st.sem(n) for n in "turned copied swT_done y_psum a_done y_done gsp gpool".split())
        four = lambda bank: bank[:].rearrange("p (c n) -> p c n", c=NC4)
        with nc.Block() as block:
            @block.sync
            def _(sp):
                def load(u):
                    free(sp, turned, u, gate=gsp)
                    sw.load(sp, u, d.sw)
                    free(sp, y_done, u, gate=gsp)
                    x3.load(sp, u, d.x3)
                pipeline(sp, (load, 0))

            @block.gpsimd
            def _(pool):
                def store(u):
                    wait(pool, y_done, u.n + 1, gpool)
                    y.store(pool, u, out)
                pipeline(pool, (store, 1))
                y.all_sent(pool)

            @block.scalar
            def _(act):
                def copy(u):
                    wait(act, turned, u.n + 1)
                    free(act, y_psum, u)
                    act.activation(swT[u][:, 0, :, 0:u.w], four(k.bank[0])[:, :, 0:u.w], ACT.Copy).then_inc(swT_done, 1)
                pipeline(act, (copy, 0))

            @block.vector
            def _(dve):
                def copy(u):
                    if u.k == 2:
                        wait(dve, turned, u.n + 1)
                        free(dve, y_psum, u)
                        dve.tensor_copy(swT[u][:, 1, :, :], four(k.bank[1])).then_inc(copied, 1)

                def add(u):
                    wait(dve, y_psum, u.n + 1)
                    y.sent(dve, u)
                    for j, w in enumerate(u.tiles):
                        ins = dve.tensor_tensor(y[u][0:w, j, :], k.bank[2 + j][0:w, 0:D], k.bout[0:w, :], ALU.add)
                    ins.then_inc(a_done, 1)
                    wait(dve, a_done, u.n + 1)
                    x3.landed(dve, u)
                    dve.tensor_tensor(y.part(u), y.part(u), x3.part(u), ALU.add).then_inc(y_done, 1)
                pipeline(dve, (copy, 0), (add, 1))

            @block.tensor
            def _(pe):
                def turn(u):
                    sw.landed(pe, u)
                    wait(pe, swT_done, u.n)
                    wait(pe, copied, u.n)
                    for j, w in enumerate(u.tiles):
                        for c in range(NC4):
                            ins = pe.transpose(k.bank[j][:, c * P:c * P + w], sw[u][0:w, j, c * P:(c + 1) * P], k.ident[0:w, 0:w])
                    ins.then_inc(turned, 1)

                def product(u):
                    wait(pe, swT_done, u.n + 1)
                    wait(pe, copied, min(u.n + 1, FULL) if isinstance(u.n, int) else u.n + 1)
                    wait(pe, a_done, u.n)
                    for j, w in enumerate(u.tiles):
                        for c in range(NC4):
                            ins = pe.matmul(k.bank[2 + j][0:w, 0:D], swT[u][:, j, c, 0:w], k.mout[:, c, :], start=(c == 0), stop=(c == NC4 - 1))
                    ins.then_inc(y_psum, 1)
                pipeline(pe, (turn, 0), (product, 1))


def build(nc, a, out):
    HS = HEADS * SLICES
    with ExitStack() as ctx:
        k, d = Kit(), Kit()
        k.ctx, k.stages = ctx, 0

        def sb(name, shape, dt=F32):
            return ctx.enter_context(nc.sbuf_tensor(name, shape, dt))

        def dram(name, shape, dt=F32):
            return nc.dram_tensor("d_" + name, shape, dt).ap()
        k.bank = [ctx.enter_context(nc.psum_tensor(f"bank{b}", [P, 512], F32)) for b in range(8)]
        d.xn = dram("xn", [N, D])
        d.xm = dram("xm", [N, D])
        d.xs = dram("xs", [SORTED * P, D])
        d.ys = dram("ys", [SORTED * P, D])
        d.x1 = dram("x1", [N, D])
        d.t1 = dram("t1", [N, D])
        d.t2 = dram("t2", [N, D])
        d.x2 = dram("x2", [N, D])
        d.x3 = dram("x3", [N, D])
        d.dst = dram("dst", [NG * GE], I32)
        d.sw = dram("sw", [N, HS], F32)
        d.acc = dram("acc", [NTILE * P, AW], F32)
        k.ident = sb("ident", [P, P])
        k.tri = sb("tri", [P, P])
        k.hmask = sb("hmask", [P, P])
        k.ones = sb("ones", [P, P])
        k.iota_i = sb("iota_i", [P, P], I32)
        k.iota = sb("iota", [P, P])
        k.eps = sb("eps", [P, 1])
        k.mhalf = sb("mhalf", [P, 2])
        k.zeros = sb("zeros", [P, 7 * AW])
        k.wq0 = sb("wq0", [P, C, D])
        k.wo0 = sb("wo0", [P, C, D])
        k.wg1 = sb("wg1", [P, C, D])
        k.wg2 = sb("wg2", [P, C, D])
        k.w1T = sb("w1T", [P, C, D])
        k.w2T = sb("w2T", [P, C, D])
        k.wq1T = sb("wq1T", [P, C, D])
        k.m0 = sb("m0", [P, C, D])
        k.mq = sb("mq", [P, C, D])
        k.wkv0 = sb("wkv0", [P, C, 2 * D])
        k.wkv1 = sb("wkv1", [P, C, 2 * D])
        k.wfx = sb("wfx", [P, C, 2 * D])
        k.wxs = sb("wxs", [P, C, 2 * D])
        k.rT = sb("rT", [P, C, EXPERTS])
        k.rb2 = sb("rb2", [P, 2, EXPERTS])
        k.pos = sb("pos", [P, NTILE + 1])
        k.slot_f = sb("slot_f", [P, NTILE + 1])
        k.slot_i = sb("slot_i", [P, NTILE + 1], I32)
        k.tile_expert = sb("tile_expert", [1, SORTED], I32)
        k.upper = sb("upper", [P, P])
        k.wout = sb("wout", [SDIM, HEADS, D])
        k.wslice = sb("wslice", [SDIM, SDIM])
        k.wsq = sb("wsq", [SDIM, SDIM])
        k.wsk = sb("wsk", [SDIM, SDIM])
        k.wsv = sb("wsv", [SDIM, SDIM])
        k.bkv0 = sb("bkv0", [P, 2 * D])
        k.bkv1 = sb("bkv1", [P, 2 * D])
        k.bxs = sb("bxs", [P, 2 * D])
        k.bk1row = sb("bk1row", [P, D])
        k.bg1 = sb("bg1", [P, D])
        k.bg2 = sb("bg2", [P, D])
        k.bout = sb("bout", [P, D])
        k.bmq = sb("bmq", [P, D])
        k.bfx = sb("bfx", [1, HS])
        k.bslice_row = sb("bslice_row", [P, SLICES])
        k.temp = sb("temp", [P, HEADS])
        k.rtemp = sb("rtemp", [P, HEADS])
        k.epsw = sb("epsw", [P, 1])
        k.g1c = sb("g1c", [P, C])
        k.be1c = sb("be1c", [P, C])
        k.ghc = sb("ghc", [P, C])
        k.behc = sb("behc", [P, C])
        k.bqc = sb("bqc", [P, C])
        k.boc = sb("boc", [P, C])
        k.gmc = sb("gmc", [P, C])
        k.bemc = sb("bemc", [P, C])
        k.bq1c = sb("bq1c", [P, C])
        k.bk1c = sb("bk1c", [P, C])
        k.s1 = sb("s1", [P, C])
        k.t1 = sb("t1", [P, C])
        k.s2 = sb("s2", [P, C])
        k.t2 = sb("t2", [P, C])
        k.ks = sb("ks", [P, C, P])
        k.mout = sb("mout", [P, HS // P, D])
        k.wdeg = sb("wdeg", [P, NTILE + 1])
        k.flag = sb("flag", [1, 1], I32)
        k.dst_f = sb("dst_f", [P, NET])
        k.rank_f = sb("rank_f", [P, NET])
        k.ew_f = sb("ew_f", [P, NET])
        k.fd_f = sb("fd_f", [P, NET])
        k.src_i = sb("src_i", [P, NET], I32)
        k.dst_i = sb("dst_i", [P, NET], I32)
        k.ext = sb("ext", [P, NET, 3])
        stage_setup(nc, k, a, d)
        stage_front(nc, k, a, d)
        stage_aggregate(nc, k, a, d, d.xn, LinearAttention)
        with ExitStack() as middle:
            k.zT = middle.enter_context(nc.sbuf_tensor("zT", [P, C, N], F32))
            k.nbc = middle.enter_context(nc.sbuf_tensor("nbc", [P, N], F32))
            stage_gnn_first(nc, k, a, d)
            stage_gnn_second(nc, k, a, d)
            stage_combine(nc, k, a, d)
        stage_route(nc, k, a, d)
        stage_experts(nc, k, a, d)
        stage_second_front(nc, k, a, d)
        stage_aggregate(nc, k, a, d, d.t1, KeySums)
        stage_lambda(nc, k, a, d)
        stage_conv_between(nc, k, a, d)
        stage_aggregate(nc, k, a, d, d.t2, QueryMix)
        stage_slices(nc, k, a, d)
        stage_out(nc, k, a, d, out)


def kernel(**inputs):
    import numpy as np
    import concourse.bacc as bacc
    from concourse.bass_utils import run_bass_kernel_spmd

    nc = bacc.Bacc("TRN2", target_bir_lowering=False, num_devices=1)
    arrays, args = {}, {}
    for name, x in inputs.items():
        x = np.ascontiguousarray(x)
        arrays[f"in_{name}"] = x
        args[name] = nc.dram_tensor(f"in_{name}", x.shape, mybir.dt.from_np(x.dtype), kind="ExternalInput").ap()
    out = nc.dram_tensor("out_0", (N, D), F32, kind="ExternalOutput").ap()
    build(nc, args, out)
    return run_bass_kernel_spmd(nc, [arrays], core_ids=[0]).results[0]["out_0"]
```
